# Optimizing a Trainium2 kernel written in Bass

```python
import numpy as np
import jax
import jax.numpy as jnp

def _softmax(x, axis=-1):
    return jax.nn.softmax(x, axis=axis)

def _gelu(x):
    return jax.nn.gelu(x, approximate=True)

def _silu(x):
    return jax.nn.silu(x)

def _sigmoid(x):
    return jax.nn.sigmoid(x)

def _layernorm(x, axis=-1, eps=1e-05):
    m = jnp.mean(x, axis=axis, keepdims=True)
    v = jnp.var(x, axis=axis, keepdims=True)
    return (x - m) / jnp.sqrt(v + eps)

def _scatter_add(tgt, idx, src, axis=0):
    return tgt.at[idx].add(src)

def _segment_sum(src, seg, n):
    return jax.ops.segment_sum(src, seg, n)
kernel_name = 'mk_perceiver_d4_seqx_r4_7a2e2a'

def setup_inputs(seed: int=0):
    np.random.seed(seed)
    _w = jnp.asarray

    def _rec_inputs():
        import jax
        import jax.numpy as jnp
        _rk = jax.random.key(seed)
        x = 0.002226 + 0.9996 * jax.random.normal(jax.random.fold_in(_rk, 1), (8, 64, 256), jnp.float32)
        _lenS = 64 - jax.random.randint(jax.random.fold_in(_rk, 7), (8,), 0, max(1, 64 // 4) + 1, jnp.int32)
        _lenS2 = 1601 - jax.random.randint(jax.random.fold_in(_rk, 8), (8,), 0, max(1, 1601 // 4) + 1, jnp.int32)
        _ctx_1024P = jax.random.normal(jax.random.fold_in(_rk, 11), (8, 16, 256), jnp.float32)
        _ctx_1024c = jax.random.dirichlet(jax.random.fold_in(_rk, 511), 0.3 * jnp.ones((16,), jnp.float32), (8, 1601))
        _ctx_1024t = jnp.einsum('bsk,bkd->bsd', _ctx_1024c, _ctx_1024P)
        _ctx_1024t = _ctx_1024t * jax.lax.rsqrt(jnp.mean(jnp.square(_ctx_1024t)) + 1e-12) * 0.953939
        ctx_1024 = -0.000125008 + 0.999885 * (_ctx_1024t + 0.3 * jax.random.normal(jax.random.fold_in(_rk, 611), (8, 1601, 256), jnp.float32))
        _validS = jnp.arange(64)[None, :] < _lenS[:, None]
        _validS2 = jnp.arange(1601)[None, :] < _lenS2[:, None]
        _causal = jnp.tril(jnp.ones((64, 64), dtype=bool))
        mask_BxS2_if1 = jnp.where(jnp.ones((8, 1601), dtype=bool), 1, 0).astype(jnp.int32)
        return (x, ctx_1024, mask_BxS2_if1)
    x, ctx_1024, mask_BxS2_if1 = _rec_inputs()

    def _L0_xattn_setup():
        import jax, jax.numpy as jnp
        import numpy as np
        B, M, N, DIM, DH, H = (8, 1024, 64, 256, 128, 8)
        INNER = DH * H
        EPS = 1e-05

        def _layernorm(x, g, b):
            mu = jnp.mean(x, axis=-1, keepdims=True)
            var = jnp.var(x, axis=-1, keepdims=True)
            return (x - mu) * jax.lax.rsqrt(var + EPS) * g + b
        key = jax.random.key(seed)
        ks = jax.random.split(key, 8)
        sd = 0.02
        return {'x': jax.random.normal(ks[0], (B, M, DIM), jnp.float32), 'latents': jax.random.normal(ks[1], (B, N, DIM), jnp.float32), 'gamma_media': jnp.ones((DIM,), jnp.float32), 'beta_media': jnp.zeros((DIM,), jnp.float32), 'gamma_lat': jnp.ones((DIM,), jnp.float32), 'beta_lat': jnp.zeros((DIM,), jnp.float32), 'Wq': jax.random.normal(ks[2], (DIM, INNER), jnp.float32) * sd, 'bq': jnp.zeros((INNER,), jnp.float32), 'Wkv': jax.random.normal(ks[3], (DIM, 2 * INNER), jnp.float32) * sd, 'bkv': jnp.zeros((2 * INNER,), jnp.float32), 'Wo': jax.random.normal(ks[4], (INNER, DIM), jnp.float32) * sd, 'bo': jnp.zeros((DIM,), jnp.float32)}
    _L0_xattn_all = _L0_xattn_setup()
    _L0_xattn_in = {k: v for k, v in _L0_xattn_all.items() if k in ('gamma_media', 'beta_media', 'gamma_lat', 'beta_lat', 'Wq', 'bq', 'Wkv', 'bkv', 'Wo', 'bo')}
    del _L0_xattn_all

    def _L0_attn_setup():
        import jax, jax.numpy as jnp
        import numpy as np
        L, E, H = (4, 256, 16)
        HD = E // H
        EPS_LN = 1e-05

        def _layernorm(x, w, b):
            m = jnp.mean(x, axis=-1, keepdims=True)
            v = jnp.mean((x - m) ** 2, axis=-1, keepdims=True)
            return (x - m) / jnp.sqrt(v + EPS_LN) * w + b

        def _to_quaternion(x):
            p1 = jnp.diff(x, axis=1, prepend=x[:, :1])
            p2 = jnp.roll(x, 1, axis=2)
            p3 = jnp.cos(x)
            return jnp.stack([x, p1, p2, p3], axis=-1)

        def _hamilton(a, b):
            a0, a1, a2, a3 = (a[..., 0], a[..., 1], a[..., 2], a[..., 3])
            b0, b1, b2, b3 = (b[..., 0], b[..., 1], b[..., 2], b[..., 3])
            return jnp.stack([a0 * b0 - a1 * b1 - a2 * b2 - a3 * b3, a0 * b1 + a1 * b0 + a2 * b3 - a3 * b2, a0 * b2 - a1 * b3 + a2 * b0 + a3 * b1, a0 * b3 + a1 * b2 - a2 * b1 + a3 * b0], axis=-1)

        def _spectral_filter(S):
            ks = jnp.fft.fftfreq(S).astype(jnp.float32)[:, None, None]
            kh = jnp.fft.fftfreq(H).astype(jnp.float32)[None, :, None]
            kd = jnp.fft.fftfreq(HD).astype(jnp.float32)[None, None, :]
            km = jnp.sqrt(ks ** 2 + kh ** 2 + kd ** 2 + 1e-10)
            f = jnp.exp(1j * jnp.arctan(jnp.log(km + 1e-10)))
            return f[None, :, :, :, None].astype(jnp.complex64)

        def _modulation(S):
            lam = jnp.arange(S, dtype=jnp.float32) / S
            t = jnp.arange(S, dtype=jnp.float32) * 0.1
            probe = jnp.sin(t + lam)
            phase = t - 2.0 * lam + 0.5 * lam ** 2
            return (probe * jnp.cos(phase))[None, :, None, None]

        def _attention(x, aw, ab, pw, pb):
            B, S, _ = x.shape
            qkv = (x @ aw + ab).reshape(B, S, H, 3 * HD)
            q, k, v = jnp.split(qkv, 3, axis=-1)
            qk = _hamilton(_to_quaternion(q), _to_quaternion(k))
            qkv_p = _hamilton(qk, _to_quaternion(v))
            f = jnp.fft.fftn(qkv_p.astype(jnp.complex64), axes=(-3, -2))
            out = jnp.fft.ifftn(f * _spectral_filter(S), axes=(-3, -2)).real
            a = out[..., 0] * (1.0 + 0.1 * _modulation(S))
            return a.reshape(B, S, E) @ pw + pb

        def _layer(x, p):
            ln1w, ln1b, aw, ab, pw, pb, ln2w, ln2b, fw, fb, mw, mb = p
            x = x + _attention(_layernorm(x, ln1w, ln1b), aw, ab, pw, pb)
            h = _layernorm(x, ln2w, ln2b)
            h = jax.nn.gelu(h @ fw + fb, approximate=False) @ mw + mb
            return x + h
        key = jax.random.key(seed)
        ks = jax.random.split(key, 6)
        s = 0.02
        return {'x': jax.random.normal(ks[0], (2, 512, E), jnp.float32), 'ln1_w': jnp.ones((L, E), jnp.float32), 'ln1_b': jnp.zeros((L, E), jnp.float32), 'attn_w': jax.random.normal(ks[1], (L, E, 3 * E), jnp.float32) * s, 'attn_b': jnp.zeros((L, 3 * E), jnp.float32), 'aproj_w': jax.random.normal(ks[2], (L, E, E), jnp.float32) * s, 'aproj_b': jnp.zeros((L, E), jnp.float32), 'ln2_w': jnp.ones((L, E), jnp.float32), 'ln2_b': jnp.zeros((L, E), jnp.float32), 'fc_w': jax.random.normal(ks[3], (L, E, 4 * E), jnp.float32) * s, 'fc_b': jnp.zeros((L, 4 * E), jnp.float32), 'mproj_w': jax.random.normal(ks[4], (L, 4 * E, E), jnp.float32) * s, 'mproj_b': jnp.zeros((L, E), jnp.float32)}
    _L0_attn_all = _L0_attn_setup()
    _L0_attn_in = {k: v for k, v in _L0_attn_all.items() if k in ('ln1_w', 'ln1_b', 'attn_w', 'attn_b', 'aproj_w', 'aproj_b', 'ln2_w', 'ln2_b', 'fc_w', 'fc_b', 'mproj_w', 'mproj_b')}
    del _L0_attn_all

    def _L0_ffn_setup():
        import jax, jax.numpy as jnp
        import numpy as np
        D_MODEL = 256
        FFN = 256
        N_EXPERTS = 8
        N_SHARED = 1
        TOP_K = 2
        B, S = (2, 512)

        def _swiglu(h):
            a, b = jnp.split(h, 2, axis=-1)
            return jax.nn.silu(a) * b
        key = jax.random.key(seed)
        ks = jax.random.split(key, 12)
        sc = 0.02
        return {'x': jax.random.normal(ks[0], (B, S, D_MODEL), dtype=jnp.float32), 'gate_w': jax.random.normal(ks[1], (D_MODEL, N_EXPERTS), dtype=jnp.float32) * sc, 'gate_b': jnp.zeros((N_EXPERTS,), dtype=jnp.float32), 'sw1': jax.random.normal(ks[2], (N_SHARED, D_MODEL, 2 * FFN), dtype=jnp.float32) * sc, 'sb1': jnp.zeros((N_SHARED, 2 * FFN), dtype=jnp.float32), 'sw2': jax.random.normal(ks[3], (N_SHARED, FFN, D_MODEL), dtype=jnp.float32) * sc, 'sb2': jnp.zeros((N_SHARED, D_MODEL), dtype=jnp.float32), 'rw1': jax.random.normal(ks[4], (N_EXPERTS, D_MODEL, 2 * FFN), dtype=jnp.float32) * sc, 'rb1': jnp.zeros((N_EXPERTS, 2 * FFN), dtype=jnp.float32), 'rw2': jax.random.normal(ks[5], (N_EXPERTS, FFN, D_MODEL), dtype=jnp.float32) * sc, 'rb2': jnp.zeros((N_EXPERTS, D_MODEL), dtype=jnp.float32)}
    _L0_ffn_all = _L0_ffn_setup()
    _L0_ffn_in = {k: v for k, v in _L0_ffn_all.items() if k in ('gate_w', 'gate_b', 'sw1', 'sb1', 'sw2', 'sb2', 'rw1', 'rb1', 'rw2', 'rb2')}
    del _L0_ffn_all

    def _L1_xattn_setup():
        import jax, jax.numpy as jnp
        import numpy as np
        D_MODEL = 256
        NUM_HEADS = 16
        D_KEY = D_MODEL // NUM_HEADS
        MASK_FUTURE = True
        NEG_INF = -jnp.inf
        key = jax.random.key(seed)
        ks = jax.random.split(key, 7)
        B, N = (4, 512)
        return {'query': jax.random.normal(ks[0], (B, N, D_MODEL), dtype=jnp.float32), 'key': jax.random.normal(ks[1], (B, N, D_MODEL), dtype=jnp.float32), 'value': jax.random.normal(ks[2], (B, N, D_MODEL), dtype=jnp.float32), 'mask': jnp.ones((B, N), dtype=jnp.int32), 'Wq': jax.random.normal(ks[3], (D_MODEL, D_MODEL), dtype=jnp.float32) * 0.02, 'Wk': jax.random.normal(ks[4], (D_MODEL, D_MODEL), dtype=jnp.float32) * 0.02, 'Wv': jax.random.normal(ks[5], (D_MODEL, D_MODEL), dtype=jnp.float32) * 0.02, 'Wo': jax.random.normal(ks[6], (D_MODEL, D_MODEL), dtype=jnp.float32) * 0.02}
    _L1_xattn_all = _L1_xattn_setup()
    _L1_xattn_in = {k: v for k, v in _L1_xattn_all.items() if k in ('Wq', 'Wk', 'Wv', 'Wo')}
    del _L1_xattn_all

    def _L1_attn_setup():
        import jax, jax.numpy as jnp
        import numpy as np
        NUM_HEADS = 16
        GROUP_SIZE = 4
        DIM = 256
        HEAD_DIM = DIM // NUM_HEADS
        NUM_GROUPS = max(1, NUM_HEADS // GROUP_SIZE)
        SCALE = HEAD_DIM ** (-0.5)
        key = jax.random.key(seed)
        k1, k2, k3, k4, k5 = jax.random.split(key, 5)
        B, T = (1, 1024)
        x = jax.random.normal(k1, (B, T, DIM), dtype=jnp.float32)
        Wq = jax.random.normal(k2, (DIM, NUM_HEADS * HEAD_DIM), dtype=jnp.float32) * DIM ** (-0.5)
        Wk = jax.random.normal(k3, (DIM, NUM_GROUPS * HEAD_DIM), dtype=jnp.float32) * DIM ** (-0.5)
        Wv = jax.random.normal(k4, (DIM, NUM_GROUPS * HEAD_DIM), dtype=jnp.float32) * DIM ** (-0.5)
        Wo = jax.random.normal(k5, (NUM_HEADS * HEAD_DIM, DIM), dtype=jnp.float32) * DIM ** (-0.5)
        return {'x': x, 'Wq': Wq, 'Wk': Wk, 'Wv': Wv, 'Wo': Wo}
    _L1_attn_all = _L1_attn_setup()
    _L1_attn_in = {k: v for k, v in _L1_attn_all.items() if k in ('Wq', 'Wk', 'Wv', 'Wo')}
    del _L1_attn_all

    def _L1_ffn_setup():
        import jax, jax.numpy as jnp
        import numpy as np
        TOP_K = 2
        key = jax.random.key(seed)
        k1, k2, k3, k4, k5 = jax.random.split(key, 5)
        B, S, D, F, E = (2, 256, 256, 512, 8)
        return {'x': jax.random.normal(k1, (B, S, D), dtype=jnp.float32), 'router_kernel_DE': jax.random.normal(k2, (D, E), dtype=jnp.float32) * 0.02, 'kernel_gating_EDF': jax.random.normal(k3, (E, D, F), dtype=jnp.float32) * 0.02, 'kernel_up_EDF': jax.random.normal(k4, (E, D, F), dtype=jnp.float32) * 0.02, 'kernel_down_EFD': jax.random.normal(k5, (E, F, D), dtype=jnp.float32) * 0.02}
    _L1_ffn_all = _L1_ffn_setup()
    _L1_ffn_in = {k: v for k, v in _L1_ffn_all.items() if k in ('router_kernel_DE', 'kernel_gating_EDF', 'kernel_up_EDF', 'kernel_down_EFD')}
    del _L1_ffn_all

    def _L2_xattn_setup():
        import jax, jax.numpy as jnp
        import numpy as np
        N_HEADS = 16

        def _split(x, n_heads):
            b, s, d = x.shape
            return x.reshape(b, s, n_heads, d // n_heads).transpose(0, 2, 1, 3)
        key = jax.random.key(seed)
        k1, k2, k3, k4, k5 = jax.random.split(key, 5)
        B, S, D = (4, 512, 256)
        q = jax.random.normal(k1, (B, S, D), dtype=jnp.float32)
        k = jax.random.normal(k2, (B, S, D), dtype=jnp.float32)
        v = jax.random.normal(k3, (B, S, D), dtype=jnp.float32)
        Wq = jax.random.normal(k4, (D, D), dtype=jnp.float32) * D ** (-0.5)
        Wo = jax.random.normal(k5, (D, D), dtype=jnp.float32) * D ** (-0.5)
        return {'q': q, 'k': k, 'v': v, 'Wq': Wq, 'Wo': Wo}
    _L2_xattn_all = _L2_xattn_setup()
    _L2_xattn_in = {k: v for k, v in _L2_xattn_all.items() if k in ('Wq', 'Wo')}
    del _L2_xattn_all

    def _L2_attn_setup():
        import jax, jax.numpy as jnp
        import numpy as np
        NUM_HEADS = 16
        key = jax.random.key(seed)
        ks = jax.random.split(key, 6)
        B, S, D = (2, 512, 256)
        x = jax.random.normal(ks[0], (B, S, D), dtype=jnp.float32)
        s = 1.0 / np.sqrt(D)
        Wq = jax.random.normal(ks[1], (D, D), dtype=jnp.float32) * s
        Wk = jax.random.normal(ks[2], (D, D), dtype=jnp.float32) * s
        Wv = jax.random.normal(ks[3], (D, D), dtype=jnp.float32) * s
        Wff = jax.random.normal(ks[4], (D, D), dtype=jnp.float32) * s
        bff = jax.random.normal(ks[5], (D,), dtype=jnp.float32) * 0.01
        return {'x': x, 'Wq': Wq, 'Wk': Wk, 'Wv': Wv, 'Wff': Wff, 'bff': bff}
    _L2_attn_all = _L2_attn_setup()
    _L2_attn_in = {k: v for k, v in _L2_attn_all.items() if k in ('Wq', 'Wk', 'Wv', 'Wff', 'bff')}
    del _L2_attn_all

    def _L2_ffn_setup():
        import jax, jax.numpy as jnp
        import numpy as np
        B, S, D = (4, 512, 256)
        E, F = (8, 1024)
        key = jax.random.key(seed)
        ks = jax.random.split(key, 5)
        x = jax.random.normal(ks[0], (B, S, D), dtype=jnp.float32)
        switch_w = jax.random.normal(ks[1], (D, E), dtype=jnp.float32) * D ** (-0.5)
        switch_b = jnp.zeros((E,), dtype=jnp.float32)
        w1 = jax.random.normal(ks[2], (E, D, F), dtype=jnp.float32) * D ** (-0.5)
        b1 = jnp.zeros((E, F), dtype=jnp.float32)
        w2 = jax.random.normal(ks[3], (E, F, D), dtype=jnp.float32) * F ** (-0.5)
        b2 = jnp.zeros((E, D), dtype=jnp.float32)
        return {'x': x, 'switch_w': switch_w, 'switch_b': switch_b, 'w1': w1, 'b1': b1, 'w2': w2, 'b2': b2}
    _L2_ffn_all = _L2_ffn_setup()
    _L2_ffn_in = {k: v for k, v in _L2_ffn_all.items() if k in ('switch_w', 'switch_b', 'w1', 'b1', 'w2', 'b2')}
    del _L2_ffn_all

    def _L3_xattn_setup():
        import jax, jax.numpy as jnp
        import numpy as np
        D_MODEL = 256
        NUM_HEADS = 16
        HEAD_DIM = D_MODEL // NUM_HEADS

        def _split_heads(x):
            B, S, _ = x.shape
            return x.reshape(B, S, NUM_HEADS, HEAD_DIM).transpose(0, 2, 1, 3)
        key = jax.random.key(seed)
        ks = jax.random.split(key, 11)
        B, S = (2, 512)
        sc = 1.0 / np.sqrt(D_MODEL)
        inp = {'query': jax.random.normal(ks[0], (B, S, D_MODEL), jnp.float32), 'key': jax.random.normal(ks[1], (B, S, D_MODEL), jnp.float32), 'value': jax.random.normal(ks[2], (B, S, D_MODEL), jnp.float32), 'Wq': jax.random.normal(ks[3], (D_MODEL, D_MODEL), jnp.float32) * sc, 'bq': jnp.zeros((D_MODEL,), jnp.float32), 'Wk': jax.random.normal(ks[4], (D_MODEL, D_MODEL), jnp.float32) * sc, 'bk': jnp.zeros((D_MODEL,), jnp.float32), 'Wv': jax.random.normal(ks[5], (D_MODEL, D_MODEL), jnp.float32) * sc, 'bv': jnp.zeros((D_MODEL,), jnp.float32), 'Wo': jax.random.normal(ks[6], (D_MODEL, D_MODEL), jnp.float32) * sc, 'bo': jnp.zeros((D_MODEL,), jnp.float32)}
        return inp
    _L3_xattn_all = _L3_xattn_setup()
    _L3_xattn_in = {k: v for k, v in _L3_xattn_all.items() if k in ('Wq', 'bq', 'Wk', 'bk', 'Wv', 'bv', 'Wo', 'bo')}
    del _L3_xattn_all

    def _L3_attn_setup():
        import jax, jax.numpy as jnp
        import numpy as np
        DEPTH = 2
        DIM = 256
        SDIM = 64
        B = 64
        S = 64
        EPS = 1e-05

        def _run_selective_scan(x, Wd, bd, Wi, bi, A_log, Wo, bo):
            delta = jax.nn.softplus(jnp.einsum('bsd,dn->bsn', x, Wd) + bd)
            u = jnp.einsum('bsd,dn->bsn', x, Wi) + bi
            decay = jnp.exp(-delta * jax.nn.softplus(A_log))
            drive = delta * u

            def step(h, t):
                d, g = t
                h = d * h + g
                return (h, h)
            h0 = jnp.zeros((x.shape[0], Wd.shape[1]), x.dtype)
            final, hs = jax.lax.scan(step, h0, (decay.swapaxes(0, 1), drive.swapaxes(0, 1)))
            hs = hs.swapaxes(0, 1)
            y = jnp.einsum('bsn,nd->bsd', hs, Wo) + bo
            return (y, final)

        def _reference_tuple_inner(shot_embeddings, Wd, bd, Wi, bi, A_log, Wo, bo, Ws, bs, gamma, beta):
            hidden = shot_embeddings
            class_state = None
            for l in range(Wd.shape[0]):
                hidden, state = _run_selective_scan(hidden, Wd[l], bd[l], Wi[l], bi[l], A_log[l], Wo[l], bo[l])
                class_state = jnp.einsum('bn,nd->bd', state, Ws[l]) + bs[l]
                hidden = hidden + class_state[:, None, :]
            pooled = class_state + hidden.mean(axis=1)
            mu = pooled.mean(axis=-1, keepdims=True)
            var = pooled.var(axis=-1, keepdims=True)
            class_repr = (pooled - mu) / jnp.sqrt(var + EPS) * gamma + beta
            return (class_repr, hidden)
        key = jax.random.key(seed)
        ks = jax.random.split(key, 10)
        sc = 0.02
        return {'shot_embeddings': jax.random.normal(ks[0], (B, S, DIM), jnp.float32), 'Wd': jax.random.normal(ks[1], (DEPTH, DIM, SDIM), jnp.float32) * sc, 'bd': jnp.zeros((DEPTH, SDIM), jnp.float32), 'Wi': jax.random.normal(ks[2], (DEPTH, DIM, SDIM), jnp.float32) * sc, 'bi': jnp.zeros((DEPTH, SDIM), jnp.float32), 'A_log': jax.random.normal(ks[3], (DEPTH, SDIM), jnp.float32), 'Wo': jax.random.normal(ks[4], (DEPTH, SDIM, DIM), jnp.float32) * sc, 'bo': jnp.zeros((DEPTH, DIM), jnp.float32), 'Ws': jax.random.normal(ks[5], (DEPTH, SDIM, DIM), jnp.float32) * sc, 'bs': jnp.zeros((DEPTH, DIM), jnp.float32), 'gamma': jnp.ones((DIM,), jnp.float32), 'beta': jnp.zeros((DIM,), jnp.float32)}
    _L3_attn_all = _L3_attn_setup()
    _L3_attn_in = {k: v for k, v in _L3_attn_all.items() if k in ('Wd', 'bd', 'Wi', 'bi', 'A_log', 'Wo', 'bo', 'Ws', 'bs', 'gamma', 'beta')}
    del _L3_attn_all

    def _L3_ffn_setup():
        import jax, jax.numpy as jnp
        import numpy as np
        B, T, H, F, E, TOPK = (4, 256, 256, 1024, 8, 2)

        def _moe_forward(x, rw, rb, w1, b1, w2, b2, sw1, sb1, sw2, sb2):
            Bb, Tt, Hh = x.shape
            N = Bb * Tt
            Ee = rw.shape[0]
            cap = max(1, int(N / Ee * 1.0))
            xf = x.reshape(N, Hh)
            logits = xf @ rw.T + rb
            g_soft = jax.nn.softmax(logits, axis=-1)
            _, idx = jax.lax.top_k(g_soft, TOPK)
            primary, second = (idx[:, 0], idx[:, 1])
            ohp = jax.nn.one_hot(primary, Ee, dtype=jnp.int32)
            posp = jnp.cumsum(ohp, axis=0) - ohp
            pos_tok = jnp.take_along_axis(posp, primary[:, None], 1)[:, 0]
            keep_primary = pos_tok < cap
            used = jnp.minimum(ohp.sum(axis=0), cap)
            overflow = ~keep_primary
            ohs = jax.nn.one_hot(second, Ee, dtype=jnp.int32) * overflow[:, None].astype(jnp.int32)
            poss = jnp.cumsum(ohs, axis=0) - ohs
            pos2 = jnp.take_along_axis(poss, second[:, None], 1)[:, 0]
            take2 = overflow & (used[second] + pos2 < cap)
            assign = jnp.where(keep_primary, primary, jnp.where(take2, second, -1))
            overflow = overflow & ~take2
            h = jax.nn.gelu(jnp.einsum('nh,ehf->enf', xf, w1) + b1[:, None, :], approximate=False)
            stack = jnp.einsum('enf,efh->enh', h, w2) + b2[:, None, :]
            one_hot_a = jax.nn.one_hot(assign, Ee, dtype=stack.dtype)
            y = jnp.einsum('enh,ne->nh', stack, one_hot_a)
            y_fb = jax.nn.gelu(xf @ sw1 + sb1, approximate=False) @ sw2 + sb2
            y = jnp.where(overflow[:, None], y_fb, y)
            return y.reshape(Bb, Tt, Hh)
        key = jax.random.key(seed)
        ks = jax.random.split(key, 12)
        s = 0.02
        return {'x': jax.random.normal(ks[0], (B, T, H), dtype=jnp.float32), 'rw': jax.random.normal(ks[1], (E, H), dtype=jnp.float32) * s, 'rb': jnp.zeros((E,), dtype=jnp.float32), 'w1': jax.random.normal(ks[2], (E, H, F), dtype=jnp.float32) * s, 'b1': jnp.zeros((E, F), dtype=jnp.float32), 'w2': jax.random.normal(ks[3], (E, F, H), dtype=jnp.float32) * s, 'b2': jnp.zeros((E, H), dtype=jnp.float32), 'sw1': jax.random.normal(ks[4], (H, F), dtype=jnp.float32) * s, 'sb1': jnp.zeros((F,), dtype=jnp.float32), 'sw2': jax.random.normal(ks[5], (F, H), dtype=jnp.float32) * s, 'sb2': jnp.zeros((H,), dtype=jnp.float32)}
    _L3_ffn_all = _L3_ffn_setup()
    _L3_ffn_in = {k: v for k, v in _L3_ffn_all.items() if k in ('rw', 'rb', 'w1', 'b1', 'w2', 'b2', 'sw1', 'sb1', 'sw2', 'sb2')}
    del _L3_ffn_all
    return {'x': x, 'ctx_1024': ctx_1024, 'mask_BxS2_if1': mask_BxS2_if1, 'L0_xattn_gamma_media': _L0_xattn_in['gamma_media'], 'L0_xattn_beta_media': _L0_xattn_in['beta_media'], 'L0_xattn_gamma_lat': _L0_xattn_in['gamma_lat'], 'L0_xattn_beta_lat': _L0_xattn_in['beta_lat'], 'L0_xattn_Wq': _L0_xattn_in['Wq'], 'L0_xattn_bq': _L0_xattn_in['bq'], 'L0_xattn_Wkv': _L0_xattn_in['Wkv'], 'L0_xattn_bkv': _L0_xattn_in['bkv'], 'L0_xattn_Wo': _L0_xattn_in['Wo'], 'L0_xattn_bo': _L0_xattn_in['bo'], 'L0_attn_ln1_w': _L0_attn_in['ln1_w'], 'L0_attn_ln1_b': _L0_attn_in['ln1_b'], 'L0_attn_attn_w': _L0_attn_in['attn_w'], 'L0_attn_attn_b': _L0_attn_in['attn_b'], 'L0_attn_aproj_w': _L0_attn_in['aproj_w'], 'L0_attn_aproj_b': _L0_attn_in['aproj_b'], 'L0_attn_ln2_w': _L0_attn_in['ln2_w'], 'L0_attn_ln2_b': _L0_attn_in['ln2_b'], 'L0_attn_fc_w': _L0_attn_in['fc_w'], 'L0_attn_fc_b': _L0_attn_in['fc_b'], 'L0_attn_mproj_w': _L0_attn_in['mproj_w'], 'L0_attn_mproj_b': _L0_attn_in['mproj_b'], 'L0_ffn_gate_w': _L0_ffn_in['gate_w'], 'L0_ffn_gate_b': _L0_ffn_in['gate_b'], 'L0_ffn_sw1': _L0_ffn_in['sw1'], 'L0_ffn_sb1': _L0_ffn_in['sb1'], 'L0_ffn_sw2': _L0_ffn_in['sw2'], 'L0_ffn_sb2': _L0_ffn_in['sb2'], 'L0_ffn_rw1': _L0_ffn_in['rw1'], 'L0_ffn_rb1': _L0_ffn_in['rb1'], 'L0_ffn_rw2': _L0_ffn_in['rw2'], 'L0_ffn_rb2': _L0_ffn_in['rb2'], 'L1_xattn_Wq': _L1_xattn_in['Wq'], 'L1_xattn_Wk': _L1_xattn_in['Wk'], 'L1_xattn_Wv': _L1_xattn_in['Wv'], 'L1_xattn_Wo': _L1_xattn_in['Wo'], 'L1_attn_Wq': _L1_attn_in['Wq'], 'L1_attn_Wk': _L1_attn_in['Wk'], 'L1_attn_Wv': _L1_attn_in['Wv'], 'L1_attn_Wo': _L1_attn_in['Wo'], 'L1_ffn_router_kernel_DE': _L1_ffn_in['router_kernel_DE'], 'L1_ffn_kernel_gating_EDF': _L1_ffn_in['kernel_gating_EDF'], 'L1_ffn_kernel_up_EDF': _L1_ffn_in['kernel_up_EDF'], 'L1_ffn_kernel_down_EFD': _L1_ffn_in['kernel_down_EFD'], 'L2_xattn_Wq': _L2_xattn_in['Wq'], 'L2_xattn_Wo': _L2_xattn_in['Wo'], 'L2_attn_Wq': _L2_attn_in['Wq'], 'L2_attn_Wk': _L2_attn_in['Wk'], 'L2_attn_Wv': _L2_attn_in['Wv'], 'L2_attn_Wff': _L2_attn_in['Wff'], 'L2_attn_bff': _L2_attn_in['bff'], 'L2_ffn_switch_w': _L2_ffn_in['switch_w'], 'L2_ffn_switch_b': _L2_ffn_in['switch_b'], 'L2_ffn_w1': _L2_ffn_in['w1'], 'L2_ffn_b1': _L2_ffn_in['b1'], 'L2_ffn_w2': _L2_ffn_in['w2'], 'L2_ffn_b2': _L2_ffn_in['b2'], 'L3_xattn_Wq': _L3_xattn_in['Wq'], 'L3_xattn_bq': _L3_xattn_in['bq'], 'L3_xattn_Wk': _L3_xattn_in['Wk'], 'L3_xattn_bk': _L3_xattn_in['bk'], 'L3_xattn_Wv': _L3_xattn_in['Wv'], 'L3_xattn_bv': _L3_xattn_in['bv'], 'L3_xattn_Wo': _L3_xattn_in['Wo'], 'L3_xattn_bo': _L3_xattn_in['bo'], 'L3_attn_Wd': _L3_attn_in['Wd'], 'L3_attn_bd': _L3_attn_in['bd'], 'L3_attn_Wi': _L3_attn_in['Wi'], 'L3_attn_bi': _L3_attn_in['bi'], 'L3_attn_A_log': _L3_attn_in['A_log'], 'L3_attn_Wo': _L3_attn_in['Wo'], 'L3_attn_bo': _L3_attn_in['bo'], 'L3_attn_Ws': _L3_attn_in['Ws'], 'L3_attn_bs': _L3_attn_in['bs'], 'L3_attn_gamma': _L3_attn_in['gamma'], 'L3_attn_beta': _L3_attn_in['beta'], 'L3_ffn_rw': _L3_ffn_in['rw'], 'L3_ffn_rb': _L3_ffn_in['rb'], 'L3_ffn_w1': _L3_ffn_in['w1'], 'L3_ffn_b1': _L3_ffn_in['b1'], 'L3_ffn_w2': _L3_ffn_in['w2'], 'L3_ffn_b2': _L3_ffn_in['b2'], 'L3_ffn_sw1': _L3_ffn_in['sw1'], 'L3_ffn_sb1': _L3_ffn_in['sb1'], 'L3_ffn_sw2': _L3_ffn_in['sw2'], 'L3_ffn_sb2': _L3_ffn_in['sb2']}

def reference(x, ctx_1024, mask_BxS2_if1, L0_xattn_gamma_media, L0_xattn_beta_media, L0_xattn_gamma_lat, L0_xattn_beta_lat, L0_xattn_Wq, L0_xattn_bq, L0_xattn_Wkv, L0_xattn_bkv, L0_xattn_Wo, L0_xattn_bo, L0_attn_ln1_w, L0_attn_ln1_b, L0_attn_attn_w, L0_attn_attn_b, L0_attn_aproj_w, L0_attn_aproj_b, L0_attn_ln2_w, L0_attn_ln2_b, L0_attn_fc_w, L0_attn_fc_b, L0_attn_mproj_w, L0_attn_mproj_b, L0_ffn_gate_w, L0_ffn_gate_b, L0_ffn_sw1, L0_ffn_sb1, L0_ffn_sw2, L0_ffn_sb2, L0_ffn_rw1, L0_ffn_rb1, L0_ffn_rw2, L0_ffn_rb2, L1_xattn_Wq, L1_xattn_Wk, L1_xattn_Wv, L1_xattn_Wo, L1_attn_Wq, L1_attn_Wk, L1_attn_Wv, L1_attn_Wo, L1_ffn_router_kernel_DE, L1_ffn_kernel_gating_EDF, L1_ffn_kernel_up_EDF, L1_ffn_kernel_down_EFD, L2_xattn_Wq, L2_xattn_Wo, L2_attn_Wq, L2_attn_Wk, L2_attn_Wv, L2_attn_Wff, L2_attn_bff, L2_ffn_switch_w, L2_ffn_switch_b, L2_ffn_w1, L2_ffn_b1, L2_ffn_w2, L2_ffn_b2, L3_xattn_Wq, L3_xattn_bq, L3_xattn_Wk, L3_xattn_bk, L3_xattn_Wv, L3_xattn_bv, L3_xattn_Wo, L3_xattn_bo, L3_attn_Wd, L3_attn_bd, L3_attn_Wi, L3_attn_bi, L3_attn_A_log, L3_attn_Wo, L3_attn_bo, L3_attn_Ws, L3_attn_bs, L3_attn_gamma, L3_attn_beta, L3_ffn_rw, L3_ffn_rb, L3_ffn_w1, L3_ffn_b1, L3_ffn_w2, L3_ffn_b2, L3_ffn_sw1, L3_ffn_sb1, L3_ffn_sw2, L3_ffn_sb2):
    import jax
    import jax.numpy as jnp

    def _L0_xattn_ref(x, latents, gamma_media, beta_media, gamma_lat, beta_lat, Wq, bq, Wkv, bkv, Wo, bo):
        import jax, jax.numpy as jnp
        import numpy as np
        B, M, N, DIM, DH, H = (8, 1024, 64, 256, 128, 8)
        INNER = DH * H
        EPS = 1e-05

        def _layernorm(x, g, b):
            mu = jnp.mean(x, axis=-1, keepdims=True)
            var = jnp.var(x, axis=-1, keepdims=True)
            return (x - mu) * jax.lax.rsqrt(var + EPS) * g + b
        b = x.shape[0]
        xn = _layernorm(x, gamma_media, beta_media)
        ln = _layernorm(latents, gamma_lat, beta_lat)
        q = ln @ Wq + bq
        kv_input = jnp.concatenate([xn, ln], axis=1)
        kv = kv_input @ Wkv + bkv
        k, v = jnp.split(kv, 2, axis=-1)

        def to_heads(t):
            return t.reshape(b, t.shape[1], H, DH).transpose(0, 2, 1, 3)
        q, k, v = (to_heads(q), to_heads(k), to_heads(v))
        q = q * DH ** (-0.5)
        sim = jnp.einsum('bhid,bhjd->bhij', q, k)
        attn = jax.nn.softmax(sim, axis=-1)
        out = jnp.einsum('bhij,bhjd->bhid', attn, v)
        out = out.transpose(0, 2, 1, 3).reshape(b, -1, INNER)
        return out @ Wo + bo

    def _L0_attn_ref(x, ln1_w, ln1_b, attn_w, attn_b, aproj_w, aproj_b, ln2_w, ln2_b, fc_w, fc_b, mproj_w, mproj_b):
        import jax, jax.numpy as jnp
        import numpy as np
        L, E, H = (4, 256, 16)
        HD = E // H
        EPS_LN = 1e-05

        def _layernorm(x, w, b):
            m = jnp.mean(x, axis=-1, keepdims=True)
            v = jnp.mean((x - m) ** 2, axis=-1, keepdims=True)
            return (x - m) / jnp.sqrt(v + EPS_LN) * w + b

        def _to_quaternion(x):
            p1 = jnp.diff(x, axis=1, prepend=x[:, :1])
            p2 = jnp.roll(x, 1, axis=2)
            p3 = jnp.cos(x)
            return jnp.stack([x, p1, p2, p3], axis=-1)

        def _hamilton(a, b):
            a0, a1, a2, a3 = (a[..., 0], a[..., 1], a[..., 2], a[..., 3])
            b0, b1, b2, b3 = (b[..., 0], b[..., 1], b[..., 2], b[..., 3])
            return jnp.stack([a0 * b0 - a1 * b1 - a2 * b2 - a3 * b3, a0 * b1 + a1 * b0 + a2 * b3 - a3 * b2, a0 * b2 - a1 * b3 + a2 * b0 + a3 * b1, a0 * b3 + a1 * b2 - a2 * b1 + a3 * b0], axis=-1)

        def _spectral_filter(S):
            ks = jnp.fft.fftfreq(S).astype(jnp.float32)[:, None, None]
            kh = jnp.fft.fftfreq(H).astype(jnp.float32)[None, :, None]
            kd = jnp.fft.fftfreq(HD).astype(jnp.float32)[None, None, :]
            km = jnp.sqrt(ks ** 2 + kh ** 2 + kd ** 2 + 1e-10)
            f = jnp.exp(1j * jnp.arctan(jnp.log(km + 1e-10)))
            return f[None, :, :, :, None].astype(jnp.complex64)

        def _modulation(S):
            lam = jnp.arange(S, dtype=jnp.float32) / S
            t = jnp.arange(S, dtype=jnp.float32) * 0.1
            probe = jnp.sin(t + lam)
            phase = t - 2.0 * lam + 0.5 * lam ** 2
            return (probe * jnp.cos(phase))[None, :, None, None]

        def _attention(x, aw, ab, pw, pb):
            B, S, _ = x.shape
            qkv = (x @ aw + ab).reshape(B, S, H, 3 * HD)
            q, k, v = jnp.split(qkv, 3, axis=-1)
            qk = _hamilton(_to_quaternion(q), _to_quaternion(k))
            qkv_p = _hamilton(qk, _to_quaternion(v))
            f = jnp.fft.fftn(qkv_p.astype(jnp.complex64), axes=(-3, -2))
            out = jnp.fft.ifftn(f * _spectral_filter(S), axes=(-3, -2)).real
            a = out[..., 0] * (1.0 + 0.1 * _modulation(S))
            return a.reshape(B, S, E) @ pw + pb

        def _layer(x, p):
            ln1w, ln1b, aw, ab, pw, pb, ln2w, ln2b, fw, fb, mw, mb = p
            x = x + _attention(_layernorm(x, ln1w, ln1b), aw, ab, pw, pb)
            h = _layernorm(x, ln2w, ln2b)
            h = jax.nn.gelu(h @ fw + fb, approximate=False) @ mw + mb
            return x + h
        for i in range(L):
            x = _layer(x, (ln1_w[i], ln1_b[i], attn_w[i], attn_b[i], aproj_w[i], aproj_b[i], ln2_w[i], ln2_b[i], fc_w[i], fc_b[i], mproj_w[i], mproj_b[i]))
        return x

    def _L0_ffn_ref(x, gate_w, gate_b, sw1, sb1, sw2, sb2, rw1, rb1, rw2, rb2):
        import jax, jax.numpy as jnp
        import numpy as np
        D_MODEL = 256
        FFN = 256
        N_EXPERTS = 8
        N_SHARED = 1
        TOP_K = 2
        B, S = (2, 512)

        def _swiglu(h):
            a, b = jnp.split(h, 2, axis=-1)
            return jax.nn.silu(a) * b
        hs = jnp.einsum('bsd,ndf->nbsf', x, sw1) + sb1[:, None, None, :]
        shared_out = jnp.einsum('nbsf,nfd->bsd', _swiglu(hs), sw2) + sb2.sum(0)
        probs = jax.nn.softmax(x @ gate_w + gate_b, axis=-1)
        topk_probs, topk_idx = jax.lax.top_k(probs, TOP_K)
        cw = jnp.sum(jax.nn.one_hot(topk_idx, N_EXPERTS, dtype=x.dtype) * topk_probs[..., None], axis=2)
        hr = jnp.einsum('bsd,edf->ebsf', x, rw1) + rb1[:, None, None, :]
        out_e = jnp.einsum('ebsf,efd->ebsd', _swiglu(hr), rw2) + rb2[:, None, None, :]
        routed_out = jnp.einsum('ebsd,bse->bsd', out_e, cw)
        return shared_out + routed_out

    def _L1_xattn_ref(query, key, value, mask, Wq, Wk, Wv, Wo):
        import jax, jax.numpy as jnp
        import numpy as np
        D_MODEL = 256
        NUM_HEADS = 16
        D_KEY = D_MODEL // NUM_HEADS
        MASK_FUTURE = True
        NEG_INF = -jnp.inf
        B, Nq, _ = query.shape
        Nk = key.shape[1]

        def proj(x, W, N):
            return (x @ W).reshape(B, N, NUM_HEADS, D_KEY).transpose(0, 2, 1, 3)
        Q = proj(query, Wq, Nq)
        K = proj(key, Wk, Nk)
        V = proj(value, Wv, Nk)
        scores = jnp.einsum('bhqd,bhkd->bhqk', Q, K) / np.sqrt(D_KEY).astype(np.float32)
        scores = jnp.where(mask[:, None, None, :] == 0, NEG_INF, scores)
        if MASK_FUTURE:
            causal = jnp.triu(jnp.ones((Nq, Nk), dtype=jnp.bool_), k=1)
            scores = jnp.where(causal[None, None, :, :], NEG_INF, scores)
        attn = jax.nn.softmax(scores, axis=-1)
        out = jnp.einsum('bhqk,bhkd->bhqd', attn, V)
        out = out.transpose(0, 2, 1, 3).reshape(B, Nq, D_MODEL)
        return out @ Wo

    def _L1_attn_ref(x, Wq, Wk, Wv, Wo):
        import jax, jax.numpy as jnp
        import numpy as np
        NUM_HEADS = 16
        GROUP_SIZE = 4
        DIM = 256
        HEAD_DIM = DIM // NUM_HEADS
        NUM_GROUPS = max(1, NUM_HEADS // GROUP_SIZE)
        SCALE = HEAD_DIM ** (-0.5)
        B, T, C = x.shape
        rep = NUM_HEADS // NUM_GROUPS
        q = (x @ Wq).reshape(B, T, NUM_HEADS, HEAD_DIM)
        k = (x @ Wk).reshape(B, T, NUM_GROUPS, HEAD_DIM)
        v = (x @ Wv).reshape(B, T, NUM_GROUPS, HEAD_DIM)
        k = jnp.repeat(k, rep, axis=2)
        v = jnp.repeat(v, rep, axis=2)
        scores = jnp.einsum('bqhd,bkhd->bhqk', q, k) * SCALE
        weights = jax.nn.softmax(scores, axis=-1)
        out = jnp.einsum('bhqk,bkhd->bqhd', weights, v)
        out = out.reshape(B, T, NUM_HEADS * HEAD_DIM)
        return out @ Wo

    def _L1_ffn_ref(x, router_kernel_DE, kernel_gating_EDF, kernel_up_EDF, kernel_down_EFD):
        import jax, jax.numpy as jnp
        import numpy as np
        TOP_K = 2
        E = router_kernel_DE.shape[-1]
        x = x.astype(jnp.float32)
        logits_BSE = jnp.einsum('BSD,DE->BSE', x, router_kernel_DE)
        probs_BSE = jax.nn.softmax(logits_BSE.astype(jnp.float32), axis=-1)
        weights_BSK, indices_BSK = jax.lax.top_k(probs_BSE, TOP_K)
        norm_weights_BSK = jax.nn.softmax(weights_BSK, axis=-1)
        one_hot_BSKE = jax.nn.one_hot(indices_BSK, num_classes=E, dtype=x.dtype)
        full_weights_BSE = jnp.sum(one_hot_BSKE * norm_weights_BSK[..., None], axis=2)
        gating_BSEF = jnp.einsum('BSD,EDF->BSEF', x, kernel_gating_EDF)
        act_BSEF = jax.nn.silu(gating_BSEF)
        up_BSEF = jnp.einsum('BSD,EDF->BSEF', x, kernel_up_EDF)
        fuse_BSEF = act_BSEF * up_BSEF
        down_BSED = jnp.einsum('BSEF,EFD->BSED', fuse_BSEF, kernel_down_EFD)
        out_BSD = jnp.einsum('BSED,BSE->BSD', down_BSED, full_weights_BSE)
        return out_BSD.astype(jnp.float32)

    def _L2_xattn_ref(q, k, v, Wq, Wo):
        import jax, jax.numpy as jnp
        import numpy as np
        N_HEADS = 16

        def _split(x, n_heads):
            b, s, d = x.shape
            return x.reshape(b, s, n_heads, d // n_heads).transpose(0, 2, 1, 3)
        d_model = q.shape[-1]
        d_k = d_model // N_HEADS
        Q = _split(q @ Wq.T, N_HEADS)
        K = _split(k @ Wq.T, N_HEADS)
        V = _split(v @ Wq.T, N_HEADS)
        scores = jnp.einsum('bhqd,bhkd->bhqk', Q, K) / jnp.sqrt(jnp.asarray(d_k, Q.dtype))
        attn = jax.nn.softmax(scores, axis=-1)
        out = jnp.einsum('bhqk,bhkd->bhqd', attn, V)
        b, h, s, dk = out.shape
        out = out.transpose(0, 2, 1, 3).reshape(b, s, h * dk)
        return out @ Wo.T

    def _L2_attn_ref(x, Wq, Wk, Wv, Wff, bff):
        import jax, jax.numpy as jnp
        import numpy as np
        NUM_HEADS = 16
        B, S, D = x.shape
        H = NUM_HEADS
        Dh = D // H
        q = x @ Wq.T * (1.0 / jnp.sqrt(jnp.asarray(D, x.dtype)))
        k = x @ Wk.T
        v = x @ Wv.T
        q = q.reshape(B, S, H, Dh)
        k = k.reshape(B, S, H, Dh)
        v = v.reshape(B, S, H, Dh)
        scores = jnp.einsum('bqhd,bkhd->bhqk', q, k)
        attn = jax.nn.softmax(scores, axis=-1)
        out = jnp.einsum('bhqk,bkhd->bqhd', attn, v).reshape(B, S, D)
        return out @ Wff.T + bff

    def _L2_ffn_ref(x, switch_w, switch_b, w1, b1, w2, b2):
        import jax, jax.numpy as jnp
        import numpy as np
        B, S, D = (4, 512, 256)
        E, F = (8, 1024)
        b, s, d = x.shape
        t = x.reshape(-1, d)
        logits = t @ switch_w + switch_b
        route_prob = jax.nn.softmax(logits, axis=-1)
        route_prob_max = jnp.max(route_prob, axis=-1)
        routes = jnp.argmax(route_prob, axis=-1)
        out = jnp.zeros_like(t)
        n_experts = w1.shape[0]
        for e in range(n_experts):
            h = jax.nn.gelu(t @ w1[e] + b1[e])
            y = h @ w2[e] + b2[e]
            mask = (routes == e)[:, None]
            out = jnp.where(mask, y, out)
        out = out * route_prob_max[:, None]
        return out.reshape(b, s, d)

    def _L3_xattn_ref(query, key, value, Wq, bq, Wk, bk, Wv, bv, Wo, bo):
        import jax, jax.numpy as jnp
        import numpy as np
        D_MODEL = 256
        NUM_HEADS = 16
        HEAD_DIM = D_MODEL // NUM_HEADS

        def _split_heads(x):
            B, S, _ = x.shape
            return x.reshape(B, S, NUM_HEADS, HEAD_DIM).transpose(0, 2, 1, 3)
        Q = _split_heads(query @ Wq.T + bq)
        K = _split_heads(key @ Wk.T + bk)
        V = _split_heads(value @ Wv.T + bv)
        scores = jnp.einsum('bhqd,bhkd->bhqk', Q, K) / jnp.sqrt(jnp.float32(HEAD_DIM))
        attn = jax.nn.softmax(scores, axis=-1)
        out = jnp.einsum('bhqk,bhkd->bhqd', attn, V)
        B, H, S, Dh = out.shape
        out = out.transpose(0, 2, 1, 3).reshape(B, S, H * Dh)
        return out @ Wo.T + bo

    def _L3_attn_ref(shot_embeddings, Wd, bd, Wi, bi, A_log, Wo, bo, Ws, bs, gamma, beta):
        import jax, jax.numpy as jnp
        import numpy as np
        DEPTH = 2
        DIM = 256
        SDIM = 64
        B = 64
        S = 64
        EPS = 1e-05

        def _run_selective_scan(x, Wd, bd, Wi, bi, A_log, Wo, bo):
            delta = jax.nn.softplus(jnp.einsum('bsd,dn->bsn', x, Wd) + bd)
            u = jnp.einsum('bsd,dn->bsn', x, Wi) + bi
            decay = jnp.exp(-delta * jax.nn.softplus(A_log))
            drive = delta * u

            def step(h, t):
                d, g = t
                h = d * h + g
                return (h, h)
            h0 = jnp.zeros((x.shape[0], Wd.shape[1]), x.dtype)
            final, hs = jax.lax.scan(step, h0, (decay.swapaxes(0, 1), drive.swapaxes(0, 1)))
            hs = hs.swapaxes(0, 1)
            y = jnp.einsum('bsn,nd->bsd', hs, Wo) + bo
            return (y, final)

        def _reference_tuple_inner(shot_embeddings, Wd, bd, Wi, bi, A_log, Wo, bo, Ws, bs, gamma, beta):
            hidden = shot_embeddings
            class_state = None
            for l in range(Wd.shape[0]):
                hidden, state = _run_selective_scan(hidden, Wd[l], bd[l], Wi[l], bi[l], A_log[l], Wo[l], bo[l])
                class_state = jnp.einsum('bn,nd->bd', state, Ws[l]) + bs[l]
                hidden = hidden + class_state[:, None, :]
            pooled = class_state + hidden.mean(axis=1)
            mu = pooled.mean(axis=-1, keepdims=True)
            var = pooled.var(axis=-1, keepdims=True)
            class_repr = (pooled - mu) / jnp.sqrt(var + EPS) * gamma + beta
            return (class_repr, hidden)
        return _reference_tuple_inner(shot_embeddings, Wd, bd, Wi, bi, A_log, Wo, bo, Ws, bs, gamma, beta)[1]

    def _L3_ffn_ref(x, rw, rb, w1, b1, w2, b2, sw1, sb1, sw2, sb2):
        import jax, jax.numpy as jnp
        import numpy as np
        B, T, H, F, E, TOPK = (4, 256, 256, 1024, 8, 2)

        def _moe_forward(x, rw, rb, w1, b1, w2, b2, sw1, sb1, sw2, sb2):
            Bb, Tt, Hh = x.shape
            N = Bb * Tt
            Ee = rw.shape[0]
            cap = max(1, int(N / Ee * 1.0))
            xf = x.reshape(N, Hh)
            logits = xf @ rw.T + rb
            g_soft = jax.nn.softmax(logits, axis=-1)
            _, idx = jax.lax.top_k(g_soft, TOPK)
            primary, second = (idx[:, 0], idx[:, 1])
            ohp = jax.nn.one_hot(primary, Ee, dtype=jnp.int32)
            posp = jnp.cumsum(ohp, axis=0) - ohp
            pos_tok = jnp.take_along_axis(posp, primary[:, None], 1)[:, 0]
            keep_primary = pos_tok < cap
            used = jnp.minimum(ohp.sum(axis=0), cap)
            overflow = ~keep_primary
            ohs = jax.nn.one_hot(second, Ee, dtype=jnp.int32) * overflow[:, None].astype(jnp.int32)
            poss = jnp.cumsum(ohs, axis=0) - ohs
            pos2 = jnp.take_along_axis(poss, second[:, None], 1)[:, 0]
            take2 = overflow & (used[second] + pos2 < cap)
            assign = jnp.where(keep_primary, primary, jnp.where(take2, second, -1))
            overflow = overflow & ~take2
            h = jax.nn.gelu(jnp.einsum('nh,ehf->enf', xf, w1) + b1[:, None, :], approximate=False)
            stack = jnp.einsum('enf,efh->enh', h, w2) + b2[:, None, :]
            one_hot_a = jax.nn.one_hot(assign, Ee, dtype=stack.dtype)
            y = jnp.einsum('enh,ne->nh', stack, one_hot_a)
            y_fb = jax.nn.gelu(xf @ sw1 + sb1, approximate=False) @ sw2 + sb2
            y = jnp.where(overflow[:, None], y_fb, y)
            return y.reshape(Bb, Tt, Hh)
        return _moe_forward(x, rw, rb, w1, b1, w2, b2, sw1, sb1, sw2, sb2)
    x = x + _L0_xattn_ref(ctx_1024, _layernorm(x, axis=-1), L0_xattn_gamma_media, L0_xattn_beta_media, L0_xattn_gamma_lat, L0_xattn_beta_lat, L0_xattn_Wq, L0_xattn_bq, L0_xattn_Wkv, L0_xattn_bkv, L0_xattn_Wo, L0_xattn_bo)
    x = x + _L0_attn_ref(_layernorm(x, axis=-1), L0_attn_ln1_w, L0_attn_ln1_b, L0_attn_attn_w, L0_attn_attn_b, L0_attn_aproj_w, L0_attn_aproj_b, L0_attn_ln2_w, L0_attn_ln2_b, L0_attn_fc_w, L0_attn_fc_b, L0_attn_mproj_w, L0_attn_mproj_b)
    x = x + _L0_ffn_ref(_layernorm(x, axis=-1), L0_ffn_gate_w, L0_ffn_gate_b, L0_ffn_sw1, L0_ffn_sb1, L0_ffn_sw2, L0_ffn_sb2, L0_ffn_rw1, L0_ffn_rb1, L0_ffn_rw2, L0_ffn_rb2)
    x = x + _L1_xattn_ref(_layernorm(x, axis=-1), ctx_1024, ctx_1024, mask_BxS2_if1, L1_xattn_Wq, L1_xattn_Wk, L1_xattn_Wv, L1_xattn_Wo)
    x = x + _L1_attn_ref(_layernorm(x, axis=-1), L1_attn_Wq, L1_attn_Wk, L1_attn_Wv, L1_attn_Wo)
    x = x + _L1_ffn_ref(_layernorm(x, axis=-1), L1_ffn_router_kernel_DE, L1_ffn_kernel_gating_EDF, L1_ffn_kernel_up_EDF, L1_ffn_kernel_down_EFD)
    x = x + _L2_xattn_ref(_layernorm(x, axis=-1), ctx_1024, ctx_1024, L2_xattn_Wq, L2_xattn_Wo)
    x = x + _L2_attn_ref(_layernorm(x, axis=-1), L2_attn_Wq, L2_attn_Wk, L2_attn_Wv, L2_attn_Wff, L2_attn_bff)
    x = x + _L2_ffn_ref(_layernorm(x, axis=-1), L2_ffn_switch_w, L2_ffn_switch_b, L2_ffn_w1, L2_ffn_b1, L2_ffn_w2, L2_ffn_b2)
    x = x + _L3_xattn_ref(_layernorm(x, axis=-1), ctx_1024, ctx_1024, L3_xattn_Wq, L3_xattn_bq, L3_xattn_Wk, L3_xattn_bk, L3_xattn_Wv, L3_xattn_bv, L3_xattn_Wo, L3_xattn_bo)
    x = x + _L3_attn_ref(_layernorm(x, axis=-1), L3_attn_Wd, L3_attn_bd, L3_attn_Wi, L3_attn_bi, L3_attn_A_log, L3_attn_Wo, L3_attn_bo, L3_attn_Ws, L3_attn_bs, L3_attn_gamma, L3_attn_beta)
    x = x + _L3_ffn_ref(_layernorm(x, axis=-1), L3_ffn_rw, L3_ffn_rb, L3_ffn_w1, L3_ffn_b1, L3_ffn_w2, L3_ffn_b2, L3_ffn_sw1, L3_ffn_sb1, L3_ffn_sw2, L3_ffn_sb2)
    return x

_drawn_inputs = setup_inputs


def setup_inputs(seed=0):
    import zlib

    import numpy as np

    out = dict(_drawn_inputs(seed))
    spreads = {'L0_xattn_gamma_media': (1.0, 0.2),
     'L0_xattn_beta_media': (0.0, 0.281),
     'L0_xattn_gamma_lat': (1.0, 0.6),
     'L0_xattn_beta_lat': (0.0, 0.8),
     'L0_xattn_bq': (0.0, 0.8),
     'L0_xattn_bkv': (0.0, 0.1),
     'L0_xattn_bo': (0.0, 0.1),
     'L0_attn_ln1_w': (1.0, 0.2),
     'L0_attn_ln1_b': (0.0, 0.333),
     'L0_attn_attn_b': (0.0, 0.1),
     'L0_attn_aproj_b': (0.0, 0.1),
     'L0_attn_ln2_w': (1.0, 0.556),
     'L0_attn_ln2_b': (0.0, 0.475),
     'L0_attn_fc_b': (0.0, 0.1),
     'L0_attn_mproj_b': (0.0, 0.1),
     'L0_ffn_gate_b': (0.0, 0.788),
     'L0_ffn_sb1': (0.0, 0.8),
     'L0_ffn_sb2': (0.0, 0.1),
     'L0_ffn_rb1': (0.0, 0.8),
     'L0_ffn_rb2': (0.0, 0.457),
     'L2_ffn_switch_b': (0.0, 1.02),
     'L2_ffn_b1': (0.0, 1.364),
     'L2_ffn_b2': (0.0, 1.221),
     'L3_xattn_bq': (0.0, 1.705),
     'L3_xattn_bk': (0.0, 2.0),
     'L3_xattn_bv': (0.0, 0.361),
     'L3_xattn_bo': (0.0, 0.394),
     'L3_attn_bd': (0.0, 2.0),
     'L3_attn_bi': (0.0, 0.303),
     'L3_attn_bo': (0.0, 0.479),
     'L3_attn_bs': (0.0, 0.377),
     'L3_attn_gamma': (1.0, 0.2),
     'L3_attn_beta': (0.0, 0.1),
     'L3_ffn_rb': (0.0, 0.1),
     'L3_ffn_b1': (0.0, 1.781),
     'L3_ffn_b2': (0.0, 0.712),
     'L3_ffn_sb1': (0.0, 0.8),
     'L3_ffn_sb2': (0.0, 1.877)}
    factors = {'L0_xattn_Wq': 7.364,
     'L0_ffn_gate_w': 4.254,
     'L0_ffn_sw1': 3.807,
     'L0_ffn_sw2': 3.77,
     'L0_ffn_rw1': 8.0,
     'L0_ffn_rw2': 8.0,
     'L1_xattn_Wq': 8.0,
     'L1_xattn_Wk': 8.0,
     'L1_ffn_router_kernel_DE': 4.431,
     'L1_ffn_kernel_gating_EDF': 4.508,
     'L1_ffn_kernel_up_EDF': 4.042,
     'L1_ffn_kernel_down_EFD': 4.789,
     'L2_attn_bff': 25.396,
     'L3_attn_Wd': 8.0,
     'L3_attn_Wi': 2.74,
     'L3_ffn_sw1': 3.153,
     'L3_ffn_sw2': 2.92,
     'L2_attn_Wq': 5.484,
     'L2_attn_Wk': 6.841,
     'L3_ffn_w1': 3.926}
    for name, (base, spread) in spreads.items():
        noise = np.random.default_rng([zlib.crc32(name.encode()), seed]).standard_normal(out[name].shape)
        drawn = base * np.exp(spread * noise) if base else spread * noise
        out[name] = jnp.asarray(drawn.astype(out[name].dtype))
    for name, factor in factors.items():
        out[name] = (out[name] * factor).astype(out[name].dtype)
    return out
```

```python
from contextlib import ExitStack

import numpy as np

import concourse.bass as bass
from concourse import mybir

F32 = mybir.dt.float32
I32 = mybir.dt.int32
ALU = mybir.AluOpType
ACT = mybir.ActivationFunctionType
AX = mybir.AxisListType
ds = bass.ds

P = 128
B, S, D = 8, 64, 256
N = B * S
T = N // P
K2 = D // P
KEYS = 1601
FULL = KEYS // P
TAIL = KEYS - FULL * P
KT = FULL + 1
H0, DH0 = 8, 128
H = 16
HD = D // H
HG = P // HD
E = 8
LAYERS = 4
CAP = N // E
BLOCKED = -1e30
EPS = 1e-5
TWO_PI = float(2 * np.pi)
ROUND = 1.5 * 2 ** 23
CHUNK = 512

COLS = dict(g_media=2, b_media=2, g_lat=2, b_lat=2, bq0=8, bv0=8,
            ln1_w=8, ln1_b=8, ln2_w=8, ln2_b=8, fc_b=32,
            sw_b1=36, l2_b1=64, l3_b1=72, bq3=2, bk3=2, bv3=2, bo_scan=4, bs_scan=4)
CONSTS = dict(ident=P, same_batch=P, causal=P, diff=P, head_of=HG, first_of=E, spectrum=2 * S, basis=2 * D,
              split9=E + 1, rest9=1)
ROWS = dict(bo0=D, aproj_b=LAYERS * D, mproj_b=LAYERS * D, gate_b=E, switch_b=E, router_b=E, bff2=D, bo3=D)


def offsets(widths):
    at, out = 0, {}
    for name, w in widths.items():
        out[name] = (at, w)
        at += w
    return out, at


def program(nc, A, out):
    with ExitStack() as ctx:
        def sb(name, shape, dt=F32):
            return ctx.enter_context(nc.sbuf_tensor(name, shape, dt))

        def sem(name):
            return ctx.enter_context(nc.semaphore(name))

        col_at, ncol = offsets(COLS)
        const_at, nconst = offsets(CONSTS)
        row_at, nrow = offsets(ROWS)

        x = sb("x", [P, T, D])
        x0 = sb("x0", [P, T, D])
        hn = sb("hn", [P, T, D])
        hT = sb("hT", [P, K2, N])
        cols = sb("cols", [P, ncol])
        consts = sb("consts", [P, nconst])
        rows = sb("rows", [1, nrow])
        b2_l0 = sb("b2_l0", [E + 1, D])
        b2_l2 = sb("b2_l2", [E, D])
        b2_l3 = sb("b2_l3", [E + 1, D])
        routers = sb("routers", [P, 4, K2, E])
        ones = sb("ones", [P, P])
        ln_st = sb("ln_st", [P, KT, 6])
        ln_mv = sb("ln_mv", [P, KT, 2])
        ln_ve = sb("ln_ve", [P, KT])
        ln_sd = sb("ln_sd", [P, KT])
        ln_rs = sb("ln_rs", [P, KT])
        w1 = [sb(f"w1_{i}", [P, K2, 1024]) for i in range(2)]
        w2 = [sb(f"w2_{i}", [P, 8, D]) for i in range(2)]
        wp = [sb(f"wp_{i}", [P, 4, K2, D]) for i in range(2)]
        SCRATCH = 29700
        scratch = sb("scratch", [P, SCRATCH])
        ps = ctx.enter_context(nc.psum_tensor("ps", [P, 8, CHUNK], F32))

        def col(name, i=0, w=1):
            a = col_at[name][0]
            return cols[:, a + i:a + i + w]

        def dcol(name, i):
            return cols[:, ds(i + col_at[name][0], 1)]

        def const(name, rows_=P):
            a, w = const_at[name]
            return consts[0:rows_, a:a + w]

        def row(name, i=0, w=None):
            a, full = row_at[name]
            return rows[0:1, a + i:a + i + (w or full)]

        def carve(*shapes):
            at, views = 0, []
            for shape in shapes:
                n = int(np.prod(shape))
                v = scratch[:, at:at + n]
                if len(shape) == 2:
                    v = v.rearrange("p (a b) -> p a b", a=shape[0])
                if len(shape) == 3:
                    v = v.rearrange("p (a b c) -> p a b c", a=shape[0], b=shape[1])
                views.append(v)
                at += n
            assert at <= SCRATCH, at
            return views

        ident = const("ident")
        one_row = ones[0:1, :]

        def bank(i, w=CHUNK, p=P):
            return ps[0:p, i, 0:w]

        stage_done = sem("stage_done")
        inputs_loaded = sem("inputs_loaded")
        stored = sem("stored")
        ones_ready = sem("ones_ready")
        ln_var, ln_std, ln_norm, ln_turned = (sem(n) for n in ("ln_var", "ln_std", "ln_norm", "ln_turned"))
        wp_loaded = [sem("wp_loaded0"), sem("wp_loaded1")]
        ffn_w = [sem("ffn_w0"), sem("ffn_w1")]
        hid_psum, silu_ready, hid_ready = sem("hid_psum"), sem("silu_ready"), sem("hid_ready")
        y_psum, y_used = sem("y_psum"), sem("y_used")
        x0_loaded = sem("x_weights_loaded")
        ctx_loaded = sem("ctx_loaded")
        latent_keys_loaded = sem("latent_keys_loaded")
        kvraw_loaded = sem("kvraw_loaded")
        lw_loaded = sem("layer_weights_loaded")
        lnorm = "ln"

        def ln_dve(dve, s, n, src, dst):
            dve.wait_ge(stage_done, s)
            for t in range(T):
                dve.bn_stats(ln_st[:, t, :], src[:, t, :])
            dve.drain()
            for t in range(T):
                dve.bn_aggr(ln_mv[:, t, :], ln_st[:, t, :])
            dve.drain()
            dve.tensor_scalar(ln_ve[:, 0:T], ln_mv[:, 0:T, 1], EPS, None, ALU.add).then_inc(ln_var, 1)
            dve.wait_ge(ln_std, n + 1)
            dve.reciprocal(ln_rs[:, 0:T], ln_sd[:, 0:T])
            dve.drain()
            for t in range(T):
                ins = dve.tensor_scalar(dst[:, t, :], src[:, t, :], ln_mv[:, t, 0:1], ln_rs[:, t:t + 1],
                                        ALU.subtract, ALU.mult)
            ins.then_inc(ln_norm, 1)

        def ln_act(act, s, n, scale=None, bias=None):
            act.wait_ge(stage_done, s)
            act.wait_ge(ln_var, n + 1)
            act.activation(ln_sd[:, 0:T], ln_ve[:, 0:T], ACT.Sqrt).then_inc(ln_std, 1)
            act.wait_ge(ln_turned, n + 1)
            for k in range(K2):
                if scale is None:
                    ins = act.activation(hT[:, k, :], bank(k), ACT.Copy)
                else:
                    ins = act.activation(hT[:, k, :], bank(k), ACT.Identity, bias=bias(k), scale=scale(k))
            act.drain().then_inc(stage_done, 1)

        def ln_pe(pe, s, n, src):
            pe.wait_ge(stage_done, s)
            pe.wait_ge(ln_norm, n + 1)
            for k in range(K2):
                for t in range(T):
                    ins = pe.transpose(ps[:, k, t * P:(t + 1) * P], src[:, t, k * P:(k + 1) * P], ident)
            ins.then_inc(ln_turned, 1)

        hid = None

        def ffn_load(sp, par, first, second, third):
            for dst, src in (first, second, third):
                sp.dma_start(dst, src).then_inc(ffn_w[par], 16)

        def ffn_pe(pe, par, loads, c, h0, nh, glu, steady, hid2, b2row=None):
            pe.wait_ge(ffn_w[par], 48 * loads)
            depth = 2 if glu else 4
            for j in range(nh):
                if steady or j >= depth:
                    pe.wait_ge(hid_ready, h0 + j - depth + 1)
                parts = ((2 * (j % 2), j), (2 * (j % 2) + 1, nh + j)) if glu else ((j % 4, j),)
                for bk, m in parts:
                    for k in range(K2):
                        ins = pe.matmul(bank(bk), w1[par][:, k, m * P:(m + 1) * P], hT[:, k, :],
                                        start=(k == 0), stop=(k == K2 - 1))
                ins.then_inc(hid_psum, 1)
            for m in range(nh):
                pe.wait_ge(hid_ready, h0 + m + 1)
                for t in range(T):
                    if m == 0 and steady:
                        pe.wait_ge(y_used, 4 * c - 4 + t + 1)
                    if m == 0 and b2row is not None:
                        pe.matmul(bank(4 + t, D), one_row, b2row, start=True, stop=False)
                    ins = pe.matmul(bank(4 + t, D), hid2[:, m, t * P:(t + 1) * P], w2[par][:, m, :],
                                    start=(m == 0 and b2row is None), stop=(m == nh - 1))
                    if m == nh - 1:
                        ins.then_inc(y_psum, 1)

        def ffn_act(act, c, h0, nh, func, bias, steady, hid2, gated=None):
            if steady:
                act.wait_ge(y_psum, 4 * c - 4)
            for j in range(nh):
                act.wait_ge(hid_psum, h0 + j + 1)
                kw = dict(bias=bias(j)) if bias else {}
                if gated is None:
                    act.activation(hid2[:, j, :], bank(j % 4), func, **kw).then_inc(hid_ready, 1)
                else:
                    act.activation(gated[:, j % 2, :], bank(2 * (j % 2)), func, **kw).then_inc(silu_ready, 1)

        def ffn_dve(dve, c, h0, g0, nh, cw, acc, hid2, gated=None, bias=None):
            if gated is not None:
                for j in range(nh):
                    dve.wait_ge(silu_ready, g0 + j + 1)
                    up = bank(2 * (j % 2) + 1)
                    if bias:
                        dve.scalar_tensor_tensor(out=hid2[:, j, :], in0=up, scalar=bias(j), in1=gated[:, j % 2, :],
                                                 op0=ALU.add, op1=ALU.mult).then_inc(hid_ready, 1)
                    else:
                        dve.tensor_tensor(hid2[:, j, :], up, gated[:, j % 2, :], ALU.mult).then_inc(hid_ready, 1)
            for t in range(T):
                dve.wait_ge(y_psum, 4 * c + t + 1)
                if cw is None:
                    dve.tensor_tensor(acc[:, t, :], bank(4 + t, D), acc[:, t, :], ALU.add).then_inc(y_used, 1)
                else:
                    dve.scalar_tensor_tensor(out=acc[:, t, :], in0=bank(4 + t, D), scalar=cw(t), in1=acc[:, t, :],
                                             op0=ALU.mult, op1=ALU.add).then_inc(y_used, 1)
            dve.drain()

        class Moe:
            def __init__(self, name, experts, nh, func, glu, router, rbias, rule, b1, b2, c0, h0, g0, loads0):
                self.name, self.experts, self.nh, self.func, self.glu = name, experts, nh, func, glu
                self.router, self.rbias, self.rule, self.b1, self.b2 = router, rbias, rule, b1, b2
                self.c0, self.h0, self.g0, self.loads0 = c0, h0, g0, loads0
                self.logits_ready, self.shifted, self.expd, self.cw_ready = (
                    sem(name + n) for n in ("_logits", "_shifted", "_exp", "_cw_ready"))
                self.cwT_psum, self.cwT_ready, self.base_psum = (
                    sem(name + n) for n in ("_cwT_psum", "_cwT_ready", "_base_psum"))
                if rule == "capacity":
                    self.choice_psum, self.kept, self.kept_sum, self.assigned, self.plan, self.plan_ready = (
                        sem(name + n) for n in ("_choice_psum", "_kept", "_kept_sum", "_assigned", "_plan",
                                                "_plan_ready"))
                (self.hidA, self.hidB, self.gated, self.lg, self.pr, self.eq, self.oh1, self.oh2, self.mx, self.m2,
                 self.sm, self.cw, self.cwT, self.t1, self.t2, self.t3, self.t4, self.t5) = carve(
                    (8, N), (8, N), (2, N), (T, E), (T, E), (T, E), (T, E), (T, E), (T,), (T,), (T,),
                    (E + 1, T), (N,), (N,), (N,), (N,), (N,), (N,))
                self.off = experts - E if rule != "capacity" else 0
                self.bodies = [(e, e % 2) for e in range(experts)]

            def counts(self, i, par):
                e = 2 * i + par
                return e, e + self.c0, self.nh * e + self.h0, self.nh * e + self.g0, i + (self.loads0[par] + 1)

            def each(self, eng, body):
                with eng.Fori(0, self.experts // 2) as i:
                    body(*self.counts(i, 0), 0)
                    body(*self.counts(i, 1), 1)
                if self.experts % 2:
                    body(*self.counts(self.experts // 2, 0), 0)

            def b1_col(self, e, j):
                width = self.nh * (2 if self.glu else 1)
                return dcol(self.b1, e * width + j) if not isinstance(e, int) else col(self.b1, e * width + j)

            def sp(self, sp, sources):
                sp.wait_ge(y_psum, 4 * self.c0)

                def body(e, c, h, g, loads, par):
                    sp.wait_ge(y_psum, 4 * c - 4)
                    ffn_load(sp, par, *sources(e, par))
                self.each(sp, body)

            def pe(self, pe, s):
                pe.wait_ge(stage_done, s)
                for t in range(T):
                    o = ps[:, 0, t * E:(t + 1) * E]
                    if self.rbias:
                        pe.matmul(o, one_row, row(self.rbias), start=True, stop=False)
                    for k in range(K2):
                        ins = pe.matmul(o, hT[:, k, t * P:(t + 1) * P], routers[:, self.router, k, :],
                                        start=(k == 0 and not self.rbias), stop=(k == K2 - 1))
                ins.then_inc(self.logits_ready, 1)
                nE = self.experts
                if self.rule == "capacity":
                    pe.wait_ge(self.cw_ready, 1)
                    for i, oh in enumerate((self.oh1, self.oh2)):
                        for t in range(T):
                            ins = pe.transpose(ps[0:E, 1 + i, t * P:(t + 1) * P], oh[:, t, :], ident)
                    ins.then_inc(self.choice_psum, 1)
                    pe.wait_ge(self.kept, 1)
                    pe.matmul(bank(3, N, E), ones[0:E, 0:E], self.t2[0:E, :], start=True, stop=True)\
                        .then_inc(self.kept_sum, 1)
                    pe.wait_ge(self.assigned, 1)
                    pe.matmul(bank(4, N, E + 1), const("split9", E), self.t2[0:E, :], start=True, stop=True)\
                        .then_inc(self.plan, 1)
                    pe.wait_ge(self.cwT_ready, 1)
                    for t in range(T):
                        ins = pe.transpose(ps[:, 5, t * 16:t * 16 + E + 1], self.cwT[0:E + 1, t * P:(t + 1) * P],
                                           ident[0:E + 1, 0:E + 1])
                    ins.then_inc(self.plan_ready, 1)
                elif self.b2 is not None:
                    pe.wait_ge(self.cw_ready, 1)
                    for t in range(T):
                        ins = pe.transpose(ps[0:nE, 1, t * P:(t + 1) * P], self.cw[:, 0:nE, t], ident)
                    ins.then_inc(self.cwT_psum, 1)
                    pe.wait_ge(self.cwT_ready, 1)
                if self.b2 is not None:
                    for t in range(T):
                        ins = pe.matmul(ps[:, 6 + t // 2, (t % 2) * D:(t % 2 + 1) * D],
                                        self.cwT[0:nE, t * P:(t + 1) * P], self.b2[:, :], start=True, stop=True)
                    ins.then_inc(self.base_psum, 1)
                    pe.wait_ge(self.shifted, 2)
                else:
                    pe.wait_ge(self.cw_ready, 1)

                def body(e, c, h, g, loads, par):
                    ffn_pe(pe, par, loads, c, h, self.nh, self.glu, True, (self.hidA, self.hidB)[par])
                self.each(pe, body)

            def act(self, act, s):
                act.wait_ge(stage_done, s)
                act.wait_ge(self.shifted, 1)
                act.activation(self.pr, self.lg, ACT.Exp).then_inc(self.expd, 1)
                if self.rule == "renormalised":
                    act.wait_ge(self.shifted, 2)
                    act.activation(self.sm, self.m2, ACT.Exp).then_inc(self.expd, 1)

                def body(e, c, h, g, loads, par):
                    bias = (lambda j: self.b1_col(e, j)) if self.b1 else None
                    ffn_act(act, c, h, self.nh, self.func, bias, True, (self.hidA, self.hidB)[par],
                            self.gated if self.glu else None)
                self.each(act, body)

            def one_hot(self, dve, pr, mx, oh):
                dve.tensor_reduce(mx, pr, AX.X, ALU.max)
                dve.drain()
                dve.tensor_tensor(self.eq, pr, mx.unsqueeze(2).to_broadcast([P, T, E]), ALU.is_equal)
                dve.drain()
                dve.tensor_tensor(self.eq, self.eq, const("first_of").unsqueeze(1).to_broadcast([P, T, E]), ALU.mult)
                dve.drain()
                dve.tensor_reduce(self.t1[:, 0:T], self.eq, AX.X, ALU.max)
                dve.drain()
                dve.tensor_tensor(oh, self.eq, self.t1[:, 0:T].unsqueeze(2).to_broadcast([P, T, E]), ALU.is_equal)
                dve.drain()

            def dve(self, dve, s):
                bc = lambda v: v.unsqueeze(2).to_broadcast([P, T, E])
                dve.wait_ge(stage_done, s)
                dve.wait_ge(self.logits_ready, 1)
                logits = ps[:, 0, 0:T * E].rearrange("p (t e) -> p t e", t=T)
                dve.tensor_reduce(self.mx, logits, AX.X, ALU.max)
                dve.drain()
                dve.tensor_tensor(self.lg, logits, bc(self.mx), ALU.subtract).then_inc(self.shifted, 1)
                dve.wait_ge(self.expd, 1)
                dve.tensor_reduce(self.mx, self.pr, AX.X, ALU.add)
                dve.drain()
                dve.reciprocal(self.sm, self.mx)
                dve.drain()
                dve.tensor_tensor(self.pr, self.pr, bc(self.sm), ALU.mult)
                dve.drain()
                self.one_hot(dve, self.pr, self.mx, self.oh1)
                cw = self.cw.rearrange("p e t -> p t e")
                routed = cw[:, :, self.off:self.off + E]
                if self.rule == "top1":
                    dve.tensor_tensor(routed, self.oh1, bc(self.mx), ALU.mult)
                else:
                    dve.scalar_tensor_tensor(out=self.lg, in0=self.oh1, scalar=-4.0, in1=self.pr,
                                             op0=ALU.mult, op1=ALU.add)
                    dve.drain()
                    self.one_hot(dve, self.lg, self.m2, self.oh2)
                if self.rule == "top2":
                    dve.tensor_tensor(self.eq, self.oh1, self.oh2, ALU.add)
                    dve.drain()
                    dve.tensor_tensor(routed, self.eq, self.pr, ALU.mult)
                    dve.memset(self.cw[:, 0, :], 1.0)
                if self.rule == "renormalised":
                    dve.tensor_tensor(self.m2, self.m2, self.mx, ALU.subtract)
                    dve.drain().then_inc(self.shifted, 1)
                    dve.wait_ge(self.expd, 2)
                    dve.tensor_scalar(self.mx, self.sm, 1.0, None, ALU.add)
                    dve.drain()
                    dve.reciprocal(self.m2, self.mx)
                    dve.drain()
                    dve.tensor_tensor(self.sm, self.sm, self.m2, ALU.mult)
                    dve.tensor_tensor(self.oh1, self.oh1, bc(self.m2), ALU.mult)
                    dve.drain()
                    dve.tensor_tensor(self.oh2, self.oh2, bc(self.sm), ALU.mult)
                    dve.drain()
                    dve.tensor_tensor(routed, self.oh1, self.oh2, ALU.add)
                dve.drain().then_inc(self.cw_ready, 1)
                nE = self.experts
                if self.rule == "capacity":
                    o1, o2, t2, t3, t4, t5 = (v[0:E, :] for v in (self.t1, self.cwT, self.t2, self.t3, self.t4, self.t5))
                    unit = ones[0:E, 0:1].to_broadcast([E, N])
                    dve.wait_ge(self.choice_psum, 1)
                    dve.tensor_copy(o1, bank(1, N, E))
                    dve.tensor_copy(o2, bank(2, N, E))
                    dve.drain()
                    dve.tensor_tensor_scan(t3, unit, o1, 0.0, ALU.mult, ALU.add)
                    dve.drain()
                    dve.scalar_tensor_tensor(out=t2, in0=t3, scalar=float(CAP), in1=o1, op0=ALU.is_le, op1=ALU.mult)\
                        .then_inc(self.kept, 1)
                    dve.tensor_scalar(self.mx[0:E, 0:1], t3[:, N - 1:N], float(CAP), None, ALU.min)
                    dve.wait_ge(self.kept_sum, 1)
                    dve.tensor_scalar(t4, bank(3, N, E), -1.0, 1.0, ALU.mult, ALU.add)
                    dve.drain()
                    dve.tensor_tensor(t4, t4, o2, ALU.mult)
                    dve.drain()
                    dve.tensor_tensor_scan(t5, unit, t4, 0.0, ALU.mult, ALU.add)
                    dve.drain()
                    dve.tensor_scalar(t5, t5, self.mx[0:E, 0:1], float(CAP), ALU.add, ALU.is_le)
                    dve.drain()
                    dve.tensor_tensor(t4, t4, t5, ALU.mult)
                    dve.drain()
                    dve.tensor_tensor(t2, t2, t4, ALU.add)
                    dve.drain().then_inc(self.assigned, 1)
                    dve.wait_ge(self.plan, 1)
                    dve.tensor_scalar(self.cwT[0:E + 1, :], bank(4, N, E + 1), const("rest9", E + 1), None, ALU.add)\
                        .then_inc(self.cwT_ready, 1)
                    dve.wait_ge(self.plan_ready, 1)
                    dve.tensor_copy(cw, ps[:, 5, 0:16 * T].rearrange("p (t e) -> p t e", t=T)[:, :, 0:E + 1])
                    dve.drain()
                elif self.b2 is not None:
                    dve.wait_ge(self.cwT_psum, 1)
                    dve.tensor_copy(self.cwT[0:nE, :], bank(1, N, nE)).then_inc(self.cwT_ready, 1)
                if self.b2 is not None:
                    dve.wait_ge(self.base_psum, 1)
                    dve.tensor_tensor(x[:, :, :].rearrange("p t d -> p (t d)"),
                                      ps[:, 6:8, :].rearrange("p a b -> p (a b)"),
                                      x[:, :, :].rearrange("p t d -> p (t d)"), ALU.add)
                    dve.drain().then_inc(self.shifted, 1)
                flat = self.cw.rearrange("p e t -> p (e t)")

                def body(e, c, h, g, loads, par):
                    weight = lambda t: (flat[:, ds(e * T + t, 1)] if not isinstance(e, int)
                                        else flat[:, e * T + t:e * T + t + 1])
                    bias = (lambda j: self.b1_col(e, self.nh + j)) if self.b1 else None
                    ffn_dve(dve, c, h, g, self.nh, weight, x, (self.hidA, self.hidB)[par],
                            self.gated if self.glu else None, bias)
                self.each(dve, body)
                dve.drain().then_inc(stage_done, 1)

        LSEM = {n: sem("local_" + n) for n in (
            "kv_rows_copied", "qk_psum", "q_ready", "k_ready", "v_psum", "v_ready", "scores_psum", "shifted", "exp",
            "p_ready", "pT_psum", "pT_ready", "o_psum", "o_ready", "oT_psum", "oT_ready", "y_psum", "y_added",
            "prepared")}

        class Local:

            def __init__(self, order, slot, loads, scale, mask, kvsrc, extra_mask=False, grouped=False, bo=None):
                self.t0 = T * order
                self.slot, self.loads, self.scale, self.mask, self.bo = slot, loads, scale, mask, bo
                self.extra_mask, self.grouped = extra_mask, grouped
                (self.copied, self.qk_psum, self.q_ready, self.k_ready, self.v_psum, self.v_ready, self.s_psum,
                 self.shifted, self.expd, self.p_ready, self.pT_psum, self.pT_ready, self.o_psum, self.o_ready,
                 self.oT_psum, self.oT_ready, self.y_ps, self.added, self.prepared) = (
                    LSEM[n] for n in
                    ("kv_rows_copied", "qk_psum", "q_ready", "k_ready", "v_psum", "v_ready", "scores_psum",
                     "shifted", "exp", "p_ready", "pT_psum", "pT_ready", "o_psum", "o_ready", "oT_psum", "oT_ready",
                     "y_psum", "y_added", "prepared"))
                (self.src64, self.kvt, self.q, self.k, self.v, self.sm, self.pT, self.o, self.oT, self.mx, self.rs,
                 self.keysT, self.maskt, self.keyrow, self.raw, self.keyraw, self.kraw) = carve(
                    (K2, N), (K2, P), (K2, P), (K2, HG, P), (D,), (H, P), (H, P), (D,), (K2, P), (H,), (H,),
                    (T, D), (T, P), (N,), (K2, P), (N,), (K2, P))
                self.kvsrc = self.src64 if kvsrc is None else kvsrc

            def pe(self, pe, s):
                W = wp[self.slot]
                pe.wait_ge(stage_done, s)
                pe.wait_ge(wp_loaded[self.slot], 64 * self.loads)
                if self.extra_mask:
                    pe.wait_ge(latent_keys_loaded, 32)
                    for k in range(K2):
                        for t in range(T):
                            pe.transpose(ps[:, k, t * P:(t + 1) * P], self.keysT[:, t, k * P:(k + 1) * P], ident)
                    pe.wait_ge(self.prepared, 1)
                    pe.matmul(bank(2), one_row, self.keyrow[0:1, :], start=True, stop=True).then_inc(self.qk_psum, 1)
                    pe.wait_ge(self.prepared, 3)
                if self.grouped:
                    pe.wait_ge(self.prepared, 4)
                with pe.Fori(0, T) as t:
                    pe.wait_ge(self.added, t + (self.t0 + 1))
                    for m in range(K2):
                        for k in range(K2):
                            pe.matmul(ps[:, 7, m * P:(m + 1) * P], W[:, 0, k, m * P:(m + 1) * P],
                                      hT[:, k, ds(t * P, P)], start=(k == 0), stop=(k == K2 - 1))
                    pe.wait_ge(self.copied, t + (self.t0 + 1))
                    for m in range(K2):
                        for k in range(K2):
                            ins = pe.matmul(ps[:, 0, D + m * P:D + (m + 1) * P], W[:, 1, k, m * P:(m + 1) * P],
                                            self.kvt[:, k, :], start=(k == 0), stop=(k == K2 - 1))
                    ins.then_inc(self.qk_psum, 1)
                    for k in range(K2):
                        ins = pe.matmul(bank(1, D), self.kvt[:, k, :], W[:, 2, k, :], start=(k == 0), stop=(k == K2 - 1))
                    ins.then_inc(self.v_psum, 1)
                    pe.wait_ge(self.q_ready, t + (self.t0 + 1))
                    pe.wait_ge(self.k_ready, t + (self.t0 + 1))
                    for g in range(K2):
                        for half in range(2):
                            ins = pe.matmul(bank(2 + 2 * g + half), self.q[:, g, :],
                                            self.k[:, g, 4 * half:4 * half + 4, :], start=True, stop=True)
                    ins.then_inc(self.s_psum, 1)
                    pe.wait_ge(self.p_ready, t + (self.t0 + 1))
                    for h in range(H):
                        ins = pe.transpose(ps[:, 2 + h // 4, (h % 4) * P:(h % 4 + 1) * P], self.sm[:, h, :], ident)
                    ins.then_inc(self.pT_psum, 1)
                    pe.wait_ge(self.pT_ready, t + (self.t0 + 1))
                    pe.wait_ge(self.v_ready, t + (self.t0 + 1))
                    for h in range(H):
                        ins = pe.matmul(ps[:, 6, h * HD:(h + 1) * HD], self.pT[:, h, :], self.v[:, h * HD:(h + 1) * HD],
                                        start=True, stop=True)
                    ins.then_inc(self.o_psum, 1)
                    pe.wait_ge(self.o_ready, t + (self.t0 + 1))
                    for k in range(K2):
                        ins = pe.transpose(ps[:, 7, k * P:(k + 1) * P], self.o[:, k * P:(k + 1) * P], ident)
                    ins.then_inc(self.oT_psum, 1)
                    pe.wait_ge(self.oT_ready, t + (self.t0 + 1))
                    if self.bo:
                        pe.matmul(bank(1, D), one_row, row(self.bo), start=True, stop=False)
                    for k in range(K2):
                        ins = pe.matmul(bank(1, D), self.oT[:, k, :], W[:, 3, k, :], start=(k == 0 and not self.bo),
                                        stop=(k == K2 - 1))
                    ins.then_inc(self.y_ps, 1)

            def act(self, act, s):
                act.wait_ge(stage_done, s)
                if self.extra_mask:
                    act.wait_ge(self.prepared, 3)
                with act.Fori(0, T) as t:
                    act.activation(self.kvt, self.kvsrc[:, :, ds(t * P, P)], ACT.Copy).then_inc(self.copied, 1)
                    act.wait_ge(self.qk_psum, t + (self.t0 + 2))
                    act.activation(self.q, ps[:, 7, 0:D].rearrange("p (m n) -> p m n", m=K2), ACT.Copy,
                                   scale=self.scale).then_inc(self.q_ready, 1)
                    act.wait_ge(self.v_psum, t + (self.t0 + 1))
                    act.activation(self.v, bank(1, D), ACT.Copy).then_inc(self.v_ready, 1)
                    act.wait_ge(self.shifted, t + (self.t0 + 1))
                    act.activation(self.sm, self.sm, ACT.Exp).then_inc(self.expd, 1)
                    act.wait_ge(self.pT_psum, t + (self.t0 + 1))
                    act.activation(self.pT.rearrange("p h n -> p (h n)"), ps[:, 2:6, :].rearrange("p a b -> p (a b)"),
                                   ACT.Copy).then_inc(self.pT_ready, 1)
                    act.wait_ge(self.oT_psum, t + (self.t0 + 1))
                    act.activation(self.oT, ps[:, 7, 0:D].rearrange("p (m n) -> p m n", m=K2), ACT.Copy)\
                        .then_inc(self.oT_ready, 1)

            def dve(self, dve, s):
                dve.wait_ge(stage_done, s)
                if self.extra_mask:
                    dve.wait_ge(latent_keys_loaded, 32)
                    dve.tensor_copy(self.keyrow[0:1, :], self.keyraw[0:1, :].bitcast(I32))
                    dve.drain()
                    dve.tensor_scalar(self.keyrow[0:1, :], self.keyrow[0:1, :], 0.0, BLOCKED, ALU.is_equal, ALU.mult)\
                        .then_inc(self.prepared, 1)
                    dve.wait_ge(self.qk_psum, 1)
                    dve.tensor_copy(self.src64, ps[:, 0:2, :]).then_inc(self.prepared, 1)
                    dve.tensor_tensor(self.maskt, ps[:, 2, :].rearrange("p (t n) -> p t n", t=T),
                                      const(self.mask).unsqueeze(1).to_broadcast([P, T, P]), ALU.add)\
                        .then_inc(self.prepared, 1)
                if self.grouped:
                    dve.wait_ge(kvraw_loaded, 32)
                    dve.wait_ge(wp_loaded[self.slot], 64 * self.loads)
                    for i, raw in enumerate((self.raw, self.kraw)):
                        for k in range(K2):
                            g = raw[:, k, 0:64].rearrange("p (g d) -> p g d", g=4).unsqueeze(2).to_broadcast([P, 4, 4, HD])
                            o = wp[self.slot][:, 1 + i, k, :].rearrange("p (g r d) -> p g r d", g=4, r=4)
                            dve.tensor_copy(o, g)
                    dve.drain().then_inc(self.prepared, 1)
                dve.drain()
                heads = lambda v: v.unsqueeze(2).to_broadcast([P, H, P])
                with dve.Fori(0, T) as t:
                    dve.wait_ge(self.qk_psum, t + (self.t0 + 2))
                    for g in range(K2):
                        ins = dve.tensor_tensor(self.k[:, g, :, :],
                                                ps[:, 0, D + g * P:D + (g + 1) * P].unsqueeze(1).to_broadcast([P, HG, P]),
                                                const("head_of").unsqueeze(2).to_broadcast([P, HG, P]), ALU.mult)
                    ins.then_inc(self.k_ready, 1)
                    dve.wait_ge(self.s_psum, t + (self.t0 + 1))
                    scores = ps[:, 2:6, :].rearrange("p a (c n) -> p (a c) n", n=P)
                    m = (self.maskt[:, ds(t, 1), :] if self.extra_mask else const(self.mask).unsqueeze(1))
                    dve.tensor_tensor(self.sm, scores, m.to_broadcast([P, H, P]), ALU.add)
                    dve.drain()
                    dve.tensor_reduce(self.mx, self.sm, AX.X, ALU.max)
                    dve.drain()
                    dve.tensor_tensor(self.sm, self.sm, heads(self.mx), ALU.subtract).then_inc(self.shifted, 1)
                    dve.wait_ge(self.expd, t + (self.t0 + 1))
                    dve.tensor_reduce(self.mx, self.sm, AX.X, ALU.add)
                    dve.drain()
                    dve.reciprocal(self.rs, self.mx)
                    dve.drain()
                    dve.tensor_tensor(self.sm, self.sm, heads(self.rs), ALU.mult).then_inc(self.p_ready, 1)
                    dve.wait_ge(self.o_psum, t + (self.t0 + 1))
                    dve.tensor_copy(self.o, bank(6, D)).then_inc(self.o_ready, 1)
                    dve.wait_ge(self.y_ps, t + (self.t0 + 1))
                    xt = x[:, ds(t, 1), :]
                    dve.tensor_tensor(xt, bank(1, D).unsqueeze(1), xt, ALU.add).then_inc(self.added, 1)
                dve.drain().then_inc(stage_done, 1)

        chunks = [(c * CHUNK, min(CHUNK, KEYS - c * CHUNK)) for c in range(4)]

        FSEM, CSEM = {}, {}

        def cross_sem(n):
            if n not in CSEM:
                CSEM[n] = sem("cross_" + n)
            return CSEM[n]

        class Flash:

            def __init__(self, name, nj, tiles):
                if name not in FSEM:
                    FSEM[name] = [sem(f"{name}_{n}") for n in ("scores_psum", "max_ready", "exp_done", "p_ready",
                                                               "pT_psum", "pT_ready", "o_psum", "o_taken",
                                                               "batch_done")]
                self.nj, self.tiles = nj, tiles
                self.keys = sum(tiles)
                self.turns = [range(c, min(c + 4, len(tiles))) for c in range(0, len(tiles), 4)]
                (self.s_psum, self.max_ready, self.exp_done, self.p_ready, self.pT_psum, self.pT_ready, self.o_psum,
                 self.o_taken, self.batch_done) = FSEM[name]

            def start(self, kt):
                return kt * P if kt < KT else KEYS

            def pe_turn(self, pe, J, p, pT):
                pe.wait_ge(self.p_ready, J + 1)
                for c, tiles in enumerate(self.turns):
                    if c >= 2:
                        pe.wait_ge(self.pT_ready, 4 * J + c - 1)
                    for i, kt in enumerate(tiles):
                        n = self.tiles[kt]
                        ins = pe.transpose(ps[0:n, 4 + c % 2, i * P:(i + 1) * P],
                                           p[:, self.start(kt):self.start(kt) + n], ident)
                    ins.then_inc(self.pT_psum, 1)

            def act_turn(self, act, J, pT):
                for c, tiles in enumerate(self.turns):
                    act.wait_ge(self.pT_psum, 4 * J + c + 1)
                    full = [kt for kt in tiles if self.tiles[kt] == P]
                    last = [kt for kt in tiles if self.tiles[kt] != P]
                    ins = None
                    if full:
                        ins = act.activation(pT[:, full[0]:full[-1] + 1, :],
                                             ps[:, 4 + c % 2, 0:len(full) * P].rearrange("p (a b) -> p a b", b=P),
                                             ACT.Copy)
                    for kt in last:
                        n = self.tiles[kt]
                        i = kt - tiles[0]
                        ins = act.activation(pT[0:n, kt, :], ps[0:n, 4 + c % 2, i * P:(i + 1) * P], ACT.Copy)
                    ins.then_inc(self.pT_ready, 1)

            def act_exp(self, act, J, p, negmax, den):
                act.wait_ge(self.max_ready, J + 1)
                act.activation(p, ps[:, 0:4, :].rearrange("p a b -> p (a b)")[:, 0:self.keys], ACT.Exp,
                               bias=negmax, accum_out=den).then_inc(self.exp_done, 1)

            def dve_softmax(self, dve, J, p, negmax, den, rden):
                dve.wait_ge(self.s_psum, J + 1)
                dve.tensor_reduce(negmax, ps[:, 0:4, :].rearrange("p a b -> p (a b)")[:, 0:self.keys], AX.X, ALU.max,
                                  negate=True).then_inc(self.max_ready, 1)
                dve.wait_ge(self.exp_done, J + 2)
                dve.reciprocal(rden, den)
                dve.drain()
                dve.tensor_scalar(p, p, rden, None, ALU.mult).then_inc(self.p_ready, 1)

        class Cross(Flash):

            def __init__(self, order, slot, loads, ctx_before, biased):
                super().__init__("cross", H // 2, [P] * FULL + [TAIL])
                self.b0, self.order = B * order, order
                self.slot, self.loads, self.ctx_before, self.biased = slot, loads, ctx_before, biased
                (self.q_psum, self.q_ready, self.qbd_ready, self.turned, self.ctxT_act, self.ctxT_dve, self.k_psum,
                 self.k_act, self.k_dve, self.v_psum, self.v_act, self.v_dve, self.oT_final, self.y_ps) = (
                    cross_sem(n) for n in ("q_psum", "q_ready", "q_blocks", "ctx_turned", "ctxT_by_act",
                                                 "ctxT_by_dve", "k_psum", "k_by_act", "k_by_dve", "v_psum",
                                                 "v_by_act", "v_by_dve", "oT_final", "y_psum"))
                (self.ctx, self.ctxT, self.kT, self.v, self.p0, self.p1, self.pT, self.q, self.oT, self.qbd,
                 self.tmp, self.st) = carve((KT, D), (K2, KEYS), (K2, KEYS), (KT, D), (KEYS,), (KEYS,), (KT, P),
                                            (K2, N), (K2, N), (K2, HG * S), (S,), (8,))
                self.p = (self.p0, self.p1)

            def sp(self, sp, s, ctx_rows):
                sp.wait_ge(stage_done, s)
                with sp.Fori(0, B) as b:
                    n = b + self.b0
                    sp.wait_ge(self.turned, 8 * n + 8)
                    sp.dma_start(self.ctx[:, 0:FULL, :],
                                 ctx_rows[b, 0:FULL * P, :].rearrange("(t p) d -> p t d", p=P)).then_inc(ctx_loaded, 16)
                    sp.dma_start(self.ctx[0:TAIL, FULL, :], ctx_rows[b, FULL * P:KEYS, :]).then_inc(ctx_loaded, 16)

            def pe(self, pe, s):
                W = wp[self.slot]
                pe.wait_ge(stage_done, s)
                pe.wait_ge(wp_loaded[self.slot], 64 * self.loads)
                for m in range(K2):
                    for k in range(K2):
                        ins = pe.matmul(bank(m), W[:, 0, k, m * P:(m + 1) * P], hT[:, k, :], start=(k == 0),
                                        stop=(k == K2 - 1))
                ins.then_inc(self.q_psum, 1)
                pe.wait_ge(self.q_ready, self.order + 1)
                with pe.Fori(0, B) as b:
                    u = b + self.b0
                    pe.wait_ge(self.batch_done, u + 1)
                    pe.wait_ge(ctx_loaded, 32 * b + (32 * self.ctx_before + 32))
                    for f in range(K2):
                        for c in range(4):
                            for i, kt in enumerate(self.turns[c]):
                                n = self.tiles[kt]
                                ins = pe.transpose(ps[:, 4 * f + c, i * P:i * P + n],
                                                   self.ctx[0:n, kt, f * P:(f + 1) * P], ident[0:n, 0:n])
                            ins.then_inc(self.turned, 1)
                    for m in range(K2):
                        for c, (a, w) in enumerate(chunks):
                            pe.wait_ge(self.ctxT_act, 4 * u + c + 1)
                            pe.wait_ge(self.ctxT_dve, 4 * u + c + 1)
                            for k in range(K2):
                                ins = pe.matmul(bank(4 * m + c, w), W[:, 1, k, m * P:(m + 1) * P],
                                                self.ctxT[:, k, a:a + w], start=(k == 0), stop=(k == K2 - 1))
                            ins.then_inc(self.k_psum, 1)
                    for i in range((KT + 1) // 2):
                        if i < 4:
                            pe.wait_ge(self.k_act, 4 * u + i + 1)
                        else:
                            pe.wait_ge(self.k_dve, 4 * u + i - 4 + 1)
                        for kt in range(2 * i, min(2 * i + 2, KT)):
                            n = self.tiles[kt]
                            for k in range(K2):
                                ins = pe.matmul(ps[0:n, i, (kt % 2) * D:(kt % 2 + 1) * D],
                                                self.ctxT[:, k, kt * P:kt * P + n], W[:, 2, k, :], start=(k == 0),
                                                stop=(k == K2 - 1))
                        ins.then_inc(self.v_psum, 1)
                    pe.wait_ge(self.qbd_ready, u + 1)
                    pe.wait_ge(self.k_dve, 4 * u + 4)
                    pe.wait_ge(self.v_act, 4 * u + 4)
                    pe.wait_ge(self.v_dve, 3 * u + 3)
                    for j in range(self.nj + 1):
                        if j < self.nj:
                            g, jj = j // 4, j % 4
                            pe.wait_ge(self.exp_done, self.nj * u + j + 1)
                            for c, (a, w) in enumerate(chunks):
                                ins = pe.matmul(bank(c, w), self.qbd[:, g, 2 * jj * S:(2 * jj + 2) * S],
                                                self.kT[:, g, a:a + w], start=True, stop=True)
                            ins.then_inc(self.s_psum, 1)
                        if j:
                            J, g, jj = self.nj * u + (j - 1), (j - 1) // 4, (j - 1) % 4
                            self.pe_turn(pe, J, self.p[(j - 1) % 2], self.pT)
                            pe.wait_ge(self.o_taken, J + 1)
                            for c, tiles in enumerate(self.turns):
                                pe.wait_ge(self.pT_ready, 4 * J + c + 1)
                                for kt in tiles:
                                    n = self.tiles[kt]
                                    f0 = g * P + 32 * jj
                                    ins = pe.matmul(ps[32 * jj:32 * jj + 32, 6, 0:P], self.v[0:n, kt, f0:f0 + 32],
                                                    self.pT[0:n, kt, :], start=(kt == 0), stop=(kt == KT - 1),
                                                    tile_position=(0, 32 * jj))
                            ins.then_inc(self.o_psum, 1)
                pe.wait_ge(self.oT_final, self.order + 1)
                for t in range(T):
                    if self.biased:
                        pe.matmul(bank(t, D), one_row, row("bo3"), start=True, stop=False)
                    for k in range(K2):
                        ins = pe.matmul(bank(t, D), self.oT[:, k, t * P:(t + 1) * P], W[:, 3, k, :],
                                        start=(k == 0 and not self.biased), stop=(k == K2 - 1))
                    ins.then_inc(self.y_ps, 1)

            def act(self, act, s):
                act.wait_ge(stage_done, s)
                with act.Fori(0, B) as b:
                    u = b + self.b0
                    for c, (a, w) in enumerate(chunks):
                        act.wait_ge(self.turned, 8 * u + 8 + c + 1)
                        act.activation(self.ctxT[:, 0, a:a + w], bank(c, w), ACT.Copy).then_inc(self.ctxT_act, 1)
                    for c, (a, w) in enumerate(chunks):
                        act.wait_ge(self.k_psum, 8 * u + c + 1)
                        if self.biased:
                            ins = act.activation(self.kT[:, 0, a:a + w], bank(c, w), ACT.Identity, bias=col("bk3", 0))
                        else:
                            ins = act.activation(self.kT[:, 0, a:a + w], bank(c, w), ACT.Copy)
                        ins.then_inc(self.k_act, 1)
                    for i in range(0, (KT + 1) // 2, 2):
                        act.wait_ge(self.v_psum, 7 * u + i + 1)
                        if 2 * i + 1 < KT:
                            act.activation(self.v[:, 2 * i:2 * i + 2, :].rearrange("p a b -> p (a b)"), bank(i), ACT.Copy)\
                                .then_inc(self.v_act, 1)
                        else:
                            act.activation(self.v[0:TAIL, 2 * i, :], bank(i, D, TAIL), ACT.Copy).then_inc(self.v_act, 1)
                    for j in range(self.nj + 1):
                        J = self.nj * u + j
                        if j:
                            self.act_turn(act, self.nj * u + (j - 1), self.pT)
                        if j < self.nj:
                            q = j % 2
                            self.act_exp(act, J, self.p[q], self.st[:, q:q + 1], self.st[:, 2 + q:3 + q])

            def dve(self, dve, s):
                dve.wait_ge(stage_done, s)
                dve.wait_ge(self.q_psum, self.order + 1)
                for m in range(K2):
                    if self.biased:
                        ins = dve.tensor_scalar(self.q[:, m, :], bank(m), col("bq3", m), HD ** -0.5, ALU.add, ALU.mult)
                    else:
                        ins = dve.tensor_scalar(self.q[:, m, :], bank(m), HD ** -0.5, None, ALU.mult)
                dve.drain().then_inc(self.q_ready, 1)
                with dve.Fori(0, B) as b:
                    u = b + self.b0
                    for g in range(K2):
                        dve.tensor_tensor(self.qbd[:, g, :].rearrange("p (h q) -> p h q", h=HG),
                                          self.q[:, g, ds(b * S, S)].unsqueeze(1).to_broadcast([P, HG, S]),
                                          const("head_of").unsqueeze(2).to_broadcast([P, HG, S]), ALU.mult)
                    dve.drain().then_inc(self.qbd_ready, 1)
                    for c, (a, w) in enumerate(chunks):
                        dve.wait_ge(self.turned, 8 * u + 8 + 4 + c + 1)
                        dve.tensor_copy(self.ctxT[:, 1, a:a + w], bank(4 + c, w)).then_inc(self.ctxT_dve, 1)
                    for c, (a, w) in enumerate(chunks):
                        dve.wait_ge(self.k_psum, 8 * u + 4 + c + 1)
                        if self.biased:
                            ins = dve.tensor_scalar(self.kT[:, 1, a:a + w], bank(4 + c, w), col("bk3", 1), None, ALU.add)
                        else:
                            ins = dve.tensor_copy(self.kT[:, 1, a:a + w], bank(4 + c, w))
                        ins.then_inc(self.k_dve, 1)
                    for i in range(1, (KT + 1) // 2, 2):
                        dve.wait_ge(self.v_psum, 7 * u + i + 1)
                        dve.tensor_copy(self.v[:, 2 * i:2 * i + 2, :].rearrange("p a b -> p (a b)"), bank(i))\
                            .then_inc(self.v_dve, 1)
                    for j in range(self.nj + 1):
                        J = self.nj * u + j
                        if j < self.nj:
                            q = j % 2
                            self.dve_softmax(dve, J, self.p[q], self.st[:, q:q + 1], self.st[:, 2 + q:3 + q],
                                             self.st[:, 4 + q:5 + q])
                        if j:
                            g, jj = (j - 1) // 4, (j - 1) % 4
                            r = slice(32 * jj, 32 * jj + 32)
                            dve.wait_ge(self.o_psum, self.nj * u + (j - 1) + 1)
                            dve.tensor_scalar(self.tmp[r, :], ps[r, 6, S:2 * S], self.odd[r, :], None, ALU.mult)
                            dve.drain()
                            dve.scalar_tensor_tensor(out=self.oT[r, g, ds(b * S, S)], in0=ps[r, 6, 0:S],
                                                     scalar=self.even[r, :], in1=self.tmp[r, :], op0=ALU.mult,
                                                     op1=ALU.add).then_inc(self.o_taken, 1)
                    dve.drain().then_inc(self.batch_done, 1)
                if self.biased:
                    for k in range(K2):
                        dve.tensor_scalar(self.oT[:, k, :], self.oT[:, k, :], col("bv3", k), None, ALU.add)
                dve.drain().then_inc(self.oT_final, 1)
                for t in range(T):
                    dve.wait_ge(self.y_ps, 4 * self.order + t + 1)
                    dve.tensor_tensor(x[:, t, :], bank(t, D), x[:, t, :], ALU.add)
                dve.drain().then_inc(stage_done, 1)

        parity = sb("parity", [P, 2])

        class First(Flash):

            def __init__(self):
                super().__init__("x0", H0 // 2, [P] * FULL + [TAIL, S])
                name = "x0"
                (self.q_psum, self.q_ready, self.qp_psum, self.qp_ready, self.var, self.std, self.norm, self.turned,
                 self.xT_act, self.xT_dve, self.lat_psum, self.lat_ready, self.kv_ready, self.oh_psum,
                 self.y_ps, self.bcast, self.bcast_ready) = (
                    sem(f"{name}_{n}") for n in ("q_psum", "q_ready", "qk_psum", "qk_ready", "var", "std", "norm",
                                                 "ctx_turned", "xT_by_act", "xT_by_dve", "latents_psum",
                                                 "latents_ready", "kv_ready", "heads_psum", "y_psum", "affine_loaded",
                                                 "affine_ready"))
                (self.ctx, self.kv, self.xT, self.p0, self.p1, self.pT, self.qT, self.oT, self.qp, self.uT, self.gb,
                 self.st) = carve((KT, D), (KT + 1, D), (K2, KEYS + S), (KEYS + S,), (KEYS + S,), (KT + 1, P),
                                  (H0, N), (H0, N), (K2, H0 * S), (K2, H0 * S), (2, D), (8,))
                self.p = (self.p0, self.p1)
                self.wq = w1[0]
                self.wv = w1[1]
                self.wkT = w2[0]
                self.wo = w2[1]

            chunks = [(c * CHUNK, min(CHUNK, KEYS + S - c * CHUNK)) for c in range(4)]

            def sp(self, sp, ctx_rows):
                sp.dma_start(self.wq[:, :, :], A["Wq0"].rearrange("(k p) n -> p k n", p=P)).then_inc(x0_loaded, 16)
                sp.dma_start(self.wkT[:, :, :], A["Wk0T"].rearrange("(h p) n -> p h n", p=P)).then_inc(x0_loaded, 16)
                sp.dma_start(self.wv[:, :, :], A["Wv0"].rearrange("(k p) n -> p k n", p=P)).then_inc(x0_loaded, 16)
                sp.dma_start(self.wo[:, :, :], A["Wo0"].rearrange("(h p) n -> p h n", p=P)).then_inc(x0_loaded, 16)
                sp.dma_start(self.gb[:, 0, :], A["g_media_row"].to_broadcast([P, D])).then_inc(self.bcast, 16)
                sp.dma_start(self.gb[:, 1, :], A["b_media_row"].to_broadcast([P, D])).then_inc(self.bcast, 16)
                with sp.Fori(0, B) as b:
                    sp.wait_ge(self.kv_ready, b + 1)
                    sp.dma_start(self.ctx[:, 0:FULL, :],
                                 ctx_rows[b, 0:FULL * P, :].rearrange("(t p) d -> p t d", p=P)).then_inc(ctx_loaded, 16)
                    sp.dma_start(self.ctx[0:TAIL, FULL, :], ctx_rows[b, FULL * P:KEYS, :]).then_inc(ctx_loaded, 16)

            def pool(self, pool):
                pool.wait_ge(self.bcast, 32)
                with pool.Fori(0, B) as b:
                    pool.wait_ge(self.batch_done, b + 1)
                    pool.wait_ge(self.norm, b + 1)
                    for n, lo, hi in ((P, 0, FULL), (TAIL, FULL, KT)):
                        bc = lambda i: self.gb[0:n, i, :].unsqueeze(1).to_broadcast([n, hi - lo, D])
                        pool.tensor_tensor(self.kv[0:n, lo:hi, :], self.ctx[0:n, lo:hi, :], bc(0), ALU.mult)
                        pool.drain()
                        if n == TAIL:
                            pool.wait_ge(self.turned, 8 * b + 16)
                        pool.tensor_tensor(self.kv[0:n, lo:hi, :], self.kv[0:n, lo:hi, :], bc(1), ALU.add)
                    pool.drain().then_inc(self.kv_ready, 1)

            def pe(self, pe, s):
                pe.wait_ge(stage_done, s)
                pe.wait_ge(x0_loaded, 64)
                for h in range(H0):
                    for k in range(K2):
                        ins = pe.matmul(bank(h), self.wq[:, k, h * P:(h + 1) * P], hT[:, k, :], start=(k == 0),
                                        stop=(k == K2 - 1))
                ins.then_inc(self.q_psum, 1)
                pe.wait_ge(self.q_ready, 1)
                with pe.Fori(0, B) as b:
                    pe.wait_ge(self.batch_done, b + 1)
                    for f in range(K2):
                        for h in range(H0):
                            ins = pe.matmul(ps[:, f, h * S:(h + 1) * S], self.wkT[:, h, f * P:(f + 1) * P],
                                            self.qT[:, h, ds(b * S, S)], start=True, stop=True)
                    ins.then_inc(self.qp_psum, 1)
                    pe.wait_ge(self.norm, b + 1)
                    pe.wait_ge(self.qp_ready, b + 1)
                    for f in range(K2):
                        for c in range(4):
                            for i, kt in enumerate(self.turns[c][0:4 if c < 3 else 1]):
                                n = self.tiles[kt]
                                ins = pe.transpose(ps[:, 4 * f + c, i * P:i * P + n],
                                                   self.ctx[0:n, kt, f * P:(f + 1) * P], ident[0:n, 0:n])
                            ins.then_inc(self.turned, 1)
                    pe.wait_ge(self.xT_dve, 5 * b + 5)
                    pe.wait_ge(self.xT_act, 4 * b + 4)
                    for f in range(K2):
                        ins = pe.matmul(ps[0:S, 7, f * P:(f + 1) * P], self.xT[:, f, KEYS:KEYS + S], ident,
                                        start=True, stop=True)
                    ins.then_inc(self.lat_psum, 1)
                    for j in range(self.nj + 1):
                        if j < self.nj:
                            pe.wait_ge(self.exp_done, self.nj * b + j + 1)
                            for c, (a, w) in enumerate(self.chunks):
                                for k in range(K2):
                                    ins = pe.matmul(bank(c, w), self.qp[:, k, 2 * j * S:(2 * j + 2) * S],
                                                    self.xT[:, k, a:a + w], start=(k == 0), stop=(k == K2 - 1))
                            ins.then_inc(self.s_psum, 1)
                        if j:
                            J = self.nj * b + (j - 1)
                            self.pe_turn(pe, J, self.p[(j - 1) % 2], self.pT)
                            pe.wait_ge(self.kv_ready, b + 2)
                            pe.wait_ge(self.lat_ready, b + 1)
                            pe.wait_ge(self.o_taken, J + 1)
                            for f in range(K2):
                                for c, tiles in enumerate(self.turns):
                                    pe.wait_ge(self.pT_ready, 4 * J + c + 1)
                                    for kt in tiles:
                                        n = self.tiles[kt]
                                        ins = pe.matmul(ps[:, 6, f * P:(f + 1) * P],
                                                        self.kv[0:n, kt, f * P:(f + 1) * P], self.pT[0:n, kt, :],
                                                        start=(kt == 0), stop=(kt == KT))
                            ins.then_inc(self.o_psum, 1)
                    pe.wait_ge(self.o_taken, self.nj * b + self.nj + 1)
                    for h in range(H0):
                        for k in range(K2):
                            ins = pe.matmul(ps[:, 7, h * S:(h + 1) * S], self.wv[:, k, h * P:(h + 1) * P],
                                            self.uT[:, k, h * S:(h + 1) * S], start=(k == 0), stop=(k == K2 - 1))
                    ins.then_inc(self.oh_psum, 1)
                pe.wait_ge(self.batch_done, B + 1)
                for t in range(T):
                    pe.matmul(bank(t, D), one_row, row("bo0"), start=True, stop=False)
                    for h in range(H0):
                        ins = pe.matmul(bank(t, D), self.oT[:, h, t * P:(t + 1) * P], self.wo[:, h, :], start=False,
                                        stop=(h == H0 - 1))
                    ins.then_inc(self.y_ps, 1)

            def act(self, act, s):
                act.wait_ge(stage_done, s)
                with act.Fori(0, B) as b:
                    act.wait_ge(self.qp_psum, b + 1)
                    act.activation(self.qp, ps[:, 0:2, :], ACT.Copy).then_inc(self.qp_ready, 1)
                    act.wait_ge(self.var, b + 1)
                    act.activation(ln_sd[:, :], ln_ve[:, :], ACT.Sqrt).then_inc(self.std, 1)
                    for c, (a, w) in enumerate(chunks):
                        act.wait_ge(self.turned, 8 * b + 8 + c + 1)
                        act.activation(self.xT[:, 0, a:a + w], bank(c, w), ACT.Identity, bias=col("b_media", 0),
                                       scale=col("g_media", 0)).then_inc(self.xT_act, 1)
                    for j in range(self.nj + 1):
                        if j:
                            self.act_turn(act, self.nj * b + (j - 1), self.pT)
                        if j < self.nj:
                            q = j % 2
                            self.act_exp(act, self.nj * b + j, self.p[q], self.st[:, q:q + 1],
                                         self.st[:, 2 + q:3 + q])

            def dve(self, dve, s):
                dve.wait_ge(stage_done, s)
                dve.wait_ge(self.q_psum, 1)
                for h in range(H0):
                    dve.tensor_scalar(self.qT[:, h, :], bank(h), col("bq0", h), DH0 ** -0.5, ALU.add, ALU.mult)
                dve.drain().then_inc(self.q_ready, 1)
                with dve.Fori(0, B) as b:
                    dve.wait_ge(ctx_loaded, 32 * b + 32)
                    for kt in range(KT):
                        n = self.tiles[kt]
                        dve.bn_stats(ln_st[0:n, kt, :], self.ctx[0:n, kt, :])
                    dve.drain()
                    for kt in range(KT):
                        n = self.tiles[kt]
                        dve.bn_aggr(ln_mv[0:n, kt, :], ln_st[0:n, kt, :])
                    dve.drain()
                    dve.tensor_scalar(ln_ve[:, :], ln_mv[:, :, 1], EPS, None, ALU.add).then_inc(self.var, 1)
                    dve.wait_ge(self.std, b + 1)
                    dve.reciprocal(ln_rs[:, :], ln_sd[:, :])
                    dve.drain()
                    for kt in range(KT):
                        n = self.tiles[kt]
                        dve.tensor_scalar(self.ctx[0:n, kt, :], self.ctx[0:n, kt, :], ln_mv[0:n, kt, 0:1],
                                          ln_rs[0:n, kt:kt + 1], ALU.subtract, ALU.mult)
                    dve.drain().then_inc(self.norm, 1)
                    dve.tensor_copy(self.xT[:, :, KEYS:KEYS + S], hT[:, :, ds(b * S, S)]).then_inc(self.xT_dve, 1)
                    for c, (a, w) in enumerate(chunks):
                        dve.wait_ge(self.turned, 8 * b + 8 + 4 + c + 1)
                        dve.tensor_scalar(self.xT[:, 1, a:a + w], bank(4 + c, w), col("g_media", 1), col("b_media", 1),
                                          ALU.mult, ALU.add).then_inc(self.xT_dve, 1)
                    dve.wait_ge(self.lat_psum, b + 1)
                    dve.tensor_copy(self.kv[0:S, KT, :], bank(7, D, S)).then_inc(self.lat_ready, 1)
                    for j in range(self.nj + 1):
                        if j < self.nj:
                            q = j % 2
                            self.dve_softmax(dve, self.nj * b + j, self.p[q], self.st[:, q:q + 1],
                                             self.st[:, 2 + q:3 + q], self.st[:, 4 + q:5 + q])
                        if j:
                            dve.wait_ge(self.o_psum, self.nj * b + (j - 1) + 1)
                            dve.tensor_copy(self.uT[:, :, (j - 1) * P:j * P],
                                            ps[:, 6, 0:D].rearrange("p (f n) -> p f n", f=K2)).then_inc(self.o_taken, 1)
                    dve.wait_ge(self.oh_psum, b + 1)
                    dve.tensor_tensor(self.oT[:, :, ds(b * S, S)], ps[:, 7, :].rearrange("p (h q) -> p h q", h=H0),
                                      col("bv0", 0, H0).unsqueeze(2).to_broadcast([P, H0, S]), ALU.add)
                    dve.drain().then_inc(self.batch_done, 1)
                for t in range(T):
                    dve.wait_ge(self.y_ps, t + 1)
                    dve.tensor_tensor(x[:, t, :], bank(t, D), x[:, t, :], ALU.add)
                dve.drain().then_inc(stage_done, 1)

        class Quat:

            def __init__(self):
                (self.pw_psum, self.pw_ready, self.qkv_psum, self.qkv_ready, self.diff_psum, self.diff_ready,
                 self.rolled, self.reduced, self.cos_ready, self.p3_ready, self.c_ready, self.cT_psum, self.cT_ready,
                 self.z_psum, self.z_ready, self.y_ps) = (
                    sem(f"quat_{n}") for n in ("pw_psum", "pw_ready", "qkv_psum", "qkv_ready", "diff_psum",
                                               "diff_ready", "rolled", "reduced", "cos_ready", "p3_ready",
                                               "c_ready", "cT_psum", "cT_ready", "z_psum", "z_ready", "y_psum"))
                TD = T * D
                (self.aw, self.pw, self.ab, self.pw2, self.q, self.k, self.v, self.red, self.pr, self.tmp,
                 self.ptmp) = carve((K2, 3 * D), (K2, D), (3 * D,), (K2, D), (4, TD), (4, TD), (4, TD), (3, TD),
                                    (4, TD), (TD,), (TD,))
                self.parts = (self.q, self.k, self.v)
                self.hid = self.red
                self.cT = self.q[:, 0, :].rearrange("p (k n) -> p k n", k=K2)
                self.zT = self.q[:, 1, :].rearrange("p (k n) -> p k n", k=K2)
                self.hidden = scratch[:, 3072:3072 + 8 * N].rearrange("p (a b) -> p a b", a=8)

            def sp(self, sp, s0):
                sp.wait_ge(stage_done, s0)
                with sp.Fori(0, LAYERS) as l:
                    sp.wait_ge(stage_done, 4 * l + (s0 - 2))
                    sp.dma_start(self.aw, A["attn_w"][l, :, :].rearrange("(k p) n -> p k n", p=P)).then_inc(lw_loaded, 16)
                    sp.dma_start(self.pw, A["aproj_w"][l, :, :].rearrange("(k p) n -> p k n", p=P)).then_inc(lw_loaded, 16)
                    sp.dma_start(self.ab, A["attn_b"][ds(l, 1), :].to_broadcast([P, 3 * D])).then_inc(lw_loaded, 16)
                    sp.wait_ge(y_psum, 4 * l + 4)
                    fc = A["fc_w"][l, :, :].rearrange("(k p) n -> p k n", p=P)
                    ffn_load(sp, 0, (w1[0][:, 0, :], fc[:, 0, :]), (w1[0][:, 1, :], fc[:, 1, :]),
                             (w2[0][:, :, :], A["mproj_w"][l, :, :].rearrange("(k p) n -> p k n", p=P)))

            def pe(self, pe, s, l):
                pe.wait_ge(stage_done, s)
                pe.wait_ge(lw_loaded, 48 * l + 48)
                basis = const("basis").rearrange("p (k n) -> p k n", k=K2)
                for m in range(K2):
                    for k in range(K2):
                        ins = pe.matmul(ps[:, 6, m * D:(m + 1) * D], basis[:, k, m * P:(m + 1) * P], self.pw[:, k, :],
                                        start=(k == 0), stop=(k == K2 - 1))
                ins.then_inc(self.pw_psum, 1)
                for t in range(T):
                    b0 = 2 * (t % 2)
                    if t >= 2:
                        pe.wait_ge(self.qkv_ready, 4 * l + t - 1)
                    for bk, a, w in ((b0, 0, CHUNK), (b0 + 1, CHUNK, 3 * D - CHUNK)):
                        for k in range(K2):
                            ins = pe.matmul(bank(bk, w), hT[:, k, t * P:(t + 1) * P], self.aw[:, k, a:a + w],
                                            start=(k == 0), stop=(k == K2 - 1))
                    ins.then_inc(self.qkv_psum, 1)
                pe.wait_ge(self.qkv_ready, 4 * l + 4)
                for i, part in enumerate(self.parts):
                    for t in range(T):
                        at = i * T + t
                        ins = pe.matmul(ps[:, at // 2, (at % 2) * D:(at % 2 + 1) * D], const("diff"),
                                        part[:, 0, t * D:(t + 1) * D], start=True, stop=True)
                    ins.then_inc(self.diff_psum, 1)
                pe.wait_ge(self.c_ready, l + 1)
                for k in range(K2):
                    for t in range(T):
                        ins = pe.transpose(ps[:, k, t * P:(t + 1) * P], self.pr[:, 0, t * D + k * P:t * D + (k + 1) * P],
                                           ident)
                ins.then_inc(self.cT_psum, 1)
                pe.wait_ge(self.cT_ready, l + 1)
                for m in range(K2):
                    for k in range(K2):
                        ins = pe.matmul(bank(2 + m), basis[:, k, m * P:(m + 1) * P], self.cT[:, k, :], start=(k == 0),
                                        stop=(k == K2 - 1))
                ins.then_inc(self.z_psum, 1)
                pe.wait_ge(self.z_ready, l + 1)
                pe.wait_ge(self.pw_ready, l + 1)
                pbias = rows[0:1, ds(l * D + row_at["aproj_b"][0], D)]
                for t in range(T):
                    pe.matmul(bank(4 + t, D), one_row, pbias, start=True, stop=False)
                    for k in range(K2):
                        ins = pe.matmul(bank(4 + t, D), self.zT[:, k, t * P:(t + 1) * P], self.pw2[:, k, :],
                                        start=False, stop=(k == K2 - 1))
                    ins.then_inc(self.y_ps, 1)

            def act(self, act, s, l):
                act.wait_ge(stage_done, s)
                act.wait_ge(self.pw_psum, l + 1)
                act.activation(self.pw2.rearrange("p k n -> p (k n)"), bank(6), ACT.Copy).then_inc(self.pw_ready, 1)
                act.wait_ge(self.qkv_ready, 4 * l + 4)
                for part in self.parts:
                    dst = part[:, 2, :].rearrange("p (t d) -> p t d", t=T)
                    src = part[:, 0, :].rearrange("p (t d) -> p t d", t=T)
                    act.activation(dst[:, :, HD:D], src[:, :, 0:D - HD], ACT.Copy)
                    act.activation(dst[:, :, 0:HD], src[:, :, D - HD:D], ACT.Copy)
                act.drain().then_inc(self.rolled, 1)
                for i, part in enumerate(self.parts):
                    act.wait_ge(self.diff_psum, 3 * l + i + 1)
                    act.activation(part[:, 1, :], ps[:, 2 * i:2 * i + 2, :].rearrange("p a b -> p (a b)"), ACT.Copy)\
                        .then_inc(self.diff_ready, 1)
                act.wait_ge(self.reduced, l + 1)
                act.activation(self.red, self.red, ACT.Abs)
                act.drain()
                for i, part in enumerate(self.parts):
                    act.activation(part[:, 3, :], self.red[:, i, :], ACT.Sin, bias=half_pi[:, :], scale=-1.0)\
                        .then_inc(self.cos_ready, 1)
                act.wait_ge(self.cT_psum, l + 1)
                act.activation(self.cT, ps[:, 0:2, :], ACT.Copy).then_inc(self.cT_ready, 1)

            def pool(self, pool, l):
                pool.wait_ge(self.rolled, l + 1)
                pool.wait_ge(self.diff_ready, 3 * l + 2)
                pool.wait_ge(self.cos_ready, 3 * l + 2)
                self.combine(pool, 3, self.ptmp)
                pool.drain().then_inc(self.p3_ready, 1)

            TERMS = {0: ((0, 0, 1), (1, 1, -1), (2, 2, -1), (3, 3, -1)),
                     1: ((0, 1, 1), (1, 0, 1), (2, 3, 1), (3, 2, -1)),
                     2: ((0, 2, 1), (1, 3, -1), (2, 0, 1), (3, 1, 1)),
                     3: ((0, 3, 1), (1, 2, 1), (2, 1, -1), (3, 0, 1))}

            def combine(self, eng, c, tmp):
                for n, (i, j, sign) in enumerate(self.TERMS[c]):
                    dst = self.pr[:, c, :] if n == 0 else tmp
                    eng.tensor_tensor(dst, self.q[:, i, :], self.k[:, j, :], ALU.mult)
                    eng.drain()
                    if n:
                        eng.tensor_tensor(self.pr[:, c, :], self.pr[:, c, :], tmp, ALU.add if sign > 0 else ALU.subtract)
                        eng.drain()

            def dve(self, dve, s, l):
                dve.wait_ge(stage_done, s)
                dve.wait_ge(lw_loaded, 48 * l + 48)
                qkv = scratch[:, self.q_at:self.q_at + 12 * T * D].rearrange("p (c j n) -> p c j n", c=3, j=4)
                bias = self.ab.rearrange("p (h c d) -> p c h d", c=3, d=HD)
                for t in range(T):
                    b0 = 2 * (t % 2)
                    dve.wait_ge(self.qkv_psum, 4 * l + t + 1)
                    src = ps[:, b0:b0 + 2, :].rearrange("p a b -> p (a b)")[:, 0:3 * D]\
                        .rearrange("p (h c d) -> p c h d", c=3, d=HD)
                    for c in range(3):
                        ins = dve.tensor_tensor(qkv[:, c, 0, t * D:(t + 1) * D].rearrange("p (h d) -> p h d", h=H),
                                                src[:, c, :, :], bias[:, c, :, :], ALU.add)
                    ins.then_inc(self.qkv_ready, 1)
                dve.drain()
                vals = qkv[:, :, 0, :]
                dve.tensor_scalar(self.red, vals, 1.0 / TWO_PI, ROUND, ALU.mult, ALU.add)
                dve.drain()
                dve.tensor_scalar(self.red, self.red, ROUND, -TWO_PI, ALU.subtract, ALU.mult)
                dve.drain()
                dve.tensor_tensor(self.red, self.red, vals, ALU.add).then_inc(self.reduced, 1)
                dve.wait_ge(self.diff_ready, 3 * l + 3)
                dve.wait_ge(self.rolled, l + 1)
                dve.wait_ge(self.cos_ready, 3 * l + 3)
                for c in range(3):
                    self.combine(dve, c, self.tmp)
                c0 = self.pr[:, 0, :]
                dve.tensor_tensor(c0, c0, self.v[:, 0, :], ALU.mult)
                for c in (1, 2, 3):
                    dve.drain()
                    if c == 3:
                        dve.wait_ge(self.p3_ready, l + 1)
                    dve.tensor_tensor(self.tmp, self.pr[:, c, :], self.v[:, c, :], ALU.mult)
                    dve.drain()
                    dve.tensor_tensor(c0, c0, self.tmp, ALU.subtract)
                dve.drain().then_inc(self.c_ready, 1)
                dve.wait_ge(self.z_psum, l + 1)
                spectrum = const("spectrum").rearrange("p (k s) -> p k s", k=K2)
                for m in range(K2):
                    dve.tensor_tensor(self.zT[:, m, :].rearrange("p (b s) -> p b s", b=B),
                                      ps[:, 2 + m, :].rearrange("p (b s) -> p b s", b=B),
                                      spectrum[:, m, :].unsqueeze(1).to_broadcast([P, B, S]), ALU.mult)
                dve.drain().then_inc(self.z_ready, 1)
                for t in range(T):
                    dve.wait_ge(self.y_ps, 4 * l + t + 1)
                    dve.tensor_tensor(x0[:, t, :], bank(4 + t, D), x0[:, t, :], ALU.add)
                dve.drain().then_inc(stage_done, 1)

        half_pi = sb("half_pi", [P, 1])

        class Scan:
            NS = 64

            def __init__(self):
                (self.loaded, self.a_ready, self.z_psum, self.z_ready, self.e_ready, self.l_ready, self.d_ready,
                 self.decay_ready, self.hs_ready, self.y_ps, self.hid_next, self.out_psum, self.asp) = (
                    sem(f"scan_{n}") for n in ("loaded", "a_softplus", "z_psum", "z_ready", "exp", "log", "delta_ready",
                                               "decay_ready", "states_ready", "y_psum", "hidden_ready", "out_psum",
                                               "a_steps"))
                (self.win, self.wout, self.small, self.z, self.az, self.delta, self.decay, self.drive, self.hs,
                 self.cs, self.hid, self.sa) = carve((4 * K2, self.NS), (4, D), (6,), (N,), (N,), (N,), (N,), (N,),
                                                     (N,), (K2, B), (K2, N), (8,))

            def sp(self, sp, s):
                sp.wait_ge(stage_done, s)
                for l in range(2):
                    for i, name in enumerate(("Wd", "Wi")):
                        a = (2 * l + i) * K2
                        sp.dma_start(self.win[:, a:a + K2, :], A[name][l, :, :].rearrange("(k p) n -> p k n", p=P))\
                            .then_inc(self.loaded, 16)
                    for i, name in enumerate(("Wos", "Wss")):
                        sp.dma_start(self.wout[0:self.NS, 2 * l + i, :], A[name][l, :, :]).then_inc(self.loaded, 16)
                sp.dma_start(self.small[0:self.NS, :], A["scan_small"]).then_inc(self.loaded, 16)

            def pe(self, pe, s):
                ns = self.NS
                pe.wait_ge(stage_done, s)
                pe.wait_ge(self.loaded, 16 * 9)
                for l in range(2):
                    src = hT if l == 0 else self.hid
                    if l:
                        pe.wait_ge(self.hid_next, 1)
                    for i in range(2):
                        for k in range(K2):
                            ins = pe.matmul(bank(i, N, ns), self.win[:, (2 * l + i) * K2 + k, :], src[:, k, :],
                                            start=(k == 0), stop=(k == K2 - 1))
                    ins.then_inc(self.z_psum, 1)
                    pe.wait_ge(self.hs_ready, l + 1)
                    last = self.hs[0:ns, :].rearrange("p (b s) -> p b s", b=B)[:, :, S - 1]
                    for m in range(K2):
                        pe.matmul(bank(2 + m), self.wout[0:ns, 2 * l, m * P:(m + 1) * P], self.hs[0:ns, :],
                                  start=True, stop=True)
                        ins = pe.matmul(bank(4 + m, B), self.wout[0:ns, 2 * l + 1, m * P:(m + 1) * P], last,
                                        start=True, stop=True)
                    ins.then_inc(self.y_ps, 1)
                pe.wait_ge(self.hid_next, 2)
                for t in range(T):
                    for k in range(K2):
                        ins = pe.transpose(ps[:, t // 2, (t % 2) * D + k * P:(t % 2) * D + (k + 1) * P],
                                           self.hid[:, k, t * P:(t + 1) * P], ident)
                ins.then_inc(self.out_psum, 1)

            def act(self, act, s):
                ns = self.NS
                act.wait_ge(stage_done, s)
                act.wait_ge(self.loaded, 16 * 9)
                al = self.small[0:ns, 4:6]
                ab, ex, lg = (self.sa[0:ns, i:i + 2] for i in (0, 2, 4))
                act.activation(ab, al, ACT.Abs)
                act.drain()
                act.activation(ex, ab, ACT.Exp, scale=-1.0)
                act.drain()
                act.activation(lg, ex, ACT.Ln, bias=ones[0:ns, 0:1]).then_inc(self.asp, 1)
                for l in range(2):
                    act.wait_ge(self.z_psum, l + 1)
                    act.activation(self.z[0:ns, :], bank(0, N, ns), ACT.Identity, bias=self.small[0:ns, l:l + 1])\
                        .then_inc(self.z_ready, 1)
                    act.drain()
                    act.activation(self.az[0:ns, :], self.z[0:ns, :], ACT.Abs)
                    act.drain()
                    act.activation(self.az[0:ns, :], self.az[0:ns, :], ACT.Exp, scale=-1.0)
                    act.drain()
                    act.activation(self.az[0:ns, :], self.az[0:ns, :], ACT.Ln, bias=ones[0:ns, 0:1])\
                        .then_inc(self.l_ready, 1)
                    act.wait_ge(self.d_ready, l + 1)
                    act.activation(self.decay[0:ns, :], self.delta[0:ns, :], ACT.Exp, scale=self.sa[0:ns, 6 + l:7 + l])\
                        .then_inc(self.decay_ready, 1)

            def dve(self, dve, s):
                ns = self.NS
                dve.wait_ge(stage_done, s)
                dve.wait_ge(self.asp, 1)
                sp_a = self.sa[0:ns, 6:8]
                dve.scalar_tensor_tensor(out=sp_a, in0=self.small[0:ns, 4:6], scalar=0.0, in1=self.sa[0:ns, 4:6],
                                         op0=ALU.max, op1=ALU.add)
                dve.drain()
                dve.tensor_scalar(sp_a, sp_a, -1.0, None, ALU.mult)
                for l in range(2):
                    dve.drain()
                    dve.wait_ge(self.l_ready, l + 1)
                    dve.scalar_tensor_tensor(out=self.delta[0:ns, :], in0=self.z[0:ns, :], scalar=0.0,
                                             in1=self.az[0:ns, :], op0=ALU.max, op1=ALU.add)
                    dve.drain().then_inc(self.d_ready, 1)
                    dve.scalar_tensor_tensor(out=self.drive[0:ns, :], in0=bank(1, N, ns),
                                             scalar=self.small[0:ns, 2 + l:3 + l], in1=self.delta[0:ns, :],
                                             op0=ALU.add, op1=ALU.mult)
                    dve.wait_ge(self.decay_ready, l + 1)
                    dve.memset(self.decay[0:ns, :].rearrange("p (b s) -> p b s", b=B)[:, :, 0], 0.0)
                    dve.drain()
                    dve.tensor_tensor_scan(self.hs[0:ns, :], self.decay[0:ns, :], self.drive[0:ns, :], 0.0,
                                           ALU.mult, ALU.add).then_inc(self.hs_ready, 1)
                    dve.wait_ge(self.y_ps, l + 1)
                    for m in range(K2):
                        dve.tensor_scalar(self.cs[:, m, :], bank(4 + m, B), col("bs_scan", 2 * l + m),
                                          col("bo_scan", 2 * l + m), ALU.add, ALU.add)
                    dve.drain()
                    for m in range(K2):
                        dve.tensor_tensor(self.hid[:, m, :].rearrange("p (b s) -> p b s", b=B),
                                          ps[:, 2 + m, :].rearrange("p (b s) -> p b s", b=B),
                                          self.cs[:, m, :].unsqueeze(2).to_broadcast([P, B, S]), ALU.add)
                    dve.drain().then_inc(self.hid_next, 1)
                dve.wait_ge(self.out_psum, 1)
                dve.tensor_tensor(x[:, :, :].rearrange("p t d -> p (t d)"), ps[:, 0:2, :].rearrange("p a b -> p (a b)"),
                                  x[:, :, :].rearrange("p t d -> p (t d)"), ALU.add)
                dve.drain().then_inc(stage_done, 1)

        first = First()
        quat = Quat()
        quat.q_at = 2 * K2 * 0 + (K2 * 3 * D + K2 * D + 3 * D + K2 * D)
        moe0 = Moe("moe0", 9, 2, ACT.Silu, True, 0, "gate_b", "top2", "sw_b1", b2_l0, 5, 32, 0, (4, 0))
        moe1 = Moe("moe1", 8, 4, ACT.Silu, True, 1, None, "renormalised", None, None, 14, 50, 18, (9, 4))
        moe2 = Moe("moe2", 8, 8, ACT.Gelu_apprx_tanh, False, 2, "switch_b", "top1", "l2_b1", b2_l2, 22, 82, 50,
                   (13, 8))
        moe3 = Moe("moe3", 9, 8, ACT.Gelu, False, 3, "router_b", "capacity", "l3_b1", b2_l3, 30, 146, 50, (17, 12))
        cross1 = Local(0, 0, 1, HD ** -0.5, "causal", None, extra_mask=True)
        self1 = Local(1, 1, 1, HD ** -0.5, "same_batch", hT, grouped=True)
        cross2 = Cross(0, 0, 2, B, False)
        self2 = Local(2, 1, 2, D ** -0.5, "same_batch", hT, bo="bff2")
        cross3 = Cross(1, 0, 3, 2 * B, True)
        scan = Scan()
        for c in (cross2, cross3):
            c.even, c.odd = parity[:, 0:1], parity[:, 1:2]

        (LN_A, LN_B, FIRST, LN_C, QUAT) = range(5)
        QUAT_END = QUAT + 4 * LAYERS
        (LN_D, MOE0, LN_E, CROSS1, LN_F, SELF1, LN_G, MOE1, LN_H, CROSS2, LN_I, SELF2, LN_J, MOE2, LN_K, CROSS3,
         LN_L, SCAN, LN_M, MOE3, END) = range(QUAT_END + 1, QUAT_END + 22)
        NL = 3 + 2 * LAYERS

        LAST = A["last"]
        block = ctx.enter_context(nc.Block())

        @block.sync
        def _(sp):
            sp.dma_start(x[:, :, :], A["x"].rearrange("(t p) d -> p t d", p=P)).then_inc(inputs_loaded, 16)
            sp.dma_start(cols[:, :], A["cols"]).then_inc(inputs_loaded, 16)
            sp.dma_start(consts[:, :], A["consts"]).then_inc(inputs_loaded, 16)
            sp.dma_start(rows[:, :], A["rows"]).then_inc(inputs_loaded, 16)
            sp.dma_start(b2_l0[:, :], A["b2_l0"]).then_inc(inputs_loaded, 16)
            sp.dma_start(b2_l2[:, :], A["b2_l2"]).then_inc(inputs_loaded, 16)
            sp.dma_start(b2_l3[:, :], A["b2_l3"]).then_inc(inputs_loaded, 16)
            sp.dma_start(routers[:, :, :, :], A["routers"].rearrange("r (k p) e -> p r k e", p=P))\
                .then_inc(inputs_loaded, 16)

            def attention_weights(slot, names):
                for i, name in enumerate(names):
                    dst = wp[slot][:, i, :, :]
                    sp.dma_start(dst, A[name].rearrange("(k p) n -> p k n", p=P)).then_inc(wp_loaded[slot], 16)

            if LAST >= 1:
                first.sp(sp, A["ctx"])
            if LAST >= 4:
                attention_weights(0, ("Wq1", "Wk1", "Wv1", "Wo1"))
            if LAST >= 5:
                attention_weights(1, ("Wqa", "Wqa", "Wqa", "Woa"))
            if LAST >= 2:
                quat.sp(sp, QUAT)

            def shared_then_routed(e, par):
                w = A["w1_l0"][e, :, :].rearrange("(k p) n -> p k n", p=P)
                return ((w1[par][:, 0, 0:512], w[:, 0, :]), (w1[par][:, 1, 0:512], w[:, 1, :]),
                        (w2[par][:, 0:2, :], A["w2_l0"][e, :, :].rearrange("(k p) n -> p k n", p=P)))

            def gate_up_down(e, par):
                return ((w1[par][:, :, 0:512], A["gate_l1"][e, :, :].rearrange("(k p) n -> p k n", p=P)),
                        (w1[par][:, :, 512:1024], A["up_l1"][e, :, :].rearrange("(k p) n -> p k n", p=P)),
                        (w2[par][:, 0:4, :], A["down_l1"][e, :, :].rearrange("(k p) n -> p k n", p=P)))

            def wide(a, b):
                def sources(e, par):
                    w = A[a][e, :, :].rearrange("(k p) n -> p k n", p=P)
                    return ((w1[par][:, 0, :], w[:, 0, :]), (w1[par][:, 1, :], w[:, 1, :]),
                            (w2[par][:, :, :], A[b][e, :, :].rearrange("(k p) n -> p k n", p=P)))
                return sources

            if LAST >= 3:
                moe0.sp(sp, shared_then_routed)
            if LAST >= 4:
                sp.wait_ge(stage_done, CROSS1)
                sp.dma_start(cross1.keysT, A["ctx64"].rearrange("(t p) d -> p t d", p=P)).then_inc(latent_keys_loaded, 16)
                sp.dma_start(cross1.keyraw[0:1, :].bitcast(I32), A["mask64"]).then_inc(latent_keys_loaded, 16)
            if LAST >= 5:
                sp.wait_ge(stage_done, SELF1)
                sp.dma_start(self1.raw[:, :, 0:64], A["Wka"].rearrange("(k p) n -> p k n", p=P)).then_inc(kvraw_loaded, 16)
                sp.dma_start(self1.kraw[:, :, 0:64], A["Wva"].rearrange("(k p) n -> p k n", p=P)).then_inc(kvraw_loaded, 16)
            if LAST >= 7:
                attention_weights(0, ("Wq2", "Wq2", "Wq2", "Wo2"))
            if LAST >= 6:
                sp.wait_ge(stage_done, LN_G)
                if LAST >= 8:
                    attention_weights(1, ("Wqb", "Wkb", "Wvb", "Wff"))
                moe1.sp(sp, gate_up_down)
            if LAST >= 7:
                cross2.sp(sp, CROSS2, A["ctx"])
            if LAST >= 9:
                moe2.sp(sp, wide("w1_l2", "w2_l2"))
            if LAST >= 10:
                attention_weights(0, ("Wq3", "Wk3", "Wv3", "Wo3"))
                cross3.sp(sp, CROSS3, A["ctx"])
            if LAST >= 11:
                scan.sp(sp, SCAN)
            if LAST >= 12:
                moe3.sp(sp, wide("w1_l3", "w2_l3"))
            final = {0: LN_A, 1: LN_C, 2: LN_D, 3: LN_E, 4: LN_F, 5: LN_G, 6: LN_H, 7: LN_I, 8: LN_J, 9: LN_K,
                     10: LN_L, 11: LN_M, 12: END}[LAST]
            sp.wait_ge(stage_done, final)
            sp.dma_start(out.rearrange("(t p) d -> p t d", p=P), x[:, :, :]).then_inc(stored, 16)
            sp.wait_ge(stored, 16)

        @block.gpsimd
        def _(pool):
            pool.drain().then_inc(first.kv_ready, 1)
            pool.memset(ones[:, :], 1.0)
            pool.memset(half_pi[:, :], float(np.pi / 2))
            pool.memset(ln_mv[:, :, :], 0.0)
            pool.drain().then_inc(ones_ready, 1)
            if LAST >= 1:
                first.pool(pool)
            if LAST >= 2:
                with pool.Fori(0, LAYERS) as l:
                    quat.pool(pool, l)

        @block.tensor
        def _(pe):
            pe.drain().then_inc(first.turned, 8)
            pe.drain().then_inc(cross2.turned, 8)
            pe.drain().then_inc(y_psum, 4)
            pe.wait_ge(inputs_loaded, 128)
            pe.wait_ge(ones_ready, 1)
            ln = lambda s, n: ln_pe(pe, s, n, hn)
            if LAST >= 1:
                ln(LN_A, 0)
                ln(LN_B, 1)
                first.pe(pe, FIRST)
            if LAST >= 2:
                ln(LN_C, 2)
                with pe.Fori(0, LAYERS) as l:
                    s = 4 * l + (QUAT + 1)
                    ln(s - 1 + 0 + 0, 2 * l + 3)
                    quat.pe(pe, 4 * l + (QUAT + 1), l)
                    ln(4 * l + (QUAT + 2), 2 * l + 4)
                    pe.wait_ge(stage_done, 4 * l + (QUAT + 3))
                    ffn_pe(pe, 0, l + 1, l + 1, 8 * l, 8, False, False, quat.hidden,
                           rows[0:1, ds(l * D + row_at["mproj_b"][0], D)])
            tail = ((3, LN_D, MOE0, moe0), (4, LN_E, CROSS1, cross1), (5, LN_F, SELF1, self1), (6, LN_G, MOE1, moe1),
                    (7, LN_H, CROSS2, cross2), (8, LN_I, SELF2, self2), (9, LN_J, MOE2, moe2),
                    (10, LN_K, CROSS3, cross3), (11, LN_L, SCAN, scan), (12, LN_M, MOE3, moe3))
            for i, (at, norm_at, stage_at, stage) in enumerate(tail):
                if LAST >= at:
                    ln(norm_at, NL + i)
                    stage.pe(pe, stage_at)

        @block.scalar
        def _(act):
            act.drain().then_inc(first.exp_done, 1)
            act.drain().then_inc(cross2.exp_done, 1)
            act.wait_ge(inputs_loaded, 128)
            act.wait_ge(ones_ready, 1)
            if LAST >= 1:
                ln_act(act, LN_A, 0)
                ln_act(act, LN_B, 1, lambda k: col("g_lat", k), lambda k: col("b_lat", k))
                first.act(act, FIRST)
            if LAST >= 2:
                ln_act(act, LN_C, 2)
                with act.Fori(0, LAYERS) as l:
                    ln_act(act, 4 * l + QUAT, 2 * l + 3, lambda k: dcol("ln1_w", l * 2 + k),
                           lambda k: dcol("ln1_b", l * 2 + k))
                    quat.act(act, 4 * l + (QUAT + 1), l)
                    ln_act(act, 4 * l + (QUAT + 2), 2 * l + 4, lambda k: dcol("ln2_w", l * 2 + k),
                           lambda k: dcol("ln2_b", l * 2 + k))
                    act.wait_ge(stage_done, 4 * l + (QUAT + 3))
                    ffn_act(act, l + 1, 8 * l, 8, ACT.Gelu, lambda j: dcol("fc_b", l * 8 + j), False, quat.hidden)
            tail = ((3, LN_D, MOE0, moe0), (4, LN_E, CROSS1, cross1), (5, LN_F, SELF1, self1), (6, LN_G, MOE1, moe1),
                    (7, LN_H, CROSS2, cross2), (8, LN_I, SELF2, self2), (9, LN_J, MOE2, moe2),
                    (10, LN_K, CROSS3, cross3), (11, LN_L, SCAN, scan), (12, LN_M, MOE3, moe3))
            for i, (at, norm_at, stage_at, stage) in enumerate(tail):
                if LAST >= at:
                    ln_act(act, norm_at, NL + i)
                    stage.act(act, stage_at)

        @block.vector
        def _(dve):
            for primed in (first.o_taken, first.batch_done, cross2.o_taken, cross2.batch_done, cross1.added):
                dve.drain().then_inc(primed, 1)
            dve.drain().then_inc(y_used, 4)
            dve.wait_ge(inputs_loaded, 128)
            dve.wait_ge(ones_ready, 1)
            head = const("head_of").rearrange("p (j r) -> p r j", r=2)
            dve.tensor_reduce(parity[:, :], head, AX.X, ALU.add)
            if LAST >= 1:
                ln_dve(dve, LN_A, 0, x, hn)
                ln_dve(dve, LN_B, 1, hn, hn)
                first.dve(dve, FIRST)
            if LAST >= 2:
                ln_dve(dve, LN_C, 2, x, hn)
                dve.wait_ge(stage_done, QUAT)
                dve.tensor_copy(x0[:, :, :], hn[:, :, :])
                dve.drain()
                with dve.Fori(0, LAYERS) as l:
                    ln_dve(dve, 4 * l + QUAT, 2 * l + 3, x0, hn)
                    quat.dve(dve, 4 * l + (QUAT + 1), l)
                    ln_dve(dve, 4 * l + (QUAT + 2), 2 * l + 4, x0, hn)
                    dve.wait_ge(stage_done, 4 * l + (QUAT + 3))
                    ffn_dve(dve, l + 1, 8 * l, 0, 8, None, x0, quat.hidden)
                    dve.drain().then_inc(stage_done, 1)
                dve.tensor_tensor(x[:, :, :], x[:, :, :], x0[:, :, :], ALU.add)
                dve.drain().then_inc(stage_done, 1)
            tail = ((3, LN_D, MOE0, moe0), (4, LN_E, CROSS1, cross1), (5, LN_F, SELF1, self1), (6, LN_G, MOE1, moe1),
                    (7, LN_H, CROSS2, cross2), (8, LN_I, SELF2, self2), (9, LN_J, MOE2, moe2),
                    (10, LN_K, CROSS3, cross3), (11, LN_L, SCAN, scan), (12, LN_M, MOE3, moe3))
            for i, (at, norm_at, stage_at, stage) in enumerate(tail):
                if LAST >= at:
                    ln_dve(dve, norm_at, NL + i, x, hn)
                    stage.dve(dve, stage_at)


def shape_constants():
    p = np.arange(P)
    same = (p[:, None] // S) == (p[None, :] // S)
    c = {"ident": np.eye(P), "same_batch": np.where(same, 0.0, BLOCKED),
         "causal": np.where(same & (p[None, :] <= p[:, None]), 0.0, BLOCKED)}
    diff = np.eye(P) - np.eye(P, k=1)
    diff[:, p % S == 0] = 0.0
    c["diff"] = diff
    c["head_of"] = (p[:, None] // HD == np.arange(HG)[None, :])
    c["first_of"] = np.tile(np.arange(E, 0, -1), (P, 1))
    k = np.arange(D)
    angle = 2 * np.pi * (np.outer(k // HD, k // HD) / H + np.outer(k % HD, k % HD) / HD)
    c["basis"] = ((np.cos(angle) + np.sin(angle)) / np.sqrt(H * HD)).reshape(K2, P, D).transpose(1, 0, 2).reshape(P, -1)
    ks, kh, kd = np.fft.fftfreq(S), np.fft.fftfreq(H), np.fft.fftfreq(HD)
    km = np.sqrt(ks[None, :] ** 2 + kh[k // HD][:, None] ** 2 + kd[k % HD][:, None] ** 2 + 1e-10)
    lam, t = np.arange(S) / S, np.arange(S) * 0.1
    gain = 1.0 + 0.1 * np.sin(t + lam) * np.cos(t - 2.0 * lam + 0.5 * lam ** 2)
    c["spectrum"] = (np.cos(np.arctan(np.log(km + 1e-10))) * gain).reshape(K2, P, S).transpose(1, 0, 2).reshape(P, -1)
    split = np.zeros((P, E + 1))
    split[:E, :E] = np.eye(E)
    split[:E, E] = -1.0
    c["split9"] = split
    c["rest9"] = (p == E).astype(float)[:, None]
    return np.ascontiguousarray(np.concatenate([c[n].astype(np.float32).reshape(P, w) for n, w in CONSTS.items()], 1))


def kernel(**inputs):
    import concourse.bacc as bacc
    from concourse.bass_utils import run_bass_kernel_spmd as run

    I = {k: np.asarray(v) for k, v in inputs.items()}

    def down(v):
        return v.reshape(-1, P).T

    c = {"g_media": I["L0_xattn_gamma_media"], "b_media": I["L0_xattn_beta_media"], "g_lat": I["L0_xattn_gamma_lat"],
         "b_lat": I["L0_xattn_beta_lat"], "bq0": I["L0_xattn_bq"], "bv0": I["L0_xattn_bkv"][H0 * DH0:],
         "ln1_w": I["L0_attn_ln1_w"], "ln1_b": I["L0_attn_ln1_b"], "ln2_w": I["L0_attn_ln2_w"],
         "ln2_b": I["L0_attn_ln2_b"], "fc_b": I["L0_attn_fc_b"],
         "sw_b1": np.concatenate([I["L0_ffn_sb1"], I["L0_ffn_rb1"]], 0), "l2_b1": I["L2_ffn_b1"],
         "l3_b1": np.concatenate([I["L3_ffn_b1"], I["L3_ffn_sb1"][None]], 0),
         "bq3": I["L3_xattn_bq"], "bk3": I["L3_xattn_bk"], "bv3": I["L3_xattn_bv"],
         "bo_scan": I["L3_attn_bo"], "bs_scan": I["L3_attn_bs"]}
    r = {"bo0": I["L0_xattn_bo"], "aproj_b": I["L0_attn_aproj_b"], "mproj_b": I["L0_attn_mproj_b"],
         "gate_b": I["L0_ffn_gate_b"], "switch_b": I["L2_ffn_switch_b"], "router_b": I["L3_ffn_rb"],
         "bff2": I["L2_attn_bff"], "bo3": I["L3_xattn_bo"]}
    inner = H0 * DH0
    arrays = {
        "x": I["x"].reshape(N, D), "ctx": I["ctx_1024"], "ctx64": I["ctx_1024"][:, :S].reshape(N, D),
        "mask64": I["mask_BxS2_if1"][:, :S].reshape(1, N),
        "cols": np.concatenate([down(c[n]) for n in COLS], 1), "consts": shape_constants(),
        "rows": np.concatenate([r[n].reshape(1, -1) for n in ROWS], 1),
        "b2_l0": np.concatenate([I["L0_ffn_sb2"], I["L0_ffn_rb2"]], 0), "b2_l2": I["L2_ffn_b2"],
        "b2_l3": np.concatenate([I["L3_ffn_b2"], I["L3_ffn_sb2"][None]], 0),
        "routers": np.stack([I["L0_ffn_gate_w"], I["L1_ffn_router_kernel_DE"], I["L2_ffn_switch_w"],
                             I["L3_ffn_rw"].T], 0),
        "Wq0": I["L0_xattn_Wq"], "Wk0T": I["L0_xattn_Wkv"][:, :inner].T, "Wv0": I["L0_xattn_Wkv"][:, inner:],
        "Wo0": I["L0_xattn_Wo"], "g_media_row": I["L0_xattn_gamma_media"][None],
        "b_media_row": I["L0_xattn_beta_media"][None],
        "attn_w": I["L0_attn_attn_w"], "attn_b": I["L0_attn_attn_b"], "aproj_w": I["L0_attn_aproj_w"],
        "fc_w": I["L0_attn_fc_w"], "mproj_w": I["L0_attn_mproj_w"],
        "w1_l0": np.concatenate([I["L0_ffn_sw1"], I["L0_ffn_rw1"]], 0),
        "w2_l0": np.concatenate([I["L0_ffn_sw2"], I["L0_ffn_rw2"]], 0),
        "Wq1": I["L1_xattn_Wq"], "Wk1": I["L1_xattn_Wk"], "Wv1": I["L1_xattn_Wv"], "Wo1": I["L1_xattn_Wo"],
        "Wqa": I["L1_attn_Wq"], "Wka": I["L1_attn_Wk"], "Wva": I["L1_attn_Wv"], "Woa": I["L1_attn_Wo"],
        "gate_l1": I["L1_ffn_kernel_gating_EDF"], "up_l1": I["L1_ffn_kernel_up_EDF"],
        "down_l1": I["L1_ffn_kernel_down_EFD"],
        "Wq2": I["L2_xattn_Wq"].T, "Wo2": I["L2_xattn_Wo"].T,
        "Wqb": I["L2_attn_Wq"].T, "Wkb": I["L2_attn_Wk"].T, "Wvb": I["L2_attn_Wv"].T, "Wff": I["L2_attn_Wff"].T,
        "w1_l2": I["L2_ffn_w1"], "w2_l2": I["L2_ffn_w2"],
        "Wq3": I["L3_xattn_Wq"].T, "Wk3": I["L3_xattn_Wk"].T, "Wv3": I["L3_xattn_Wv"].T, "Wo3": I["L3_xattn_Wo"].T,
        "Wd": I["L3_attn_Wd"], "Wi": I["L3_attn_Wi"], "Wos": I["L3_attn_Wo"], "Wss": I["L3_attn_Ws"],
        "scan_small": np.concatenate([I["L3_attn_bd"].T, I["L3_attn_bi"].T, I["L3_attn_A_log"].T], 1),
        "w1_l3": np.concatenate([I["L3_ffn_w1"], I["L3_ffn_sw1"][None]], 0),
        "w2_l3": np.concatenate([I["L3_ffn_w2"], I["L3_ffn_sw2"][None]], 0),
    }
    nc = bacc.Bacc("TRN2", target_bir_lowering=False, num_devices=1)
    feed, A = {}, {"last": LAST_SUBLAYER}
    for name, a in arrays.items():
        a = np.ascontiguousarray(a)
        feed["in_" + name] = a
        A[name] = nc.dram_tensor("in_" + name, a.shape, mybir.dt.from_np(a.dtype), kind="ExternalInput").ap()
    out = nc.dram_tensor("out", (N, D), F32, kind="ExternalOutput").ap()
    program(nc, A, out)
    got = run(nc, [feed], core_ids=[0])
    return got.results[0]["out"].reshape(B, S, D)


LAST_SUBLAYER = 12
```

```python
from contextlib import ExitStack

import numpy as np

import concourse.bass as bass
from concourse import mybir

F32 = mybir.dt.float32
F32R = mybir.dt.float32r
I32 = mybir.dt.int32
ALU = mybir.AluOpType
ACT = mybir.ActivationFunctionType
AX = mybir.AxisListType
ds = bass.ds

P = 128
B, S, D = 8, 64, 256
N = B * S
T = N // P
K2 = D // P
KEYS = 1601
FULL = KEYS // P
TAIL = KEYS - FULL * P
KT = FULL + 1
H0, DH0 = 8, 128
H = 16
HD = D // H
HG = P // HD
E = 8
LAYERS = 4
CAP = N // E
BLOCKED = -1e30
EPS = 1e-5
TWO_PI = float(2 * np.pi)
ROUND = 1.5 * 2 ** 23
CHUNK = 512

COLS = dict(g_media=2, b_media=2, g_lat=2, b_lat=2, bq0=8, bv0=8,
            ln1_w=8, ln1_b=8, ln2_w=8, ln2_b=8, fc_b=32,
            sw_b1=36, l2_b1=64, l3_b1=72, bq3=2, bk3=2, bv3=2, bo_scan=4, bs_scan=4)
CONSTS = dict(ident=P, same_batch=P, causal=P, diff=P, head_of=HG, first_of=E, spectrum=2 * S, basis=2 * D,
              split9=E + 1, rest9=1, own_half=2 * HD, fold=S, stack=2 * HD)
ROWS = dict(bo0=D, aproj_b=LAYERS * D, mproj_b=LAYERS * D, gate_b=E, switch_b=E, router_b=E, bff2=D, bo3=D)


def offsets(widths):
    at, out = 0, {}
    for name, w in widths.items():
        out[name] = (at, w)
        at += w
    return out, at


def program(nc, A, out):
    with ExitStack() as ctx:
        def sb(name, shape, dt=F32):
            return ctx.enter_context(nc.sbuf_tensor(name, shape, dt))

        def sem(name):
            return ctx.enter_context(nc.semaphore(name))

        col_at, ncol = offsets(COLS)
        const_at, nconst = offsets(CONSTS)
        row_at, nrow = offsets(ROWS)

        x = sb("x", [P, T, D])
        x0 = sb("x0", [P, T, D])
        hn = sb("hn", [P, T, D])
        hT = sb("hT", [P, K2, N])
        cols = sb("cols", [P, ncol])
        consts = sb("consts", [P, nconst])
        rows = sb("rows", [1, nrow])
        b2_l0 = sb("b2_l0", [E + 1, D])
        b2_l2 = sb("b2_l2", [E, D])
        b2_l3 = sb("b2_l3", [E + 1, D])
        routers = sb("routers", [P, 4, K2, E])
        ones = sb("ones", [P, P])
        ln_st = sb("ln_st", [P, KT, 6])
        ln_mv = sb("ln_mv", [P, KT, 2])
        ln_ve = sb("ln_ve", [P, KT])
        ln_sd = sb("ln_sd", [P, KT])
        ln_rs = sb("ln_rs", [P, KT])
        w1 = [sb(f"w1_{i}", [P, K2, 1024]) for i in range(2)]
        w2 = [sb(f"w2_{i}", [P, 8, D]) for i in range(2)]
        wp = [sb(f"wp_{i}", [P, 4, K2, D]) for i in range(2)]
        SCRATCH = 30700
        scratch_at = nc.sbuf_base
        scratch = sb("scratch", [P, SCRATCH])
        ROUNDED_AT = 3368
        rounded = nc.alloc_sbuf_tensor_at("rounded", [P, SCRATCH - ROUNDED_AT], F32R,
                                          offset=scratch_at + 4 * ROUNDED_AT)
        ps = ctx.enter_context(nc.psum_tensor("ps", [P, 8, CHUNK], F32))

        def col(name, i=0, w=1):
            a = col_at[name][0]
            return cols[:, a + i:a + i + w]

        def dcol(name, i):
            return cols[:, ds(i + col_at[name][0], 1)]

        def const(name, rows_=P):
            a, w = const_at[name]
            return consts[0:rows_, a:a + w]

        def row(name, i=0, w=None):
            a, full = row_at[name]
            return rows[0:1, a + i:a + i + (w or full)]

        def carve(*shapes, start=0, memory=scratch, ends=None):
            at, views = start, []
            for shape in shapes:
                n = int(np.prod(shape))
                v = memory[:, at:at + n]
                if len(shape) == 2:
                    v = v.rearrange("p (a b) -> p a b", a=shape[0])
                if len(shape) == 3:
                    v = v.rearrange("p (a b c) -> p a b c", a=shape[0], b=shape[1])
                views.append(v)
                at += n
            assert at <= SCRATCH - (ROUNDED_AT if memory is rounded else 0), at
            if ends is not None:
                ends.append(at)
            return views

        THREE = (("hi", "hi"), ("hi", "lo"), ("lo", "hi"))

        ident = const("ident")
        one_row = ones[0:1, :]

        def bank(i, w=CHUNK, p=P):
            return ps[0:p, i, 0:w]

        stage_done = sem("stage_done")
        inputs_loaded = sem("inputs_loaded")
        stored = sem("stored")
        ones_ready = sem("ones_ready")
        ln_var, ln_std, ln_norm, ln_turned = (sem(n) for n in ("ln_var", "ln_std", "ln_norm", "ln_turned"))
        wp_loaded = [sem("wp_loaded0"), sem("wp_loaded1")]
        ffn_w = [sem("ffn_w0"), sem("ffn_w1")]
        hid_psum, silu_ready, hid_ready = sem("hid_psum"), sem("silu_ready"), sem("hid_ready")
        y_psum, y_used = sem("y_psum"), sem("y_used")
        x0_loaded = sem("x_weights_loaded")
        ctx_loaded = sem("ctx_loaded")
        latent_keys_loaded = sem("latent_keys_loaded")
        kvraw_loaded = sem("kvraw_loaded")
        lw_loaded = sem("layer_weights_loaded")
        lnorm = "ln"

        def ln_dve(dve, s, n, src, dst):
            dve.wait_ge(stage_done, s)
            for t in range(T):
                dve.bn_stats(ln_st[:, t, :], src[:, t, :])
            dve.drain()
            for t in range(T):
                dve.bn_aggr(ln_mv[:, t, :], ln_st[:, t, :])
            dve.drain()
            dve.tensor_scalar(ln_ve[:, 0:T], ln_mv[:, 0:T, 1], EPS, None, ALU.add).then_inc(ln_var, 1)
            dve.wait_ge(ln_std, n + 1)
            dve.reciprocal(ln_rs[:, 0:T], ln_sd[:, 0:T])
            dve.drain()
            for t in range(T):
                ins = dve.tensor_scalar(dst[:, t, :], src[:, t, :], ln_mv[:, t, 0:1], ln_rs[:, t:t + 1],
                                        ALU.subtract, ALU.mult)
            ins.then_inc(ln_norm, 1)

        def ln_act(act, s, n, scale=None, bias=None):
            act.wait_ge(stage_done, s)
            act.wait_ge(ln_var, n + 1)
            act.activation(ln_sd[:, 0:T], ln_ve[:, 0:T], ACT.Sqrt).then_inc(ln_std, 1)
            act.wait_ge(ln_turned, n + 1)
            for k in range(K2):
                if scale is None:
                    ins = act.activation(hT[:, k, :], bank(k), ACT.Copy)
                else:
                    ins = act.activation(hT[:, k, :], bank(k), ACT.Identity, bias=bias(k), scale=scale(k))
            act.drain().then_inc(stage_done, 1)

        def ln_pe(pe, s, n, src):
            pe.wait_ge(stage_done, s)
            pe.wait_ge(ln_norm, n + 1)
            for k in range(K2):
                for t in range(T):
                    ins = pe.transpose(ps[:, k, t * P:(t + 1) * P], src[:, t, k * P:(k + 1) * P], ident)
            ins.then_inc(ln_turned, 1)

        hid = None

        def ffn_load(sp, par, first, second, third):
            for dst, src in (first, second, third):
                sp.dma_start(dst, src).then_inc(ffn_w[par], 16)

        def ffn_pe(pe, par, loads, c, h0, nh, glu, steady, hid2, b2row=None):
            pe.wait_ge(ffn_w[par], 48 * loads)
            depth = 2 if glu else 4
            for j in range(nh):
                if steady or j >= depth:
                    pe.wait_ge(hid_ready, h0 + j - depth + 1)
                parts = ((2 * (j % 2), j), (2 * (j % 2) + 1, nh + j)) if glu else ((j % 4, j),)
                for bk, m in parts:
                    for k in range(K2):
                        ins = pe.matmul(bank(bk), w1[par][:, k, m * P:(m + 1) * P], hT[:, k, :],
                                        start=(k == 0), stop=(k == K2 - 1))
                ins.then_inc(hid_psum, 1)
            for m in range(nh):
                pe.wait_ge(hid_ready, h0 + m + 1)
                for t in range(T):
                    if m == 0 and steady:
                        pe.wait_ge(y_used, 4 * c - 4 + t + 1)
                    if m == 0 and b2row is not None:
                        pe.matmul(bank(4 + t, D), one_row, b2row, start=True, stop=False)
                    ins = pe.matmul(bank(4 + t, D), hid2[:, m, t * P:(t + 1) * P], w2[par][:, m, :],
                                    start=(m == 0 and b2row is None), stop=(m == nh - 1))
                    if m == nh - 1:
                        ins.then_inc(y_psum, 1)

        def ffn_act(act, c, h0, nh, func, bias, steady, hid2, gated=None):
            if steady:
                act.wait_ge(y_psum, 4 * c - 4)
            for j in range(nh):
                act.wait_ge(hid_psum, h0 + j + 1)
                kw = dict(bias=bias(j)) if bias else {}
                if gated is None:
                    act.activation(hid2[:, j, :], bank(j % 4), func, **kw).then_inc(hid_ready, 1)
                else:
                    act.activation(gated[:, j % 2, :], bank(2 * (j % 2)), func, **kw).then_inc(silu_ready, 1)

        def ffn_dve(dve, c, h0, g0, nh, cw, acc, hid2, gated=None, bias=None):
            if gated is not None:
                for j in range(nh):
                    dve.wait_ge(silu_ready, g0 + j + 1)
                    up = bank(2 * (j % 2) + 1)
                    if bias:
                        dve.scalar_tensor_tensor(out=hid2[:, j, :], in0=up, scalar=bias(j), in1=gated[:, j % 2, :],
                                                 op0=ALU.add, op1=ALU.mult).then_inc(hid_ready, 1)
                    else:
                        dve.tensor_tensor(hid2[:, j, :], up, gated[:, j % 2, :], ALU.mult).then_inc(hid_ready, 1)
            for t in range(T):
                dve.wait_ge(y_psum, 4 * c + t + 1)
                if cw is None:
                    dve.tensor_tensor(acc[:, t, :], bank(4 + t, D), acc[:, t, :], ALU.add).then_inc(y_used, 1)
                else:
                    dve.scalar_tensor_tensor(out=acc[:, t, :], in0=bank(4 + t, D), scalar=cw(t), in1=acc[:, t, :],
                                             op0=ALU.mult, op1=ALU.add).then_inc(y_used, 1)
            dve.drain()

        MSEM = [sem("moe_" + n) for n in ("logits_psum", "shifted", "exp", "cw_ready", "cwT_psum", "cwT_ready",
                                          "base_psum")]

        class Moe:
            def __init__(self, name, experts, nh, func, glu, router, rbias, rule, b1, b2, c0, h0, g0, loads0):
                self.name, self.experts, self.nh, self.func, self.glu = name, experts, nh, func, glu
                self.router, self.rbias, self.rule, self.b1, self.b2 = router, rbias, rule, b1, b2
                self.c0, self.h0, self.g0, self.loads0 = c0, h0, g0, loads0
                (self.logits_ready, self.shifted, self.expd, self.cw_ready, self.cwT_psum, self.cwT_ready,
                 self.base_psum) = MSEM
                o = int(name[3])
                self.o, self.exps, self.tables, self.turns = o, (0, 1, 3, 4)[o], (0, 1, 1, 2)[o], (0, 1, 1, 2)[o]
                if rule == "capacity":
                    self.choice_psum, self.kept, self.kept_sum, self.assigned, self.plan, self.plan_ready = (
                        sem(name + n) for n in ("_choice_psum", "_kept", "_kept_sum", "_assigned", "_plan",
                                                "_plan_ready"))
                (self.hidA, self.hidB, self.gated, self.lg, self.pr, self.eq, self.oh1, self.oh2, self.mx, self.m2,
                 self.sm, self.cw, self.cwT, self.t1, self.t2, self.t3, self.t4, self.t5) = carve(
                    (8, N), (8, N), (2, N), (T, E), (T, E), (T, E), (T, E), (T, E), (T,), (T,), (T,),
                    (E + 1, T), (N,), (N,), (N,), (N,), (N,), (N,))
                self.off = experts - E if rule != "capacity" else 0
                self.bodies = [(e, e % 2) for e in range(experts)]

            def counts(self, i, par):
                e = 2 * i + par
                return e, e + self.c0, self.nh * e + self.h0, self.nh * e + self.g0, i + (self.loads0[par] + 1)

            def each(self, eng, body):
                with eng.Fori(0, self.experts // 2) as i:
                    body(*self.counts(i, 0), 0)
                    body(*self.counts(i, 1), 1)
                if self.experts % 2:
                    body(*self.counts(self.experts // 2, 0), 0)

            def b1_col(self, e, j):
                width = self.nh * (2 if self.glu else 1)
                return dcol(self.b1, e * width + j) if not isinstance(e, int) else col(self.b1, e * width + j)

            def sp(self, sp, sources):
                sp.wait_ge(y_psum, 4 * self.c0)

                def body(e, c, h, g, loads, par):
                    sp.wait_ge(y_psum, 4 * c - 4)
                    ffn_load(sp, par, *sources(e, par))
                self.each(sp, body)

            def pe(self, pe, s):
                pe.wait_ge(stage_done, s)
                for t in range(T):
                    o = ps[:, 0, t * E:(t + 1) * E]
                    if self.rbias:
                        pe.matmul(o, one_row, row(self.rbias), start=True, stop=False)
                    for k in range(K2):
                        ins = pe.matmul(o, hT[:, k, t * P:(t + 1) * P], routers[:, self.router, k, :],
                                        start=(k == 0 and not self.rbias), stop=(k == K2 - 1))
                ins.then_inc(self.logits_ready, 1)
                nE = self.experts
                if self.rule == "capacity":
                    pe.wait_ge(self.cw_ready, self.o + 1)
                    for i, oh in enumerate((self.oh1, self.oh2)):
                        for t in range(T):
                            ins = pe.transpose(ps[0:E, 1 + i, t * P:(t + 1) * P], oh[:, t, :], ident)
                    ins.then_inc(self.choice_psum, 1)
                    pe.wait_ge(self.kept, 1)
                    pe.matmul(bank(3, N, E), ones[0:E, 0:E], self.t2[0:E, :], start=True, stop=True)\
                        .then_inc(self.kept_sum, 1)
                    pe.wait_ge(self.assigned, 1)
                    pe.matmul(bank(4, N, E + 1), const("split9", E), self.t2[0:E, :], start=True, stop=True)\
                        .then_inc(self.plan, 1)
                    pe.wait_ge(self.cwT_ready, self.tables + 1)
                    for t in range(T):
                        ins = pe.transpose(ps[:, 5, t * 16:t * 16 + E + 1], self.cwT[0:E + 1, t * P:(t + 1) * P],
                                           ident[0:E + 1, 0:E + 1])
                    ins.then_inc(self.plan_ready, 1)
                elif self.b2 is not None:
                    pe.wait_ge(self.cw_ready, self.o + 1)
                    for t in range(T):
                        ins = pe.transpose(ps[0:nE, 1, t * P:(t + 1) * P], self.cw[:, 0:nE, t], ident)
                    ins.then_inc(self.cwT_psum, 1)
                    pe.wait_ge(self.cwT_ready, self.tables + 1)
                if self.b2 is not None:
                    for t in range(T):
                        ins = pe.matmul(ps[:, 6 + t // 2, (t % 2) * D:(t % 2 + 1) * D],
                                        self.cwT[0:nE, t * P:(t + 1) * P], self.b2[:, :], start=True, stop=True)
                    ins.then_inc(self.base_psum, 1)
                    pe.wait_ge(self.shifted, 2 * self.o + 2)
                else:
                    pe.wait_ge(self.cw_ready, self.o + 1)

                def body(e, c, h, g, loads, par):
                    ffn_pe(pe, par, loads, c, h, self.nh, self.glu, True, (self.hidA, self.hidB)[par])
                self.each(pe, body)

            def act(self, act, s):
                act.wait_ge(stage_done, s)
                act.wait_ge(self.shifted, 2 * self.o + 1)
                act.activation(self.pr, self.lg, ACT.Exp).then_inc(self.expd, 1)
                if self.rule == "renormalised":
                    act.wait_ge(self.shifted, 2 * self.o + 2)
                    act.activation(self.sm, self.m2, ACT.Exp).then_inc(self.expd, 1)

                def body(e, c, h, g, loads, par):
                    bias = (lambda j: self.b1_col(e, j)) if self.b1 else None
                    ffn_act(act, c, h, self.nh, self.func, bias, True, (self.hidA, self.hidB)[par],
                            self.gated if self.glu else None)
                self.each(act, body)

            def one_hot(self, dve, pr, mx, oh):
                dve.tensor_reduce(mx, pr, AX.X, ALU.max)
                dve.drain()
                dve.tensor_tensor(self.eq, pr, mx.unsqueeze(2).to_broadcast([P, T, E]), ALU.is_equal)
                dve.drain()
                dve.tensor_tensor(self.eq, self.eq, const("first_of").unsqueeze(1).to_broadcast([P, T, E]), ALU.mult)
                dve.drain()
                dve.tensor_reduce(self.t1[:, 0:T], self.eq, AX.X, ALU.max)
                dve.drain()
                dve.tensor_tensor(oh, self.eq, self.t1[:, 0:T].unsqueeze(2).to_broadcast([P, T, E]), ALU.is_equal)
                dve.drain()

            def dve(self, dve, s):
                bc = lambda v: v.unsqueeze(2).to_broadcast([P, T, E])
                dve.wait_ge(stage_done, s)
                dve.wait_ge(self.logits_ready, self.o + 1)
                logits = ps[:, 0, 0:T * E].rearrange("p (t e) -> p t e", t=T)
                dve.tensor_reduce(self.mx, logits, AX.X, ALU.max)
                dve.drain()
                dve.tensor_tensor(self.lg, logits, bc(self.mx), ALU.subtract).then_inc(self.shifted, 1)
                dve.wait_ge(self.expd, self.exps + 1)
                dve.tensor_reduce(self.mx, self.pr, AX.X, ALU.add)
                dve.drain()
                dve.reciprocal(self.sm, self.mx)
                dve.drain()
                dve.tensor_tensor(self.pr, self.pr, bc(self.sm), ALU.mult)
                dve.drain()
                self.one_hot(dve, self.pr, self.mx, self.oh1)
                cw = self.cw.rearrange("p e t -> p t e")
                routed = cw[:, :, self.off:self.off + E]
                if self.rule == "top1":
                    dve.tensor_tensor(routed, self.oh1, bc(self.mx), ALU.mult)
                else:
                    dve.scalar_tensor_tensor(out=self.lg, in0=self.oh1, scalar=-4.0, in1=self.pr,
                                             op0=ALU.mult, op1=ALU.add)
                    dve.drain()
                    self.one_hot(dve, self.lg, self.m2, self.oh2)
                if self.rule == "top2":
                    dve.tensor_tensor(self.eq, self.oh1, self.oh2, ALU.add)
                    dve.drain()
                    dve.tensor_tensor(routed, self.eq, self.pr, ALU.mult)
                    dve.memset(self.cw[:, 0, :], 1.0)
                if self.rule == "renormalised":
                    dve.tensor_tensor(self.m2, self.m2, self.mx, ALU.subtract)
                    dve.drain().then_inc(self.shifted, 1)
                    dve.wait_ge(self.expd, self.exps + 2)
                    dve.tensor_scalar(self.mx, self.sm, 1.0, None, ALU.add)
                    dve.drain()
                    dve.reciprocal(self.m2, self.mx)
                    dve.drain()
                    dve.tensor_tensor(self.sm, self.sm, self.m2, ALU.mult)
                    dve.tensor_tensor(self.oh1, self.oh1, bc(self.m2), ALU.mult)
                    dve.drain()
                    dve.tensor_tensor(self.oh2, self.oh2, bc(self.sm), ALU.mult)
                    dve.drain()
                    dve.tensor_tensor(routed, self.oh1, self.oh2, ALU.add)
                dve.drain().then_inc(self.cw_ready, 1)
                nE = self.experts
                if self.rule == "capacity":
                    o1, o2, t2, t3, t4, t5 = (v[0:E, :] for v in (self.t1, self.cwT, self.t2, self.t3, self.t4, self.t5))
                    unit = ones[0:E, 0:1].to_broadcast([E, N])
                    dve.wait_ge(self.choice_psum, 1)
                    dve.tensor_copy(o1, bank(1, N, E))
                    dve.tensor_copy(o2, bank(2, N, E))
                    dve.drain()
                    dve.tensor_tensor_scan(t3, unit, o1, 0.0, ALU.mult, ALU.add)
                    dve.drain()
                    dve.scalar_tensor_tensor(out=t2, in0=t3, scalar=float(CAP), in1=o1, op0=ALU.is_le, op1=ALU.mult)\
                        .then_inc(self.kept, 1)
                    dve.tensor_scalar(self.mx[0:E, 0:1], t3[:, N - 1:N], float(CAP), None, ALU.min)
                    dve.wait_ge(self.kept_sum, 1)
                    dve.tensor_scalar(t4, bank(3, N, E), -1.0, 1.0, ALU.mult, ALU.add)
                    dve.drain()
                    dve.tensor_tensor(t4, t4, o2, ALU.mult)
                    dve.drain()
                    dve.tensor_tensor_scan(t5, unit, t4, 0.0, ALU.mult, ALU.add)
                    dve.drain()
                    dve.tensor_scalar(t5, t5, self.mx[0:E, 0:1], float(CAP), ALU.add, ALU.is_le)
                    dve.drain()
                    dve.tensor_tensor(t4, t4, t5, ALU.mult)
                    dve.drain()
                    dve.tensor_tensor(t2, t2, t4, ALU.add)
                    dve.drain().then_inc(self.assigned, 1)
                    dve.wait_ge(self.plan, 1)
                    dve.tensor_scalar(self.cwT[0:E + 1, :], bank(4, N, E + 1), const("rest9", E + 1), None, ALU.add)\
                        .then_inc(self.cwT_ready, 1)
                    dve.wait_ge(self.plan_ready, 1)
                    dve.tensor_copy(cw, ps[:, 5, 0:16 * T].rearrange("p (t e) -> p t e", t=T)[:, :, 0:E + 1])
                    dve.drain()
                elif self.b2 is not None:
                    dve.wait_ge(self.cwT_psum, self.turns + 1)
                    dve.tensor_copy(self.cwT[0:nE, :], bank(1, N, nE)).then_inc(self.cwT_ready, 1)
                if self.b2 is not None:
                    dve.wait_ge(self.base_psum, self.tables + 1)
                    dve.tensor_tensor(x[:, :, :].rearrange("p t d -> p (t d)"),
                                      ps[:, 6:8, :].rearrange("p a b -> p (a b)"),
                                      x[:, :, :].rearrange("p t d -> p (t d)"), ALU.add)
                    dve.drain().then_inc(self.shifted, 1)
                flat = self.cw.rearrange("p e t -> p (e t)")

                def body(e, c, h, g, loads, par):
                    weight = lambda t: (flat[:, ds(e * T + t, 1)] if not isinstance(e, int)
                                        else flat[:, e * T + t:e * T + t + 1])
                    bias = (lambda j: self.b1_col(e, self.nh + j)) if self.b1 else None
                    ffn_dve(dve, c, h, g, self.nh, weight, x, (self.hidA, self.hidB)[par],
                            self.gated if self.glu else None, bias)
                self.each(dve, body)
                dve.drain().then_inc(stage_done, 1)

        LSEM = {n: sem("local_" + n) for n in (
            "kv_rows_copied", "qk_psum", "q_ready", "k_ready", "v_psum", "v_ready", "scores_psum", "shifted", "exp",
            "p_ready", "pT_psum", "pT_ready", "o_psum", "o_ready", "oT_psum", "oT_ready", "y_psum", "y_added",
            "prepared")}

        class Local:

            def __init__(self, order, slot, loads, scale, mask, kvsrc, extra_mask=False, grouped=False, bo=None):
                self.t0 = T * order
                self.slot, self.loads, self.scale, self.mask, self.bo = slot, loads, scale, mask, bo
                self.extra_mask, self.grouped = extra_mask, grouped
                (self.copied, self.qk_psum, self.q_ready, self.k_ready, self.v_psum, self.v_ready, self.s_psum,
                 self.shifted, self.expd, self.p_ready, self.pT_psum, self.pT_ready, self.o_psum, self.o_ready,
                 self.oT_psum, self.oT_ready, self.y_ps, self.added, self.prepared) = (
                    LSEM[n] for n in
                    ("kv_rows_copied", "qk_psum", "q_ready", "k_ready", "v_psum", "v_ready", "scores_psum",
                     "shifted", "exp", "p_ready", "pT_psum", "pT_ready", "o_psum", "o_ready", "oT_psum", "oT_ready",
                     "y_psum", "y_added", "prepared"))
                (self.src64, self.kvt, self.q, self.k, self.v, self.sm, self.pT, self.o, self.oT, self.mx, self.rs,
                 self.keysT, self.maskt, self.keyrow, self.raw, self.keyraw, self.kraw) = carve(
                    (K2, N), (K2, P), (K2, P), (K2, HG, P), (D,), (H, P), (H, P), (D,), (K2, P), (H,), (H,),
                    (T, D), (T, P), (N,), (K2, P), (N,), (K2, P))
                self.kvsrc = self.src64 if kvsrc is None else kvsrc

            def pe(self, pe, s):
                W = wp[self.slot]
                pe.wait_ge(stage_done, s)
                pe.wait_ge(wp_loaded[self.slot], 64 * self.loads)
                if self.extra_mask:
                    pe.wait_ge(latent_keys_loaded, 32)
                    for k in range(K2):
                        for t in range(T):
                            pe.transpose(ps[:, k, t * P:(t + 1) * P], self.keysT[:, t, k * P:(k + 1) * P], ident)
                    pe.wait_ge(self.prepared, 1)
                    pe.matmul(bank(2), one_row, self.keyrow[0:1, :], start=True, stop=True).then_inc(self.qk_psum, 1)
                    pe.wait_ge(self.prepared, 3)
                if self.grouped:
                    pe.wait_ge(self.prepared, 4)
                with pe.Fori(0, T) as t:
                    pe.wait_ge(self.added, t + (self.t0 + 1))
                    for m in range(K2):
                        for k in range(K2):
                            pe.matmul(ps[:, 7, m * P:(m + 1) * P], W[:, 0, k, m * P:(m + 1) * P],
                                      hT[:, k, ds(t * P, P)], start=(k == 0), stop=(k == K2 - 1))
                    pe.wait_ge(self.copied, t + (self.t0 + 1))
                    for m in range(K2):
                        for k in range(K2):
                            ins = pe.matmul(ps[:, 0, D + m * P:D + (m + 1) * P], W[:, 1, k, m * P:(m + 1) * P],
                                            self.kvt[:, k, :], start=(k == 0), stop=(k == K2 - 1))
                    ins.then_inc(self.qk_psum, 1)
                    for k in range(K2):
                        ins = pe.matmul(bank(1, D), self.kvt[:, k, :], W[:, 2, k, :], start=(k == 0), stop=(k == K2 - 1))
                    ins.then_inc(self.v_psum, 1)
                    pe.wait_ge(self.q_ready, t + (self.t0 + 1))
                    pe.wait_ge(self.k_ready, t + (self.t0 + 1))
                    for g in range(K2):
                        for half in range(2):
                            ins = pe.matmul(bank(2 + 2 * g + half), self.q[:, g, :],
                                            self.k[:, g, 4 * half:4 * half + 4, :], start=True, stop=True)
                    ins.then_inc(self.s_psum, 1)
                    pe.wait_ge(self.p_ready, t + (self.t0 + 1))
                    for h in range(H):
                        ins = pe.transpose(ps[:, 2 + h // 4, (h % 4) * P:(h % 4 + 1) * P], self.sm[:, h, :], ident)
                    ins.then_inc(self.pT_psum, 1)
                    pe.wait_ge(self.pT_ready, t + (self.t0 + 1))
                    pe.wait_ge(self.v_ready, t + (self.t0 + 1))
                    for h in range(H):
                        ins = pe.matmul(ps[:, 6, h * HD:(h + 1) * HD], self.pT[:, h, :], self.v[:, h * HD:(h + 1) * HD],
                                        start=True, stop=True)
                    ins.then_inc(self.o_psum, 1)
                    pe.wait_ge(self.o_ready, t + (self.t0 + 1))
                    for k in range(K2):
                        ins = pe.transpose(ps[:, 7, k * P:(k + 1) * P], self.o[:, k * P:(k + 1) * P], ident)
                    ins.then_inc(self.oT_psum, 1)
                    pe.wait_ge(self.oT_ready, t + (self.t0 + 1))
                    if self.bo:
                        pe.matmul(bank(1, D), one_row, row(self.bo), start=True, stop=False)
                    for k in range(K2):
                        ins = pe.matmul(bank(1, D), self.oT[:, k, :], W[:, 3, k, :], start=(k == 0 and not self.bo),
                                        stop=(k == K2 - 1))
                    ins.then_inc(self.y_ps, 1)

            def act(self, act, s):
                act.wait_ge(stage_done, s)
                if self.extra_mask:
                    act.wait_ge(self.prepared, 3)
                with act.Fori(0, T) as t:
                    act.activation(self.kvt, self.kvsrc[:, :, ds(t * P, P)], ACT.Copy).then_inc(self.copied, 1)
                    act.wait_ge(self.qk_psum, t + (self.t0 + 2))
                    act.activation(self.q, ps[:, 7, 0:D].rearrange("p (m n) -> p m n", m=K2), ACT.Copy,
                                   scale=self.scale).then_inc(self.q_ready, 1)
                    act.wait_ge(self.v_psum, t + (self.t0 + 1))
                    act.activation(self.v, bank(1, D), ACT.Copy).then_inc(self.v_ready, 1)
                    act.wait_ge(self.shifted, t + (self.t0 + 1))
                    act.activation(self.sm, self.sm, ACT.Exp).then_inc(self.expd, 1)
                    act.wait_ge(self.pT_psum, t + (self.t0 + 1))
                    act.activation(self.pT.rearrange("p h n -> p (h n)"), ps[:, 2:6, :].rearrange("p a b -> p (a b)"),
                                   ACT.Copy).then_inc(self.pT_ready, 1)
                    act.wait_ge(self.oT_psum, t + (self.t0 + 1))
                    act.activation(self.oT, ps[:, 7, 0:D].rearrange("p (m n) -> p m n", m=K2), ACT.Copy)\
                        .then_inc(self.oT_ready, 1)

            def dve(self, dve, s):
                dve.wait_ge(stage_done, s)
                if self.extra_mask:
                    dve.wait_ge(latent_keys_loaded, 32)
                    dve.tensor_copy(self.keyrow[0:1, :], self.keyraw[0:1, :].bitcast(I32))
                    dve.drain()
                    dve.tensor_scalar(self.keyrow[0:1, :], self.keyrow[0:1, :], 0.0, BLOCKED, ALU.is_equal, ALU.mult)\
                        .then_inc(self.prepared, 1)
                    dve.wait_ge(self.qk_psum, 1)
                    dve.tensor_copy(self.src64, ps[:, 0:2, :]).then_inc(self.prepared, 1)
                    dve.tensor_tensor(self.maskt, ps[:, 2, :].rearrange("p (t n) -> p t n", t=T),
                                      const(self.mask).unsqueeze(1).to_broadcast([P, T, P]), ALU.add)\
                        .then_inc(self.prepared, 1)
                if self.grouped:
                    dve.wait_ge(kvraw_loaded, 32)
                    dve.wait_ge(wp_loaded[self.slot], 64 * self.loads)
                    for i, raw in enumerate((self.raw, self.kraw)):
                        for k in range(K2):
                            g = raw[:, k, 0:64].rearrange("p (g d) -> p g d", g=4).unsqueeze(2).to_broadcast([P, 4, 4, HD])
                            o = wp[self.slot][:, 1 + i, k, :].rearrange("p (g r d) -> p g r d", g=4, r=4)
                            dve.tensor_copy(o, g)
                    dve.drain().then_inc(self.prepared, 1)
                dve.drain()
                heads = lambda v: v.unsqueeze(2).to_broadcast([P, H, P])
                with dve.Fori(0, T) as t:
                    dve.wait_ge(self.qk_psum, t + (self.t0 + 2))
                    for g in range(K2):
                        ins = dve.tensor_tensor(self.k[:, g, :, :],
                                                ps[:, 0, D + g * P:D + (g + 1) * P].unsqueeze(1).to_broadcast([P, HG, P]),
                                                const("head_of").unsqueeze(2).to_broadcast([P, HG, P]), ALU.mult)
                    ins.then_inc(self.k_ready, 1)
                    dve.wait_ge(self.s_psum, t + (self.t0 + 1))
                    scores = ps[:, 2:6, :].rearrange("p a (c n) -> p (a c) n", n=P)
                    m = (self.maskt[:, ds(t, 1), :] if self.extra_mask else const(self.mask).unsqueeze(1))
                    dve.tensor_tensor(self.sm, scores, m.to_broadcast([P, H, P]), ALU.add)
                    dve.drain()
                    dve.tensor_reduce(self.mx, self.sm, AX.X, ALU.max)
                    dve.drain()
                    dve.tensor_tensor(self.sm, self.sm, heads(self.mx), ALU.subtract).then_inc(self.shifted, 1)
                    dve.wait_ge(self.expd, t + (self.t0 + 1))
                    dve.tensor_reduce(self.mx, self.sm, AX.X, ALU.add)
                    dve.drain()
                    dve.reciprocal(self.rs, self.mx)
                    dve.drain()
                    dve.tensor_tensor(self.sm, self.sm, heads(self.rs), ALU.mult).then_inc(self.p_ready, 1)
                    dve.wait_ge(self.o_psum, t + (self.t0 + 1))
                    dve.tensor_copy(self.o, bank(6, D)).then_inc(self.o_ready, 1)
                    dve.wait_ge(self.y_ps, t + (self.t0 + 1))
                    xt = x[:, ds(t, 1), :]
                    dve.tensor_tensor(xt, bank(1, D).unsqueeze(1), xt, ALU.add).then_inc(self.added, 1)
                dve.drain().then_inc(stage_done, 1)

        chunks = [(c * CHUNK, min(CHUNK, KEYS - c * CHUNK)) for c in range(4)]

        FSEM, CSEM = {}, {}

        def cross_sem(n):
            if n not in CSEM:
                CSEM[n] = sem("cross_" + n)
            return CSEM[n]

        def own(v):
            return v.bitcast(F32)

        class Flash:

            def __init__(self, name, nj, tiles):
                if name not in FSEM:
                    FSEM[name] = [sem(f"{name}_{n}") for n in ("scores_psum", "max_ready", "exp_done", "pT_psum",
                                                               "pT_by_act", "pT_by_dve", "o_psum", "o_taken",
                                                               "batch_done")]
                self.nj, self.tiles = nj, tiles
                self.keys = sum(tiles)
                self.chunks = [(c * CHUNK, min(CHUNK, self.keys - c * CHUNK)) for c in range(4)]
                self.turns = [range(c, min(c + 4, len(tiles))) for c in range(0, len(tiles), 4)]
                (self.s_psum, self.max_ready, self.exp_done, self.pT_psum, self.pT_act, self.pT_dve, self.o_psum,
                 self.o_taken, self.batch_done) = FSEM[name]

            def start(self, kt):
                return kt * P if kt < KT else KEYS

            def pe_turn(self, pe, J, p):
                for c, tiles in enumerate(self.turns):
                    if c != 3:
                        pe.wait_ge(self.exp_done, 3 * J + c + 4)
                    if c >= 2:
                        pe.wait_ge((self.pT_act, self.pT_dve)[c % 2], 2 * J + 1)
                    for i, kt in enumerate(tiles):
                        n = self.tiles[kt]
                        ins = pe.transpose(ps[0:n, 4 + c % 2, i * P:(i + 1) * P],
                                           p[:, self.start(kt):self.start(kt) + n], ident)
                    ins.then_inc(self.pT_psum, 1)

            def copy_turned(self, eng, copy, J, c, pT, done):
                tiles = self.turns[c]
                eng.wait_ge(self.pT_psum, 4 * J + c + 1)
                full = [kt for kt in tiles if self.tiles[kt] == P]
                if full:
                    ins = copy(pT[:, full[0]:full[-1] + 1, :],
                               ps[:, 4 + c % 2, 0:len(full) * P].rearrange("p (a b) -> p a b", b=P))
                for kt in tiles:
                    if self.tiles[kt] != P:
                        n, i = self.tiles[kt], kt - tiles[0]
                        ins = copy(pT[0:n, kt, :], ps[0:n, 4 + c % 2, i * P:(i + 1) * P])
                ins.then_inc(done, 1)

            def act_turn(self, act, J, pT):
                for c in (0, 2):
                    self.copy_turned(act, lambda o, i: act.activation(o, i, ACT.Copy), J, c, pT, self.pT_act)

            def dve_turn(self, dve, J, pT):
                for c in (1, 3):
                    self.copy_turned(dve, dve.tensor_copy, J, c, pT, self.pT_dve)

            def pe_wait_turned(self, pe, J, c):
                pe.wait_ge((self.pT_act, self.pT_dve)[c % 2], 2 * J + c // 2 + 1)

            def act_exp(self, act, J, p, negmax, den):
                act.wait_ge(self.max_ready, J + 1)
                flat = ps[:, 0:4, :].rearrange("p a b -> p (a b)")
                for g, (a, z) in enumerate(((0, CHUNK), (CHUNK, 2 * CHUNK), (2 * CHUNK, self.keys))):
                    act.activation(p[:, a:z], flat[:, a:z], ACT.Exp, bias=negmax, accum_out=den[:, g:g + 1])\
                        .then_inc(self.exp_done, 1)

            def dve_max(self, dve, J, part, negmax, which=range(4)):
                for c in which:
                    dve.wait_ge(self.s_psum, 4 * J + c + 1)
                    dve.tensor_reduce(part[:, c:c + 1], bank(c, self.chunks[c][1]), AX.X, ALU.max)
                if 3 in which:
                    dve.drain()
                    dve.tensor_reduce(negmax, part, AX.X, ALU.max, negate=True).then_inc(self.max_ready, 1)

            def dve_sums(self, dve, J, den, total, rden):
                dve.wait_ge(self.o_psum, J + 1)
                dve.tensor_reduce(total, den, AX.X, ALU.add)
                dve.drain()
                dve.reciprocal(rden, total)
                dve.drain()

        class Cross(Flash):
            WIDE = KEYS + 1

            def __init__(self, order, slot, loads, ctx_before, biased):
                super().__init__("cross", H // 2, [P] * FULL + [TAIL])
                self.b0, self.order = B * order, order
                self.slot, self.loads, self.ctx_before, self.biased = slot, loads, ctx_before, biased
                (self.w_ready, self.q_psum, self.q_ready, self.qbd_ready, self.turned, self.x_hi, self.x_lo,
                 self.k_psum, self.k_hi, self.k_lo, self.v_psum, self.v_hi, self.v_lo, self.pv_psum, self.pv_copied, self.o_rows, self.oT_psum,
                 self.oT_final, self.y_ps) = (
                    cross_sem(n) for n in ("weights_split", "q_psum", "q_split", "q_blocks", "ctx_turned", "ctxT_high",
                                           "ctxT_low", "k_psum", "k_high", "k_low", "v_psum", "v_high", "v_low",
                                           "pv_psum", "pv_copied",
                                           "o_rows", "oT_psum", "oT_final", "y_psum"))
                ends = []
                W = self.WIDE
                self.ctx, self.st = carve((KT, D), (40,), ends=ends)
                self.oT = hn[:, :, :].rearrange("p t d -> p (t d)").rearrange("p (k n) -> p k n", k=K2)
                self.o = x0[:, 0, 0:self.nj * 2 * HD].rearrange("p (j d) -> p j d", j=self.nj)
                assert ends[0] == ROUNDED_AT, ends
                names = ("x_low", "x_high", "k_high", "k_low", "qb_high", "qb_low", "q_high", "q_low", "w_high", "w_low",
                         "values", "pT_low")
                shapes = ((K2, W), (K2, W), (K2, W), (K2, W), (K2, HG * S), (K2, HG * S), (K2, N), (K2, N),
                          (2 * K2, D), (2 * K2, D), (KT * self.nj, 4 * HD), (KT, P))
                r = dict(zip(names, carve(*shapes, memory=rounded)))
                self.xT = {"hi": r["x_high"], "lo": r["x_low"]}
                self.kT = {"hi": r["k_high"], "lo": r["k_low"]}
                self.qbd = {"hi": r["qb_high"], "lo": r["qb_low"]}
                self.q = {"hi": r["q_high"], "lo": r["q_low"]}
                self.w = {"hi": r["w_high"], "lo": r["w_low"]}
                self.p = carve((KEYS,), (KEYS,), start=ROUNDED_AT)
                pT_high, = carve((KT, P), start=2 * KEYS, memory=rounded)
                self.pT = {"hi": pT_high, "lo": r["pT_low"]}
                self.v = r["values"].rearrange("p (t j) c -> p t j c", t=KT)
                self.v_part = {"hi": self.v[:, :, :, 0:2 * HD], "lo": self.v[:, :, :, 2 * HD:4 * HD]}
                self.sums = x0[0:4 * HD, 1, 0:2 * P].rearrange("p (q r) -> p q r", q=2)
                self.pT_hi, self.pT_lo = self.pT_act, self.pT_dve

            def sp(self, sp, s, ctx_rows):
                sp.wait_ge(stage_done, s)
                with sp.Fori(0, B) as b:
                    n = b + self.b0
                    sp.wait_ge(self.turned, 8 * n + 8)
                    sp.dma_start(self.ctx[:, 0:FULL, :],
                                 ctx_rows[b, 0:FULL * P, :].rearrange("(t p) d -> p t d", p=P)).then_inc(ctx_loaded, 16)
                    sp.dma_start(self.ctx[0:TAIL, FULL, :], ctx_rows[b, FULL * P:KEYS, :]).then_inc(ctx_loaded, 16)

            def pool(self, pool, s):
                pool.wait_ge(stage_done, s)
                pool.wait_ge(wp_loaded[self.slot], 64 * self.loads)
                kv = wp[self.slot][:, 1:3, :, :].rearrange("p a k n -> p (a k) n")
                pool.tensor_copy(self.w["hi"], kv)
                pool.drain()
                pool.tensor_tensor(self.w["lo"], kv, own(self.w["hi"]), ALU.subtract)
                pool.drain().then_inc(self.w_ready, 1)
                pool.wait_ge(self.q_ready, self.order + 1)
                with pool.Fori(0, B) as b:
                    u = b + self.b0
                    pool.wait_ge(self.batch_done, u + 1)
                    for part in ("hi", "lo"):
                        for g in range(K2):
                            pool.tensor_tensor(self.qbd[part][:, g, :].rearrange("p (h q) -> p h q", h=HG),
                                               own(self.q[part])[:, g, ds(b * S, S)].unsqueeze(1)
                                               .to_broadcast([P, HG, S]),
                                               const("head_of").unsqueeze(2).to_broadcast([P, HG, S]), ALU.mult)
                        pool.memset(own(self.xT[part])[:, :, KEYS:self.WIDE], 0.0)
                    pool.drain().then_inc(self.qbd_ready, 1)

            PROLOGUE = (("x", 0), ("x", 1), ("k", 0), ("x", 2), ("k", 1), ("x", 3), ("k", 2), ("k", 3))

            def width(self, c, kind):
                a, w = self.chunks[c]
                return a, (w + 1 if kind == "k" and c == 3 else w)

            def pe_rows(self, pe, J, q):
                pe.wait_ge(self.pv_copied, J + 1)
                pe.matmul(ps[:, 6 + q, P:P + 2 * HD], self.sums[:, q, :], const("stack", 4 * HD), start=True, stop=True)\
                    .then_inc(self.o_psum, 1)

            def pe_scores(self, pe, J, j, half):
                g, jj = j // 4, j % 4
                for c in (2 * half, 2 * half + 1):
                    a, w = self.width(c, "k")
                    if c < 3:
                        pe.wait_ge(self.exp_done, 3 * J + c + 1)
                    for n, (ii, kk) in enumerate(THREE):
                        ins = pe.matmul(bank(c, w), self.qbd[ii][:, g, 2 * jj * S:(2 * jj + 2) * S],
                                        self.kT[kk][:, g, a:a + w], start=(n == 0), stop=(n == 2))
                    ins.then_inc(self.s_psum, 1)

            def pe_turn(self, pe, J, p, half):
                for c in (2 * half, 2 * half + 1):
                    if c != 3:
                        pe.wait_ge(self.exp_done, 3 * J + c + 4)
                    if c >= 2:
                        pe.wait_ge(self.pT_lo, 4 * J + c - 1)
                    for i, kt in enumerate(self.turns[c]):
                        n = self.tiles[kt]
                        ins = pe.transpose(ps[0:n, 4 + c % 2, i * P:(i + 1) * P],
                                           p[:, self.start(kt):self.start(kt) + n], ident)
                    ins.then_inc(self.pT_psum, 1)

            def turned_views(self, c, part):
                tiles, n = self.turns[c], self.tiles[self.turns[c][0]]
                return (ps[0:n, 4 + c % 2, 0:len(tiles) * P].rearrange("p (a b) -> p a b", b=P),
                        self.pT[part][0:n, tiles[0]:tiles[-1] + 1, :])

            def value_views(self, i, part):
                if 2 * i + 1 < KT:
                    return (bank(i).rearrange("p (t j c) -> p t j c", t=2, j=self.nj),
                            self.v_part[part][:, 2 * i:2 * i + 2, :, :])
                return (bank(i, D, TAIL).rearrange("p (j c) -> p j c", j=self.nj), self.v_part[part][0:TAIL, 2 * i, :, :])

            def act_turn(self, act, J):
                for c in range(4):
                    act.wait_ge(self.pT_psum, 4 * J + c + 1)
                    turned, high = self.turned_views(c, "hi")
                    act.activation(high, turned, ACT.Copy).then_inc(self.pT_hi, 1)

            def dve_rows(self, dve, J, j):
                q = j % 2
                dve.wait_ge(self.o_psum, J + 1)
                dve.scalar_tensor_tensor(out=self.o[:, j, :], in0=ps[:, 6 + q, P:P + 2 * HD],
                                         scalar=self.st[:, 20 + q:21 + q], in1=const("own_half"), op0=ALU.mult,
                                         op1=ALU.mult).then_inc(self.o_taken, 1)

            def dve_turn(self, dve, J, half):
                for c in (2 * half, 2 * half + 1):
                    dve.wait_ge(self.pT_hi, 4 * J + c + 1)
                    turned, high = self.turned_views(c, "hi")
                    dve.tensor_tensor(self.turned_views(c, "lo")[1], turned, own(high), ALU.subtract)\
                        .then_inc(self.pT_lo, 1)

            def pe(self, pe, s):
                W = wp[self.slot]
                pe.wait_ge(stage_done, s)
                pe.wait_ge(wp_loaded[self.slot], 64 * self.loads)
                for m in range(K2):
                    for k in range(K2):
                        ins = pe.matmul(bank(m), W[:, 0, k, m * P:(m + 1) * P], hT[:, k, :], start=(k == 0),
                                        stop=(k == K2 - 1))
                ins.then_inc(self.q_psum, 1)
                pe.wait_ge(self.q_ready, self.order + 1)
                pe.wait_ge(self.w_ready, self.order + 1)
                with pe.Fori(0, B) as b:
                    u = b + self.b0
                    pe.wait_ge(self.batch_done, u + 1)
                    pe.wait_ge(ctx_loaded, 32 * b + (32 * self.ctx_before + 32))
                    for kind, c in self.PROLOGUE:
                        a, w = self.width(c, kind)
                        if kind == "x":
                            for f in range(K2):
                                if c >= 2:
                                    pe.wait_ge(self.x_lo, 8 * u + 2 * (c - 2) + f + 1)
                                for i, kt in enumerate(self.turns[c]):
                                    n = self.tiles[kt]
                                    ins = pe.transpose(ps[:, 2 * (c % 2) + f, i * P:i * P + n],
                                                       self.ctx[0:n, kt, f * P:(f + 1) * P], ident[0:n, 0:n])
                                ins.then_inc(self.turned, 1)
                        else:
                            pe.wait_ge(self.x_lo, 8 * u + 2 * c + 2)
                            if c == 3:
                                pe.wait_ge(self.qbd_ready, u + 1)
                            for m in range(K2):
                                if c >= 2:
                                    pe.wait_ge(self.k_lo, 8 * u + 2 * (c - 2) + m + 1)
                                for n, (i, j) in enumerate(THREE):
                                    for k in range(K2):
                                        ins = pe.matmul(bank(4 + 2 * (c % 2) + m, w),
                                                        self.w[i][:, k, m * P:(m + 1) * P],
                                                        self.xT[j][:, k, a:a + w],
                                                        start=(n == 0 and k == 0), stop=(n == 2 and k == K2 - 1))
                                ins.then_inc(self.k_psum, 1)
                    for i in range((KT + 1) // 2):
                        if i >= 4:
                            pe.wait_ge(self.k_lo, 8 * u + i + 1)
                        for kt in range(2 * i, min(2 * i + 2, KT)):
                            n = self.tiles[kt]
                            for q, (ii, jj) in enumerate(THREE):
                                for k in range(K2):
                                    ins = pe.matmul(ps[0:n, i, (kt % 2) * D:(kt % 2 + 1) * D],
                                                    self.xT[ii][:, k, kt * P:kt * P + n], self.w[jj][:, K2 + k, :],
                                                    start=(q == 0 and k == 0), stop=(q == 2 and k == K2 - 1))
                        ins.then_inc(self.v_psum, 1)
                    pe.wait_ge(self.k_lo, 8 * u + 8)
                    pe.wait_ge(self.v_lo, 7 * u + 7)
                    for j in range(self.nj + 1):
                        for half in (0, 1):
                            if j < self.nj:
                                self.pe_scores(pe, self.nj * u + j, j, half)
                            if j:
                                self.pe_turn(pe, self.nj * u + (j - 1), self.p[(j - 1) % 2], half)
                            if half == 0 and j >= 2:
                                self.pe_rows(pe, self.nj * u + (j - 2), j % 2)
                        if j:
                            J = self.nj * u + (j - 1)
                            pe.wait_ge(self.o_taken, J + 1)
                            o = 6 + (j - 1) % 2
                            for c, tiles in enumerate(self.turns):
                                pe.wait_ge(self.pT_lo, 4 * J + c + 1)
                                for kt in tiles:
                                    n = self.tiles[kt]
                                    for part in ("hi", "lo"):
                                        ins = pe.matmul(ps[0:4 * HD, o, 0:P], self.v[0:n, kt, j - 1, :],
                                                        self.pT[part][0:n, kt, :],
                                                        start=(kt == 0 and part == "hi"),
                                                        stop=(kt == KT - 1 and part == "lo"))
                            ins.then_inc(self.pv_psum, 1)
                    self.pe_rows(pe, self.nj * u + (self.nj - 1), (self.nj - 1) % 2)
                    pe.wait_ge(self.o_rows, u + 1)
                    for g in range(K2):
                        ins = pe.matmul(ps[:, 6, g * S:(g + 1) * S],
                                        self.o[:, 4 * g:4 * g + 4, :].rearrange("p a b -> p (a b)"), const("fold"),
                                        start=True, stop=True)
                    ins.then_inc(self.oT_psum, 1)
                pe.wait_ge(self.oT_final, self.order + 1)
                for t in range(T):
                    if self.biased:
                        pe.matmul(bank(t, D), one_row, row("bo3"), start=True, stop=False)
                    for k in range(K2):
                        ins = pe.matmul(bank(t, D), self.oT[:, k, t * P:(t + 1) * P], W[:, 3, k, :],
                                        start=(k == 0 and not self.biased), stop=(k == K2 - 1))
                    ins.then_inc(self.y_ps, 1)

            def act(self, act, s):
                act.wait_ge(stage_done, s)
                with act.Fori(0, B) as b:
                    u = b + self.b0
                    for kind, c in self.PROLOGUE:
                        a, w = self.width(c, kind)
                        for f in range(K2):
                            if kind == "x":
                                act.wait_ge(self.turned, 8 * u + 8 + 2 * c + f + 1)
                                act.activation(self.xT["hi"][:, f, a:a + w], bank(2 * (c % 2) + f, w), ACT.Copy)\
                                    .then_inc(self.x_hi, 1)
                            else:
                                act.wait_ge(self.k_psum, 8 * u + 2 * c + f + 1)
                                o, i = self.kT["hi"][:, f, a:a + w], bank(4 + 2 * (c % 2) + f, w)
                                if self.biased:
                                    ins = act.activation(o, i, ACT.Identity, bias=col("bk3", f))
                                else:
                                    ins = act.activation(o, i, ACT.Copy)
                                ins.then_inc(self.k_hi, 1)
                    for i in range((KT + 1) // 2):
                        act.wait_ge(self.v_psum, 7 * u + i + 1)
                        values, high = self.value_views(i, "hi")
                        act.activation(high, values, ACT.Copy).then_inc(self.v_hi, 1)
                    for j in range(self.nj + 1):
                        if j:
                            self.act_turn(act, self.nj * u + (j - 1))
                        if j < self.nj:
                            q = j % 2
                            self.act_exp(act, self.nj * u + j, self.p[q], self.st[:, q:q + 1],
                                         self.st[:, 4 + 3 * q:7 + 3 * q])
                        if j:
                            q = (j - 1) % 2
                            act.wait_ge(self.pv_psum, self.nj * u + j)
                            act.activation(self.sums[:, q, :], ps[0:4 * HD, 6 + q, 0:P], ACT.Copy)\
                                .then_inc(self.pv_copied, 1)

            def dve(self, dve, s):
                dve.wait_ge(stage_done, s)
                dve.wait_ge(self.q_psum, self.order + 1)
                for m in range(K2):
                    qf = self.oT[:, m, :]
                    if self.biased:
                        dve.tensor_scalar(qf, bank(m), col("bq3", m), HD ** -0.5, ALU.add, ALU.mult)
                    else:
                        dve.tensor_scalar(qf, bank(m), HD ** -0.5, None, ALU.mult)
                    dve.drain()
                    dve.tensor_copy(self.q["hi"][:, m, :], qf)
                    dve.drain()
                    dve.tensor_tensor(self.q["lo"][:, m, :], qf, own(self.q["hi"])[:, m, :], ALU.subtract)
                dve.drain().then_inc(self.q_ready, 1)
                with dve.Fori(0, B) as b:
                    u = b + self.b0
                    for kind, c in self.PROLOGUE:
                        a, w = self.width(c, kind)
                        for f in range(K2):
                            if kind == "x":
                                dve.wait_ge(self.x_hi, 8 * u + 2 * c + f + 1)
                                dve.tensor_tensor(self.xT["lo"][:, f, a:a + w], bank(2 * (c % 2) + f, w),
                                                  own(self.xT["hi"])[:, f, a:a + w], ALU.subtract).then_inc(self.x_lo, 1)
                            else:
                                dve.wait_ge(self.k_hi, 8 * u + 2 * c + f + 1)
                                o, i = self.kT["lo"][:, f, a:a + w], bank(4 + 2 * (c % 2) + f, w)
                                hi = own(self.kT["hi"])[:, f, a:a + w]
                                if self.biased:
                                    ins = dve.scalar_tensor_tensor(out=o, in0=i, scalar=col("bk3", f), in1=hi,
                                                                   op0=ALU.add, op1=ALU.subtract)
                                else:
                                    ins = dve.tensor_tensor(o, i, hi, ALU.subtract)
                                ins.then_inc(self.k_lo, 1)
                    for i in range((KT + 1) // 2):
                        dve.wait_ge(self.v_hi, 7 * u + i + 1)
                        values, high = self.value_views(i, "hi")
                        dve.tensor_tensor(self.value_views(i, "lo")[1], values, own(high), ALU.subtract)\
                            .then_inc(self.v_lo, 1)
                    for j in range(self.nj + 1):
                        q = j % 2
                        for half in (0, 1):
                            if j < self.nj:
                                self.dve_max(dve, self.nj * u + j, self.st[:, 12 + 4 * q:16 + 4 * q],
                                             self.st[:, q:q + 1], (2 * half, 2 * half + 1))
                            if j:
                                self.dve_turn(dve, self.nj * u + (j - 1), half)
                        if j:
                            q = (j - 1) % 2
                            dve.tensor_reduce(self.st[:, 2:3], self.st[:, 4 + 3 * q:7 + 3 * q], AX.X, ALU.add)
                            dve.drain()
                            dve.reciprocal(self.st[:, 20 + q:21 + q], self.st[:, 2:3])
                        if j >= 2:
                            self.dve_rows(dve, self.nj * u + (j - 2), j - 2)
                    dve.drain()
                    self.dve_rows(dve, self.nj * u + (self.nj - 1), self.nj - 1)
                    dve.drain().then_inc(self.o_rows, 1)
                    dve.wait_ge(self.oT_psum, u + 1)
                    dve.tensor_copy(self.oT[:, :, ds(b * S, S)], ps[:, 6, 0:K2 * S].rearrange("p (g q) -> p g q", g=K2))
                    dve.drain().then_inc(self.batch_done, 1)
                if self.biased:
                    for k in range(K2):
                        dve.tensor_scalar(self.oT[:, k, :], self.oT[:, k, :], col("bv3", k), None, ALU.add)
                dve.drain().then_inc(self.oT_final, 1)
                for t in range(T):
                    dve.wait_ge(self.y_ps, 4 * self.order + t + 1)
                    dve.tensor_tensor(x[:, t, :], bank(t, D), x[:, t, :], ALU.add)
                dve.drain().then_inc(stage_done, 1)

        class First(Flash):

            def __init__(self):
                super().__init__("x0", H0 // 2, [P] * FULL + [TAIL, S])
                name = "x0"
                (self.q_psum, self.q_ready, self.qp_psum, self.qp_ready, self.var, self.std, self.norm, self.turned,
                 self.xT_act, self.xT_dve, self.lat_psum, self.lat_ready, self.kv_ready, self.oh_psum, self.oh_ready,
                 self.y_ps, self.bcast, self.o_rows, self.u_psum, self.qp_copied) = (
                    sem(f"{name}_{n}") for n in ("q_psum", "q_ready", "qk_psum", "qk_ready", "var", "std", "norm",
                                                 "ctx_turned", "xT_by_act", "xT_by_dve", "latents_psum",
                                                 "latents_ready", "kv_ready", "heads_psum", "heads_ready", "y_psum", "affine_loaded",
                                                 "o_rows", "u_psum", "qk_copied"))
                (self.ctx, self.kv, self.xT, self.p0, self.p1, self.pT, self.oT, self.qp, self.gb, self.st,
                 self.qp_all) = carve((KT, D), (KT + 1, D), (K2, KEYS + S), (KEYS + S,), (KEYS + S,), (KT + 1, P),
                                      (H0, N), (K2, H0 * S), (2, D), (32,), (K2 * H0, N))
                self.qp_all = self.qp_all.rearrange("p (k h) n -> p k h n", k=K2)
                self.qT = self.oT
                self.u_all = self.qp_all
                self.o = hn[:, :, :]
                self.p = (self.p0, self.p1)
                self.wq = w1[0]
                self.wv = w1[1]
                self.wkT = w2[0]
                self.wo = w2[1]

            def sp(self, sp, ctx_rows):
                sp.dma_start(self.wq[:, :, :], A["Wq0"].rearrange("(k p) n -> p k n", p=P)).then_inc(x0_loaded, 16)
                sp.dma_start(self.wkT[:, :, :], A["Wk0T"].rearrange("(h p) n -> p h n", p=P)).then_inc(x0_loaded, 16)
                sp.dma_start(self.gb[:, 0, :], A["g_media_row"].to_broadcast([P, D])).then_inc(self.bcast, 16)
                sp.dma_start(self.gb[:, 1, :], A["b_media_row"].to_broadcast([P, D])).then_inc(self.bcast, 16)
                with sp.Fori(0, B) as b:
                    sp.wait_ge(self.kv_ready, b + 1)
                    sp.dma_start(self.ctx[:, 0:FULL, :],
                                 ctx_rows[b, 0:FULL * P, :].rearrange("(t p) d -> p t d", p=P)).then_inc(ctx_loaded, 16)
                    sp.dma_start(self.ctx[0:TAIL, FULL, :], ctx_rows[b, FULL * P:KEYS, :]).then_inc(ctx_loaded, 16)
                sp.dma_start(self.wv[:, :, :], A["Wv0"].rearrange("(k p) n -> p k n", p=P)).then_inc(x0_loaded, 16)
                sp.dma_start(self.wo[:, :, :], A["Wo0"].rearrange("(h p) n -> p h n", p=P)).then_inc(x0_loaded, 16)

            def pool(self, pool):
                pool.wait_ge(self.bcast, 32)
                with pool.Fori(0, B) as b:
                    pool.wait_ge(self.batch_done, b + 1)
                    pool.wait_ge(self.norm, b + 1)
                    for n, lo, hi in ((P, 0, FULL), (TAIL, FULL, KT)):
                        bc = lambda i: self.gb[0:n, i, :].unsqueeze(1).to_broadcast([n, hi - lo, D])
                        pool.tensor_tensor(self.kv[0:n, lo:hi, :], self.ctx[0:n, lo:hi, :], bc(0), ALU.mult)
                        pool.drain()
                        if n == TAIL:
                            pool.wait_ge(self.turned, 8 * b + 16)
                        pool.tensor_tensor(self.kv[0:n, lo:hi, :], self.kv[0:n, lo:hi, :], bc(1), ALU.add)
                    pool.drain().then_inc(self.kv_ready, 1)

            def pe(self, pe, s):
                pe.wait_ge(stage_done, s)
                pe.wait_ge(x0_loaded, 32)
                for h in range(H0):
                    for k in range(K2):
                        ins = pe.matmul(bank(h), self.wq[:, k, h * P:(h + 1) * P], hT[:, k, :], start=(k == 0),
                                        stop=(k == K2 - 1))
                ins.then_inc(self.q_psum, 1)
                pe.wait_ge(self.q_ready, 1)
                for f in range(K2):
                    for h in range(H0):
                        if f:
                            pe.wait_ge(self.qp_copied, h + 1)
                        pe.matmul(bank(h), self.wkT[:, h, f * P:(f + 1) * P], self.qT[:, h, :], start=True, stop=True)\
                            .then_inc(self.qp_psum, 1)
                pe.wait_ge(self.qp_copied, K2 * H0)
                with pe.Fori(0, B) as b:
                    pe.wait_ge(self.batch_done, b + 1)
                    pe.wait_ge(self.norm, b + 1)
                    for f in range(K2):
                        for c in range(4):
                            for i, kt in enumerate(self.turns[c][0:4 if c < 3 else 1]):
                                n = self.tiles[kt]
                                ins = pe.transpose(ps[:, 4 * f + c, i * P:i * P + n],
                                                   self.ctx[0:n, kt, f * P:(f + 1) * P], ident[0:n, 0:n])
                            ins.then_inc(self.turned, 1)
                    pe.wait_ge(self.xT_dve, 5 * b + 5)
                    pe.wait_ge(self.xT_act, 4 * b + 4)
                    for f in range(K2):
                        ins = pe.matmul(ps[0:S, 7, f * P:(f + 1) * P], self.xT[:, f, KEYS:KEYS + S], ident,
                                        start=True, stop=True)
                    ins.then_inc(self.lat_psum, 1)
                    pe.wait_ge(self.lat_ready, b + 1)
                    pe.wait_ge(self.qp_ready, b + 1)
                    for j in range(self.nj + 1):
                        if j < self.nj:
                            J = self.nj * b + j
                            for c, (a, w) in enumerate(self.chunks):
                                if c < 3:
                                    pe.wait_ge(self.exp_done, 3 * J + c + 1)
                                for k in range(K2):
                                    ins = pe.matmul(bank(c, w), self.qp[:, k, 2 * j * S:(2 * j + 2) * S],
                                                    self.xT[:, k, a:a + w], start=(k == 0), stop=(k == K2 - 1))
                                ins.then_inc(self.s_psum, 1)
                        if j:
                            J = self.nj * b + (j - 1)
                            self.pe_turn(pe, J, self.p[(j - 1) % 2])
                            if j == 1:
                                pe.wait_ge(self.kv_ready, b + 2)
                            pe.wait_ge(self.o_taken, J + 1)
                            for c, tiles in enumerate(self.turns):
                                self.pe_wait_turned(pe, J, c)
                                for kt in tiles:
                                    n = self.tiles[kt]
                                    ins = pe.matmul(bank(6 + (j - 1) % 2, D), self.pT[0:n, kt, :], self.kv[0:n, kt, :],
                                                    start=(kt == 0), stop=(kt == KT))
                            ins.then_inc(self.o_psum, 1)
                    pe.wait_ge(self.o_rows, b + 1)
                    for f in range(K2):
                        for j in range(self.nj):
                            ins = pe.transpose(ps[:, 4 + f, j * P:(j + 1) * P], self.o[:, j, f * P:(f + 1) * P], ident)
                    ins.then_inc(self.u_psum, 1)
                pe.wait_ge(self.batch_done, B + 1)
                pe.wait_ge(x0_loaded, 64)
                for h in range(H0):
                    for k in range(K2):
                        ins = pe.matmul(bank(h), self.wv[:, k, h * P:(h + 1) * P], self.u_all[:, k, h, :],
                                        start=(k == 0), stop=(k == K2 - 1))
                    ins.then_inc(self.oh_psum, 1)
                pe.wait_ge(self.oh_ready, 1)
                for t in range(T):
                    pe.matmul(bank(t, D), one_row, row("bo0"), start=True, stop=False)
                    for h in range(H0):
                        ins = pe.matmul(bank(t, D), self.oT[:, h, t * P:(t + 1) * P], self.wo[:, h, :], start=False,
                                        stop=(h == H0 - 1))
                    ins.then_inc(self.y_ps, 1)

            def act(self, act, s):
                act.wait_ge(stage_done, s)
                self.act_std(act, 0)
                for i in range(K2 * H0):
                    act.wait_ge(self.qp_psum, i + 1)
                    act.activation(self.qp_all[:, i // H0, i % H0, :], bank(i % H0), ACT.Copy).then_inc(self.qp_copied, 1)
                act.drain()
                with act.Fori(0, B - 1) as b:
                    self.act_batch(act, b, True)
                self.act_batch(act, B - 1, False)

            def act_std(self, act, b):
                act.wait_ge(self.var, b + 1)
                act.activation(ln_sd[:, :], ln_ve[:, :], ACT.Sqrt).then_inc(self.std, 1)

            def act_batch(self, act, b, more):
                act.activation(self.qp.rearrange("p k (h q) -> p k h q", h=H0), self.qp_all[:, :, :, ds(b * S, S)],
                               ACT.Copy).then_inc(self.qp_ready, 1)
                for c, (a, w) in enumerate(chunks):
                    act.wait_ge(self.turned, 8 * b + 8 + c + 1)
                    act.activation(self.xT[:, 0, a:a + w], bank(c, w), ACT.Identity, bias=col("b_media", 0),
                                   scale=col("g_media", 0)).then_inc(self.xT_act, 1)
                for j in range(self.nj + 1):
                    if j:
                        self.act_turn(act, self.nj * b + (j - 1), self.pT)
                    if j < self.nj:
                        q = j % 2
                        self.act_exp(act, self.nj * b + j, self.p[q], self.st[:, q:q + 1],
                                     self.st[:, 4 + 3 * q:7 + 3 * q])
                    if j == 1 and more:
                        self.act_std(act, b + 1)

            def dve(self, dve, s):
                dve.wait_ge(stage_done, s)
                self.dve_stats(dve, 0)
                dve.wait_ge(self.q_psum, 1)
                for h in range(H0):
                    dve.tensor_scalar(self.qT[:, h, :], bank(h), col("bq0", h), DH0 ** -0.5, ALU.add, ALU.mult)
                dve.drain().then_inc(self.q_ready, 1)
                self.dve_norm(dve, 0)
                with dve.Fori(0, B - 1) as b:
                    self.dve_batch(dve, b, True)
                self.dve_batch(dve, B - 1, False)
                for h in range(H0):
                    dve.wait_ge(self.oh_psum, h + 1)
                    dve.tensor_scalar(self.oT[:, h, :], bank(h), col("bv0", h), None, ALU.add)
                dve.drain().then_inc(self.oh_ready, 1)
                for t in range(T):
                    dve.wait_ge(self.y_ps, t + 1)
                    dve.tensor_tensor(x[:, t, :], bank(t, D), x[:, t, :], ALU.add)
                dve.drain().then_inc(stage_done, 1)

            def dve_stats(self, dve, b):
                dve.wait_ge(ctx_loaded, 32 * b + 32)
                for kt in range(KT):
                    n = self.tiles[kt]
                    dve.bn_stats(ln_st[0:n, kt, :], self.ctx[0:n, kt, :])
                dve.drain()
                for kt in range(KT):
                    n = self.tiles[kt]
                    dve.bn_aggr(ln_mv[0:n, kt, :], ln_st[0:n, kt, :])
                dve.drain()
                dve.tensor_scalar(ln_ve[:, :], ln_mv[:, :, 1], EPS, None, ALU.add).then_inc(self.var, 1)

            def dve_norm(self, dve, b):
                dve.wait_ge(self.std, b + 1)
                dve.reciprocal(ln_rs[:, :], ln_sd[:, :])
                dve.drain()
                for kt in range(KT):
                    n = self.tiles[kt]
                    dve.tensor_scalar(self.ctx[0:n, kt, :], self.ctx[0:n, kt, :], ln_mv[0:n, kt, 0:1],
                                      ln_rs[0:n, kt:kt + 1], ALU.subtract, ALU.mult)
                dve.drain().then_inc(self.norm, 1)

            def dve_batch(self, dve, b, more):
                dve.wait_ge(self.turned, 8 * b + 8 + 1)
                dve.tensor_copy(self.xT[:, :, KEYS:KEYS + S], hT[:, :, ds(b * S, S)]).then_inc(self.xT_dve, 1)
                for c, (a, w) in enumerate(chunks):
                    dve.wait_ge(self.turned, 8 * b + 8 + 4 + c + 1)
                    dve.tensor_scalar(self.xT[:, 1, a:a + w], bank(4 + c, w), col("g_media", 1), col("b_media", 1),
                                      ALU.mult, ALU.add).then_inc(self.xT_dve, 1)
                dve.wait_ge(self.lat_psum, b + 1)
                dve.tensor_copy(self.kv[0:S, KT, :], bank(7, D, S)).then_inc(self.lat_ready, 1)
                for j in range(self.nj + 1):
                    if j < self.nj:
                        q = j % 2
                        self.dve_max(dve, self.nj * b + j, self.st[:, 12 + 4 * q:16 + 4 * q], self.st[:, q:q + 1])
                    if j:
                        J, q = self.nj * b + (j - 1), (j - 1) % 2
                        self.dve_turn(dve, J, self.pT)
                        self.dve_sums(dve, J, self.st[:, 4 + 3 * q:7 + 3 * q], self.st[:, 2:3], self.st[:, 3:4])
                        dve.tensor_scalar(self.o[:, j - 1, :], bank(6 + q, D), self.st[:, 3:4], None, ALU.mult)\
                            .then_inc(self.o_taken, 1)
                    if j == 1 and more:
                        self.dve_stats(dve, b + 1)
                    if j == 2 and more:
                        self.dve_norm(dve, b + 1)
                dve.drain().then_inc(self.o_rows, 1)
                dve.wait_ge(self.u_psum, b + 1)
                dve.tensor_copy(self.u_all[:, :, :, ds(b * S, S)],
                                ps[:, 4:6, :].rearrange("p k (h q) -> p k h q", h=H0))
                dve.drain().then_inc(self.batch_done, 1)

        class Quat:

            def __init__(self):
                (self.pw_psum, self.pw_ready, self.qkv_psum, self.qkv_ready, self.diff_psum, self.diff_ready,
                 self.rolled, self.reduced, self.cos_ready, self.p3_ready, self.c_ready, self.cT_psum, self.cT_ready,
                 self.z_psum, self.z_ready, self.y_ps) = (
                    sem(f"quat_{n}") for n in ("pw_psum", "pw_ready", "qkv_psum", "qkv_ready", "diff_psum",
                                               "diff_ready", "rolled", "reduced", "cos_ready", "p3_ready",
                                               "c_ready", "cT_psum", "cT_ready", "z_psum", "z_ready", "y_psum"))
                TD = T * D
                (self.aw, self.pw, self.ab, self.pw2, self.q, self.k, self.v, self.red, self.pr, self.tmp,
                 self.ptmp) = carve((K2, 3 * D), (K2, D), (3 * D,), (K2, D), (4, TD), (4, TD), (4, TD), (3, TD),
                                    (4, TD), (TD,), (TD,))
                self.parts = (self.q, self.k, self.v)
                self.hid = self.red
                self.cT = self.q[:, 0, :].rearrange("p (k n) -> p k n", k=K2)
                self.zT = self.q[:, 1, :].rearrange("p (k n) -> p k n", k=K2)
                self.hidden = scratch[:, 3072:3072 + 8 * N].rearrange("p (a b) -> p a b", a=8)

            def sp(self, sp, s0):
                sp.wait_ge(stage_done, s0)
                with sp.Fori(0, LAYERS) as l:
                    sp.wait_ge(stage_done, 4 * l + (s0 - 2))
                    sp.dma_start(self.aw, A["attn_w"][l, :, :].rearrange("(k p) n -> p k n", p=P)).then_inc(lw_loaded, 16)
                    sp.dma_start(self.pw, A["aproj_w"][l, :, :].rearrange("(k p) n -> p k n", p=P)).then_inc(lw_loaded, 16)
                    sp.dma_start(self.ab, A["attn_b"][ds(l, 1), :].to_broadcast([P, 3 * D])).then_inc(lw_loaded, 16)
                    sp.wait_ge(y_psum, 4 * l + 4)
                    fc = A["fc_w"][l, :, :].rearrange("(k p) n -> p k n", p=P)
                    ffn_load(sp, 0, (w1[0][:, 0, :], fc[:, 0, :]), (w1[0][:, 1, :], fc[:, 1, :]),
                             (w2[0][:, :, :], A["mproj_w"][l, :, :].rearrange("(k p) n -> p k n", p=P)))

            def pe(self, pe, s, l):
                pe.wait_ge(stage_done, s)
                pe.wait_ge(lw_loaded, 48 * l + 48)
                basis = const("basis").rearrange("p (k n) -> p k n", k=K2)
                for m in range(K2):
                    for k in range(K2):
                        ins = pe.matmul(ps[:, 6, m * D:(m + 1) * D], basis[:, k, m * P:(m + 1) * P], self.pw[:, k, :],
                                        start=(k == 0), stop=(k == K2 - 1))
                ins.then_inc(self.pw_psum, 1)
                for t in range(T):
                    b0 = 2 * (t % 2)
                    if t >= 2:
                        pe.wait_ge(self.qkv_ready, 4 * l + t - 1)
                    for bk, a, w in ((b0, 0, CHUNK), (b0 + 1, CHUNK, 3 * D - CHUNK)):
                        for k in range(K2):
                            ins = pe.matmul(bank(bk, w), hT[:, k, t * P:(t + 1) * P], self.aw[:, k, a:a + w],
                                            start=(k == 0), stop=(k == K2 - 1))
                    ins.then_inc(self.qkv_psum, 1)
                pe.wait_ge(self.qkv_ready, 4 * l + 4)
                for i, part in enumerate(self.parts):
                    for t in range(T):
                        at = i * T + t
                        ins = pe.matmul(ps[:, at // 2, (at % 2) * D:(at % 2 + 1) * D], const("diff"),
                                        part[:, 0, t * D:(t + 1) * D], start=True, stop=True)
                    ins.then_inc(self.diff_psum, 1)
                pe.wait_ge(self.c_ready, l + 1)
                for k in range(K2):
                    for t in range(T):
                        ins = pe.transpose(ps[:, k, t * P:(t + 1) * P], self.pr[:, 0, t * D + k * P:t * D + (k + 1) * P],
                                           ident)
                ins.then_inc(self.cT_psum, 1)
                pe.wait_ge(self.cT_ready, l + 1)
                for m in range(K2):
                    for k in range(K2):
                        ins = pe.matmul(bank(2 + m), basis[:, k, m * P:(m + 1) * P], self.cT[:, k, :], start=(k == 0),
                                        stop=(k == K2 - 1))
                ins.then_inc(self.z_psum, 1)
                pe.wait_ge(self.z_ready, l + 1)
                pe.wait_ge(self.pw_ready, l + 1)
                pbias = rows[0:1, ds(l * D + row_at["aproj_b"][0], D)]
                for t in range(T):
                    pe.matmul(bank(4 + t, D), one_row, pbias, start=True, stop=False)
                    for k in range(K2):
                        ins = pe.matmul(bank(4 + t, D), self.zT[:, k, t * P:(t + 1) * P], self.pw2[:, k, :],
                                        start=False, stop=(k == K2 - 1))
                    ins.then_inc(self.y_ps, 1)

            def act(self, act, s, l):
                act.wait_ge(stage_done, s)
                act.wait_ge(self.pw_psum, l + 1)
                act.activation(self.pw2.rearrange("p k n -> p (k n)"), bank(6), ACT.Copy).then_inc(self.pw_ready, 1)
                act.wait_ge(self.qkv_ready, 4 * l + 4)
                for part in self.parts:
                    dst = part[:, 2, :].rearrange("p (t d) -> p t d", t=T)
                    src = part[:, 0, :].rearrange("p (t d) -> p t d", t=T)
                    act.activation(dst[:, :, HD:D], src[:, :, 0:D - HD], ACT.Copy)
                    act.activation(dst[:, :, 0:HD], src[:, :, D - HD:D], ACT.Copy)
                act.drain().then_inc(self.rolled, 1)
                for i, part in enumerate(self.parts):
                    act.wait_ge(self.diff_psum, 3 * l + i + 1)
                    act.activation(part[:, 1, :], ps[:, 2 * i:2 * i + 2, :].rearrange("p a b -> p (a b)"), ACT.Copy)\
                        .then_inc(self.diff_ready, 1)
                act.wait_ge(self.reduced, l + 1)
                act.activation(self.red, self.red, ACT.Abs)
                act.drain()
                for i, part in enumerate(self.parts):
                    act.activation(part[:, 3, :], self.red[:, i, :], ACT.Sin, bias=half_pi[:, :], scale=-1.0)\
                        .then_inc(self.cos_ready, 1)
                act.wait_ge(self.cT_psum, l + 1)
                act.activation(self.cT, ps[:, 0:2, :], ACT.Copy).then_inc(self.cT_ready, 1)

            def pool(self, pool, l):
                pool.wait_ge(self.rolled, l + 1)
                pool.wait_ge(self.diff_ready, 3 * l + 2)
                pool.wait_ge(self.cos_ready, 3 * l + 2)
                self.combine(pool, 3, self.ptmp)
                pool.drain().then_inc(self.p3_ready, 1)

            TERMS = {0: ((0, 0, 1), (1, 1, -1), (2, 2, -1), (3, 3, -1)),
                     1: ((0, 1, 1), (1, 0, 1), (2, 3, 1), (3, 2, -1)),
                     2: ((0, 2, 1), (1, 3, -1), (2, 0, 1), (3, 1, 1)),
                     3: ((0, 3, 1), (1, 2, 1), (2, 1, -1), (3, 0, 1))}

            def combine(self, eng, c, tmp):
                for n, (i, j, sign) in enumerate(self.TERMS[c]):
                    dst = self.pr[:, c, :] if n == 0 else tmp
                    eng.tensor_tensor(dst, self.q[:, i, :], self.k[:, j, :], ALU.mult)
                    eng.drain()
                    if n:
                        eng.tensor_tensor(self.pr[:, c, :], self.pr[:, c, :], tmp, ALU.add if sign > 0 else ALU.subtract)
                        eng.drain()

            def dve(self, dve, s, l):
                dve.wait_ge(stage_done, s)
                dve.wait_ge(lw_loaded, 48 * l + 48)
                qkv = scratch[:, self.q_at:self.q_at + 12 * T * D].rearrange("p (c j n) -> p c j n", c=3, j=4)
                bias = self.ab.rearrange("p (h c d) -> p c h d", c=3, d=HD)
                for t in range(T):
                    b0 = 2 * (t % 2)
                    dve.wait_ge(self.qkv_psum, 4 * l + t + 1)
                    src = ps[:, b0:b0 + 2, :].rearrange("p a b -> p (a b)")[:, 0:3 * D]\
                        .rearrange("p (h c d) -> p c h d", c=3, d=HD)
                    for c in range(3):
                        ins = dve.tensor_tensor(qkv[:, c, 0, t * D:(t + 1) * D].rearrange("p (h d) -> p h d", h=H),
                                                src[:, c, :, :], bias[:, c, :, :], ALU.add)
                    ins.then_inc(self.qkv_ready, 1)
                dve.drain()
                vals = qkv[:, :, 0, :]
                dve.tensor_scalar(self.red, vals, 1.0 / TWO_PI, ROUND, ALU.mult, ALU.add)
                dve.drain()
                dve.tensor_scalar(self.red, self.red, ROUND, -TWO_PI, ALU.subtract, ALU.mult)
                dve.drain()
                dve.tensor_tensor(self.red, self.red, vals, ALU.add).then_inc(self.reduced, 1)
                dve.wait_ge(self.diff_ready, 3 * l + 3)
                dve.wait_ge(self.rolled, l + 1)
                dve.wait_ge(self.cos_ready, 3 * l + 3)
                for c in range(3):
                    self.combine(dve, c, self.tmp)
                c0 = self.pr[:, 0, :]
                dve.tensor_tensor(c0, c0, self.v[:, 0, :], ALU.mult)
                for c in (1, 2, 3):
                    dve.drain()
                    if c == 3:
                        dve.wait_ge(self.p3_ready, l + 1)
                    dve.tensor_tensor(self.tmp, self.pr[:, c, :], self.v[:, c, :], ALU.mult)
                    dve.drain()
                    dve.tensor_tensor(c0, c0, self.tmp, ALU.subtract)
                dve.drain().then_inc(self.c_ready, 1)
                dve.wait_ge(self.z_psum, l + 1)
                spectrum = const("spectrum").rearrange("p (k s) -> p k s", k=K2)
                for m in range(K2):
                    dve.tensor_tensor(self.zT[:, m, :].rearrange("p (b s) -> p b s", b=B),
                                      ps[:, 2 + m, :].rearrange("p (b s) -> p b s", b=B),
                                      spectrum[:, m, :].unsqueeze(1).to_broadcast([P, B, S]), ALU.mult)
                dve.drain().then_inc(self.z_ready, 1)
                for t in range(T):
                    dve.wait_ge(self.y_ps, 4 * l + t + 1)
                    dve.tensor_tensor(x0[:, t, :], bank(4 + t, D), x0[:, t, :], ALU.add)
                dve.drain().then_inc(stage_done, 1)

        half_pi = sb("half_pi", [P, 1])

        class Scan:
            NS = 64

            def __init__(self):
                (self.loaded, self.z_psum, self.l_ready, self.d_ready, self.decay_ready, self.hs_ready, self.y_ps,
                 self.hid_next, self.out_psum, self.asp) = (
                    sem(f"scan_{n}") for n in ("loaded", "z_psum", "log_ready", "delta_ready", "decay_ready",
                                               "states_ready", "y_psum", "hidden_ready", "out_psum", "a_log_ready"))
                (self.win, self.wout, self.small, self.z, self.az, self.delta, self.decay, self.drive, self.hs,
                 self.cs, self.hid, self.sa) = carve((4 * K2, self.NS), (4, D), (6,), (N,), (N,), (N,), (N,), (N,),
                                                     (N,), (K2, B), (K2, N), (8,))

            def sp(self, sp, s):
                sp.wait_ge(stage_done, s)
                for l in range(2):
                    for i, name in enumerate(("Wd", "Wi")):
                        a = (2 * l + i) * K2
                        sp.dma_start(self.win[:, a:a + K2, :], A[name][l, :, :].rearrange("(k p) n -> p k n", p=P))\
                            .then_inc(self.loaded, 16)
                    for i, name in enumerate(("Wos", "Wss")):
                        sp.dma_start(self.wout[0:self.NS, 2 * l + i, :], A[name][l, :, :]).then_inc(self.loaded, 16)
                sp.dma_start(self.small[0:self.NS, :], A["scan_small"]).then_inc(self.loaded, 16)

            def pe(self, pe, s):
                ns = self.NS
                pe.wait_ge(stage_done, s)
                pe.wait_ge(self.loaded, 16 * 9)
                for l in range(2):
                    src = hT if l == 0 else self.hid
                    if l:
                        pe.wait_ge(self.hid_next, 1)
                    for i in range(2):
                        for k in range(K2):
                            ins = pe.matmul(bank(i, N, ns), self.win[:, (2 * l + i) * K2 + k, :], src[:, k, :],
                                            start=(k == 0), stop=(k == K2 - 1))
                    ins.then_inc(self.z_psum, 1)
                    pe.wait_ge(self.hs_ready, l + 1)
                    last = self.hs[0:ns, :].rearrange("p (b s) -> p b s", b=B)[:, :, S - 1]
                    for m in range(K2):
                        pe.matmul(bank(2 + m), self.wout[0:ns, 2 * l, m * P:(m + 1) * P], self.hs[0:ns, :],
                                  start=True, stop=True)
                        ins = pe.matmul(bank(4 + m, B), self.wout[0:ns, 2 * l + 1, m * P:(m + 1) * P], last,
                                        start=True, stop=True)
                    ins.then_inc(self.y_ps, 1)
                pe.wait_ge(self.hid_next, 2)
                for t in range(T):
                    for k in range(K2):
                        ins = pe.transpose(ps[:, t // 2, (t % 2) * D + k * P:(t % 2) * D + (k + 1) * P],
                                           self.hid[:, k, t * P:(t + 1) * P], ident)
                ins.then_inc(self.out_psum, 1)

            def act(self, act, s):
                ns = self.NS
                act.wait_ge(stage_done, s)
                act.wait_ge(self.loaded, 16 * 9)
                al = self.small[0:ns, 4:6]
                ab, ex, lg = (self.sa[0:ns, i:i + 2] for i in (0, 2, 4))
                act.activation(ab, al, ACT.Abs)
                act.drain()
                act.activation(ex, ab, ACT.Exp, scale=-1.0)
                act.drain()
                act.activation(lg, ex, ACT.Ln, bias=ones[0:ns, 0:1]).then_inc(self.asp, 1)
                for l in range(2):
                    act.wait_ge(self.z_psum, l + 1)
                    act.activation(self.z[0:ns, :], bank(0, N, ns), ACT.Identity, bias=self.small[0:ns, l:l + 1])
                    act.drain()
                    act.activation(self.az[0:ns, :], self.z[0:ns, :], ACT.Abs)
                    act.drain()
                    act.activation(self.az[0:ns, :], self.az[0:ns, :], ACT.Exp, scale=-1.0)
                    act.drain()
                    act.activation(self.az[0:ns, :], self.az[0:ns, :], ACT.Ln, bias=ones[0:ns, 0:1])\
                        .then_inc(self.l_ready, 1)
                    act.wait_ge(self.d_ready, l + 1)
                    act.activation(self.decay[0:ns, :], self.delta[0:ns, :], ACT.Exp, scale=self.sa[0:ns, 6 + l:7 + l])\
                        .then_inc(self.decay_ready, 1)

            def dve(self, dve, s):
                ns = self.NS
                dve.wait_ge(stage_done, s)
                dve.wait_ge(self.asp, 1)
                sp_a = self.sa[0:ns, 6:8]
                dve.scalar_tensor_tensor(out=sp_a, in0=self.small[0:ns, 4:6], scalar=0.0, in1=self.sa[0:ns, 4:6],
                                         op0=ALU.max, op1=ALU.add)
                dve.drain()
                dve.tensor_scalar(sp_a, sp_a, -1.0, None, ALU.mult)
                for l in range(2):
                    dve.drain()
                    dve.wait_ge(self.l_ready, l + 1)
                    dve.scalar_tensor_tensor(out=self.delta[0:ns, :], in0=self.z[0:ns, :], scalar=0.0,
                                             in1=self.az[0:ns, :], op0=ALU.max, op1=ALU.add)
                    dve.drain().then_inc(self.d_ready, 1)
                    dve.scalar_tensor_tensor(out=self.drive[0:ns, :], in0=bank(1, N, ns),
                                             scalar=self.small[0:ns, 2 + l:3 + l], in1=self.delta[0:ns, :],
                                             op0=ALU.add, op1=ALU.mult)
                    dve.wait_ge(self.decay_ready, l + 1)
                    dve.memset(self.decay[0:ns, :].rearrange("p (b s) -> p b s", b=B)[:, :, 0], 0.0)
                    dve.drain()
                    dve.tensor_tensor_scan(self.hs[0:ns, :], self.decay[0:ns, :], self.drive[0:ns, :], 0.0,
                                           ALU.mult, ALU.add).then_inc(self.hs_ready, 1)
                    dve.wait_ge(self.y_ps, l + 1)
                    for m in range(K2):
                        dve.tensor_scalar(self.cs[:, m, :], bank(4 + m, B), col("bs_scan", 2 * l + m),
                                          col("bo_scan", 2 * l + m), ALU.add, ALU.add)
                    dve.drain()
                    for m in range(K2):
                        dve.tensor_tensor(self.hid[:, m, :].rearrange("p (b s) -> p b s", b=B),
                                          ps[:, 2 + m, :].rearrange("p (b s) -> p b s", b=B),
                                          self.cs[:, m, :].unsqueeze(2).to_broadcast([P, B, S]), ALU.add)
                    dve.drain().then_inc(self.hid_next, 1)
                dve.wait_ge(self.out_psum, 1)
                dve.tensor_tensor(x[:, :, :].rearrange("p t d -> p (t d)"), ps[:, 0:2, :].rearrange("p a b -> p (a b)"),
                                  x[:, :, :].rearrange("p t d -> p (t d)"), ALU.add)
                dve.drain().then_inc(stage_done, 1)

        first = First()
        quat = Quat()
        quat.q_at = 2 * K2 * 0 + (K2 * 3 * D + K2 * D + 3 * D + K2 * D)
        moe0 = Moe("moe0", 9, 2, ACT.Silu, True, 0, "gate_b", "top2", "sw_b1", b2_l0, 5, 32, 0, (4, 0))
        moe1 = Moe("moe1", 8, 4, ACT.Silu, True, 1, None, "renormalised", None, None, 14, 50, 18, (9, 4))
        moe2 = Moe("moe2", 8, 8, ACT.Gelu_apprx_tanh, False, 2, "switch_b", "top1", "l2_b1", b2_l2, 22, 82, 50,
                   (13, 8))
        moe3 = Moe("moe3", 9, 8, ACT.Gelu, False, 3, "router_b", "capacity", "l3_b1", b2_l3, 30, 146, 50, (17, 12))
        cross1 = Local(0, 0, 1, HD ** -0.5, "causal", None, extra_mask=True)
        self1 = Local(1, 1, 1, HD ** -0.5, "same_batch", hT, grouped=True)
        cross2 = Cross(0, 0, 2, B, False)
        self2 = Local(2, 1, 2, D ** -0.5, "same_batch", hT, bo="bff2")
        cross3 = Cross(1, 0, 3, 2 * B, True)
        scan = Scan()

        (LN_A, LN_B, FIRST, LN_C, QUAT) = range(5)
        QUAT_END = QUAT + 4 * LAYERS
        (LN_D, MOE0, LN_E, CROSS1, LN_F, SELF1, LN_G, MOE1, LN_H, CROSS2, LN_I, SELF2, LN_J, MOE2, LN_K, CROSS3,
         LN_L, SCAN, LN_M, MOE3, END) = range(QUAT_END + 1, QUAT_END + 22)
        NL = 3 + 2 * LAYERS

        LAST = A["last"]
        block = ctx.enter_context(nc.Block())

        @block.sync
        def _(sp):
            sp.dma_start(x[:, :, :], A["x"].rearrange("(t p) d -> p t d", p=P)).then_inc(inputs_loaded, 16)
            sp.dma_start(cols[:, :], A["cols"]).then_inc(inputs_loaded, 16)
            sp.dma_start(consts[:, :], A["consts"]).then_inc(inputs_loaded, 16)
            sp.dma_start(rows[:, :], A["rows"]).then_inc(inputs_loaded, 16)
            sp.dma_start(b2_l0[:, :], A["b2_l0"]).then_inc(inputs_loaded, 16)
            sp.dma_start(b2_l2[:, :], A["b2_l2"]).then_inc(inputs_loaded, 16)
            sp.dma_start(b2_l3[:, :], A["b2_l3"]).then_inc(inputs_loaded, 16)
            sp.dma_start(routers[:, :, :, :], A["routers"].rearrange("r (k p) e -> p r k e", p=P))\
                .then_inc(inputs_loaded, 16)

            def attention_weights(slot, names):
                for i, name in enumerate(names):
                    dst = wp[slot][:, i, :, :]
                    sp.dma_start(dst, A[name].rearrange("(k p) n -> p k n", p=P)).then_inc(wp_loaded[slot], 16)

            if LAST >= 1:
                first.sp(sp, A["ctx"])
            if LAST >= 4:
                attention_weights(0, ("Wq1", "Wk1", "Wv1", "Wo1"))
            if LAST >= 5:
                attention_weights(1, ("Wqa", "Wqa", "Wqa", "Woa"))
            if LAST >= 2:
                quat.sp(sp, QUAT)

            def shared_then_routed(e, par):
                w = A["w1_l0"][e, :, :].rearrange("(k p) n -> p k n", p=P)
                return ((w1[par][:, 0, 0:512], w[:, 0, :]), (w1[par][:, 1, 0:512], w[:, 1, :]),
                        (w2[par][:, 0:2, :], A["w2_l0"][e, :, :].rearrange("(k p) n -> p k n", p=P)))

            def gate_up_down(e, par):
                return ((w1[par][:, :, 0:512], A["gate_l1"][e, :, :].rearrange("(k p) n -> p k n", p=P)),
                        (w1[par][:, :, 512:1024], A["up_l1"][e, :, :].rearrange("(k p) n -> p k n", p=P)),
                        (w2[par][:, 0:4, :], A["down_l1"][e, :, :].rearrange("(k p) n -> p k n", p=P)))

            def wide(a, b):
                def sources(e, par):
                    w = A[a][e, :, :].rearrange("(k p) n -> p k n", p=P)
                    return ((w1[par][:, 0, :], w[:, 0, :]), (w1[par][:, 1, :], w[:, 1, :]),
                            (w2[par][:, :, :], A[b][e, :, :].rearrange("(k p) n -> p k n", p=P)))
                return sources

            if LAST >= 3:
                moe0.sp(sp, shared_then_routed)
            if LAST >= 4:
                sp.wait_ge(stage_done, CROSS1)
                sp.dma_start(cross1.keysT, A["ctx64"].rearrange("(t p) d -> p t d", p=P)).then_inc(latent_keys_loaded, 16)
                sp.dma_start(cross1.keyraw[0:1, :].bitcast(I32), A["mask64"]).then_inc(latent_keys_loaded, 16)
            if LAST >= 5:
                sp.wait_ge(stage_done, SELF1)
                sp.dma_start(self1.raw[:, :, 0:64], A["Wka"].rearrange("(k p) n -> p k n", p=P)).then_inc(kvraw_loaded, 16)
                sp.dma_start(self1.kraw[:, :, 0:64], A["Wva"].rearrange("(k p) n -> p k n", p=P)).then_inc(kvraw_loaded, 16)
            if LAST >= 7:
                attention_weights(0, ("Wq2", "Wq2", "Wq2", "Wo2"))
            if LAST >= 6:
                sp.wait_ge(stage_done, LN_G)
                if LAST >= 8:
                    attention_weights(1, ("Wqb", "Wkb", "Wvb", "Wff"))
                moe1.sp(sp, gate_up_down)
            if LAST >= 7:
                cross2.sp(sp, CROSS2, A["ctx"])
            if LAST >= 9:
                moe2.sp(sp, wide("w1_l2", "w2_l2"))
            if LAST >= 10:
                attention_weights(0, ("Wq3", "Wk3", "Wv3", "Wo3"))
                cross3.sp(sp, CROSS3, A["ctx"])
            if LAST >= 11:
                scan.sp(sp, SCAN)
            if LAST >= 12:
                moe3.sp(sp, wide("w1_l3", "w2_l3"))
            final = {0: LN_A, 1: LN_C, 2: LN_D, 3: LN_E, 4: LN_F, 5: LN_G, 6: LN_H, 7: LN_I, 8: LN_J, 9: LN_K,
                     10: LN_L, 11: LN_M, 12: END}[LAST]
            sp.wait_ge(stage_done, final)
            sp.dma_start(out.rearrange("(t p) d -> p t d", p=P), x[:, :, :]).then_inc(stored, 16)
            sp.wait_ge(stored, 16)

        @block.gpsimd
        def _(pool):
            pool.drain().then_inc(first.kv_ready, 1)
            pool.memset(ones[:, :], 1.0)
            pool.memset(half_pi[:, :], float(np.pi / 2))
            pool.memset(ln_mv[:, :, :], 0.0)
            pool.drain().then_inc(ones_ready, 1)
            if LAST >= 1:
                first.pool(pool)
            if LAST >= 2:
                with pool.Fori(0, LAYERS) as l:
                    quat.pool(pool, l)
            if LAST >= 7:
                cross2.pool(pool, CROSS2)
            if LAST >= 10:
                cross3.pool(pool, CROSS3)

        @block.tensor
        def _(pe):
            pe.drain().then_inc(first.turned, 8)
            pe.drain().then_inc(cross2.turned, 8)
            pe.drain().then_inc(y_psum, 4)
            pe.wait_ge(inputs_loaded, 128)
            pe.wait_ge(ones_ready, 1)
            ln = lambda s, n: ln_pe(pe, s, n, hn)
            if LAST >= 1:
                ln(LN_A, 0)
                ln(LN_B, 1)
                first.pe(pe, FIRST)
            if LAST >= 2:
                ln(LN_C, 2)
                with pe.Fori(0, LAYERS) as l:
                    s = 4 * l + (QUAT + 1)
                    ln(s - 1 + 0 + 0, 2 * l + 3)
                    quat.pe(pe, 4 * l + (QUAT + 1), l)
                    ln(4 * l + (QUAT + 2), 2 * l + 4)
                    pe.wait_ge(stage_done, 4 * l + (QUAT + 3))
                    ffn_pe(pe, 0, l + 1, l + 1, 8 * l, 8, False, False, quat.hidden,
                           rows[0:1, ds(l * D + row_at["mproj_b"][0], D)])
            tail = ((3, LN_D, MOE0, moe0), (4, LN_E, CROSS1, cross1), (5, LN_F, SELF1, self1), (6, LN_G, MOE1, moe1),
                    (7, LN_H, CROSS2, cross2), (8, LN_I, SELF2, self2), (9, LN_J, MOE2, moe2),
                    (10, LN_K, CROSS3, cross3), (11, LN_L, SCAN, scan), (12, LN_M, MOE3, moe3))
            for i, (at, norm_at, stage_at, stage) in enumerate(tail):
                if LAST >= at:
                    ln(norm_at, NL + i)
                    stage.pe(pe, stage_at)

        @block.scalar
        def _(act):
            act.drain().then_inc(first.exp_done, 3)
            act.drain().then_inc(cross2.exp_done, 3)
            act.wait_ge(inputs_loaded, 128)
            act.wait_ge(ones_ready, 1)
            if LAST >= 1:
                ln_act(act, LN_A, 0)
                ln_act(act, LN_B, 1, lambda k: col("g_lat", k), lambda k: col("b_lat", k))
                first.act(act, FIRST)
            if LAST >= 2:
                ln_act(act, LN_C, 2)
                with act.Fori(0, LAYERS) as l:
                    ln_act(act, 4 * l + QUAT, 2 * l + 3, lambda k: dcol("ln1_w", l * 2 + k),
                           lambda k: dcol("ln1_b", l * 2 + k))
                    quat.act(act, 4 * l + (QUAT + 1), l)
                    ln_act(act, 4 * l + (QUAT + 2), 2 * l + 4, lambda k: dcol("ln2_w", l * 2 + k),
                           lambda k: dcol("ln2_b", l * 2 + k))
                    act.wait_ge(stage_done, 4 * l + (QUAT + 3))
                    ffn_act(act, l + 1, 8 * l, 8, ACT.Gelu, lambda j: dcol("fc_b", l * 8 + j), False, quat.hidden)
            tail = ((3, LN_D, MOE0, moe0), (4, LN_E, CROSS1, cross1), (5, LN_F, SELF1, self1), (6, LN_G, MOE1, moe1),
                    (7, LN_H, CROSS2, cross2), (8, LN_I, SELF2, self2), (9, LN_J, MOE2, moe2),
                    (10, LN_K, CROSS3, cross3), (11, LN_L, SCAN, scan), (12, LN_M, MOE3, moe3))
            for i, (at, norm_at, stage_at, stage) in enumerate(tail):
                if LAST >= at:
                    ln_act(act, norm_at, NL + i)
                    stage.act(act, stage_at)

        @block.vector
        def _(dve):
            for primed in (first.batch_done, cross2.batch_done, cross1.added):
                dve.drain().then_inc(primed, 1)
            for primed in (first.o_taken, cross2.o_taken):
                dve.drain().then_inc(primed, 2)
            dve.drain().then_inc(y_used, 4)
            dve.wait_ge(inputs_loaded, 128)
            dve.wait_ge(ones_ready, 1)
            if LAST >= 1:
                ln_dve(dve, LN_A, 0, x, hn)
                ln_dve(dve, LN_B, 1, hn, hn)
                first.dve(dve, FIRST)
            if LAST >= 2:
                ln_dve(dve, LN_C, 2, x, hn)
                dve.wait_ge(stage_done, QUAT)
                dve.tensor_copy(x0[:, :, :], hn[:, :, :])
                dve.drain()
                with dve.Fori(0, LAYERS) as l:
                    ln_dve(dve, 4 * l + QUAT, 2 * l + 3, x0, hn)
                    quat.dve(dve, 4 * l + (QUAT + 1), l)
                    ln_dve(dve, 4 * l + (QUAT + 2), 2 * l + 4, x0, hn)
                    dve.wait_ge(stage_done, 4 * l + (QUAT + 3))
                    ffn_dve(dve, l + 1, 8 * l, 0, 8, None, x0, quat.hidden)
                    dve.drain().then_inc(stage_done, 1)
                dve.tensor_tensor(x[:, :, :], x[:, :, :], x0[:, :, :], ALU.add)
                dve.drain().then_inc(stage_done, 1)
            tail = ((3, LN_D, MOE0, moe0), (4, LN_E, CROSS1, cross1), (5, LN_F, SELF1, self1), (6, LN_G, MOE1, moe1),
                    (7, LN_H, CROSS2, cross2), (8, LN_I, SELF2, self2), (9, LN_J, MOE2, moe2),
                    (10, LN_K, CROSS3, cross3), (11, LN_L, SCAN, scan), (12, LN_M, MOE3, moe3))
            for i, (at, norm_at, stage_at, stage) in enumerate(tail):
                if LAST >= at:
                    ln_dve(dve, norm_at, NL + i, x, hn)
                    stage.dve(dve, stage_at)


def shape_constants():
    p = np.arange(P)
    same = (p[:, None] // S) == (p[None, :] // S)
    c = {"ident": np.eye(P), "same_batch": np.where(same, 0.0, BLOCKED),
         "causal": np.where(same & (p[None, :] <= p[:, None]), 0.0, BLOCKED)}
    diff = np.eye(P) - np.eye(P, k=1)
    diff[:, p % S == 0] = 0.0
    c["diff"] = diff
    c["head_of"] = (p[:, None] // HD == np.arange(HG)[None, :])
    c["first_of"] = np.tile(np.arange(E, 0, -1), (P, 1))
    k = np.arange(D)
    angle = 2 * np.pi * (np.outer(k // HD, k // HD) / H + np.outer(k % HD, k % HD) / HD)
    c["basis"] = ((np.cos(angle) + np.sin(angle)) / np.sqrt(H * HD)).reshape(K2, P, D).transpose(1, 0, 2).reshape(P, -1)
    ks, kh, kd = np.fft.fftfreq(S), np.fft.fftfreq(H), np.fft.fftfreq(HD)
    km = np.sqrt(ks[None, :] ** 2 + kh[k // HD][:, None] ** 2 + kd[k % HD][:, None] ** 2 + 1e-10)
    lam, t = np.arange(S) / S, np.arange(S) * 0.1
    gain = 1.0 + 0.1 * np.sin(t + lam) * np.cos(t - 2.0 * lam + 0.5 * lam ** 2)
    c["spectrum"] = (np.cos(np.arctan(np.log(km + 1e-10))) * gain).reshape(K2, P, S).transpose(1, 0, 2).reshape(P, -1)
    split = np.zeros((P, E + 1))
    split[:E, :E] = np.eye(E)
    split[:E, E] = -1.0
    c["split9"] = split
    c["own_half"] = (p[:, None] // S == np.arange(2 * HD)[None, :] // HD)
    c["stack"] = (p[:, None] % (2 * HD) == np.arange(2 * HD)[None, :]) & (p[:, None] < 4 * HD)
    c["fold"] = (p[:, None] % S == np.arange(S)[None, :])
    c["rest9"] = (p == E).astype(float)[:, None]
    return np.ascontiguousarray(np.concatenate([c[n].astype(np.float32).reshape(P, w) for n, w in CONSTS.items()], 1))


def kernel(**inputs):
    import concourse.bacc as bacc
    from concourse.bass_utils import run_bass_kernel_spmd as run

    I = {k: np.asarray(v) for k, v in inputs.items()}

    def down(v):
        return v.reshape(-1, P).T

    c = {"g_media": I["L0_xattn_gamma_media"], "b_media": I["L0_xattn_beta_media"], "g_lat": I["L0_xattn_gamma_lat"],
         "b_lat": I["L0_xattn_beta_lat"], "bq0": I["L0_xattn_bq"], "bv0": I["L0_xattn_bkv"][H0 * DH0:],
         "ln1_w": I["L0_attn_ln1_w"], "ln1_b": I["L0_attn_ln1_b"], "ln2_w": I["L0_attn_ln2_w"],
         "ln2_b": I["L0_attn_ln2_b"], "fc_b": I["L0_attn_fc_b"],
         "sw_b1": np.concatenate([I["L0_ffn_sb1"], I["L0_ffn_rb1"]], 0), "l2_b1": I["L2_ffn_b1"],
         "l3_b1": np.concatenate([I["L3_ffn_b1"], I["L3_ffn_sb1"][None]], 0),
         "bq3": I["L3_xattn_bq"], "bk3": I["L3_xattn_bk"], "bv3": I["L3_xattn_bv"],
         "bo_scan": I["L3_attn_bo"], "bs_scan": I["L3_attn_bs"]}
    r = {"bo0": I["L0_xattn_bo"], "aproj_b": I["L0_attn_aproj_b"], "mproj_b": I["L0_attn_mproj_b"],
         "gate_b": I["L0_ffn_gate_b"], "switch_b": I["L2_ffn_switch_b"], "router_b": I["L3_ffn_rb"],
         "bff2": I["L2_attn_bff"], "bo3": I["L3_xattn_bo"]}
    inner = H0 * DH0
    arrays = {
        "x": I["x"].reshape(N, D), "ctx": I["ctx_1024"], "ctx64": I["ctx_1024"][:, :S].reshape(N, D),
        "mask64": I["mask_BxS2_if1"][:, :S].reshape(1, N),
        "cols": np.concatenate([down(c[n]) for n in COLS], 1), "consts": shape_constants(),
        "rows": np.concatenate([r[n].reshape(1, -1) for n in ROWS], 1),
        "b2_l0": np.concatenate([I["L0_ffn_sb2"], I["L0_ffn_rb2"]], 0), "b2_l2": I["L2_ffn_b2"],
        "b2_l3": np.concatenate([I["L3_ffn_b2"], I["L3_ffn_sb2"][None]], 0),
        "routers": np.stack([I["L0_ffn_gate_w"], I["L1_ffn_router_kernel_DE"], I["L2_ffn_switch_w"],
                             I["L3_ffn_rw"].T], 0),
        "Wq0": I["L0_xattn_Wq"], "Wk0T": I["L0_xattn_Wkv"][:, :inner].T, "Wv0": I["L0_xattn_Wkv"][:, inner:],
        "Wo0": I["L0_xattn_Wo"], "g_media_row": I["L0_xattn_gamma_media"][None],
        "b_media_row": I["L0_xattn_beta_media"][None],
        "attn_w": I["L0_attn_attn_w"], "attn_b": I["L0_attn_attn_b"], "aproj_w": I["L0_attn_aproj_w"],
        "fc_w": I["L0_attn_fc_w"], "mproj_w": I["L0_attn_mproj_w"],
        "w1_l0": np.concatenate([I["L0_ffn_sw1"], I["L0_ffn_rw1"]], 0),
        "w2_l0": np.concatenate([I["L0_ffn_sw2"], I["L0_ffn_rw2"]], 0),
        "Wq1": I["L1_xattn_Wq"], "Wk1": I["L1_xattn_Wk"], "Wv1": I["L1_xattn_Wv"], "Wo1": I["L1_xattn_Wo"],
        "Wqa": I["L1_attn_Wq"], "Wka": I["L1_attn_Wk"], "Wva": I["L1_attn_Wv"], "Woa": I["L1_attn_Wo"],
        "gate_l1": I["L1_ffn_kernel_gating_EDF"], "up_l1": I["L1_ffn_kernel_up_EDF"],
        "down_l1": I["L1_ffn_kernel_down_EFD"],
        "Wq2": I["L2_xattn_Wq"].T, "Wo2": I["L2_xattn_Wo"].T,
        "Wqb": I["L2_attn_Wq"].T, "Wkb": I["L2_attn_Wk"].T, "Wvb": I["L2_attn_Wv"].T, "Wff": I["L2_attn_Wff"].T,
        "w1_l2": I["L2_ffn_w1"], "w2_l2": I["L2_ffn_w2"],
        "Wq3": I["L3_xattn_Wq"].T, "Wk3": I["L3_xattn_Wk"].T, "Wv3": I["L3_xattn_Wv"].T, "Wo3": I["L3_xattn_Wo"].T,
        "Wd": I["L3_attn_Wd"], "Wi": I["L3_attn_Wi"], "Wos": I["L3_attn_Wo"], "Wss": I["L3_attn_Ws"],
        "scan_small": np.concatenate([I["L3_attn_bd"].T, I["L3_attn_bi"].T, I["L3_attn_A_log"].T], 1),
        "w1_l3": np.concatenate([I["L3_ffn_w1"], I["L3_ffn_sw1"][None]], 0),
        "w2_l3": np.concatenate([I["L3_ffn_w2"], I["L3_ffn_sw2"][None]], 0),
    }
    nc = bacc.Bacc("TRN2", target_bir_lowering=False, num_devices=1)
    feed, A = {}, {"last": LAST_SUBLAYER}
    for name, a in arrays.items():
        a = np.ascontiguousarray(a)
        feed["in_" + name] = a
        A[name] = nc.dram_tensor("in_" + name, a.shape, mybir.dt.from_np(a.dtype), kind="ExternalInput").ap()
    out = nc.dram_tensor("out", (N, D), F32, kind="ExternalOutput").ap()
    program(nc, A, out)
    got = run(nc, [feed], core_ids=[0])
    return got.results[0]["out"].reshape(B, S, D)


LAST_SUBLAYER = 12
```

```python
from contextlib import ExitStack

import numpy as np

import concourse.bass as bass
from concourse import mybir

F32 = mybir.dt.float32
F32R = mybir.dt.float32r
I32 = mybir.dt.int32
ALU = mybir.AluOpType
ACT = mybir.ActivationFunctionType
AX = mybir.AxisListType
ds = bass.ds

P = 128
B, S, D = 8, 64, 256
N = B * S
T = N // P
K2 = D // P
KEYS = 1601
FULL = KEYS // P
TAIL = KEYS - FULL * P
KT = FULL + 1
H0, DH0 = 8, 128
H = 16
HD = D // H
HG = P // HD
E = 8
LAYERS = 4
CAP = N // E
BLOCKED = -1e30
EPS = 1e-5
TWO_PI = float(2 * np.pi)
ROUND = 1.5 * 2 ** 23
CHUNK = 512

COLS = dict(g_media=2, b_media=2, g_lat=2, b_lat=2, bq0=8, bv0=8,
            ln1_w=8, ln1_b=8, ln2_w=8, ln2_b=8, fc_b=32,
            sw_b1=36, l2_b1=64, l3_b1=72, bq3=2, bk3=2, bv3=2, bo_scan=4, bs_scan=4)
CONSTS = dict(ident=P, same_batch=P, causal=P, diff=P, head_of=HG, first_of=E, spectrum=2 * S, basis=2 * D,
              split9=E + 1, rest9=1, own_half=2 * HD, fold=S, stack=2 * HD)
ROWS = dict(bo0=D, aproj_b=LAYERS * D, mproj_b=LAYERS * D, gate_b=E, switch_b=E, router_b=E, bff2=D, bo3=D)


def offsets(widths):
    at, out = 0, {}
    for name, w in widths.items():
        out[name] = (at, w)
        at += w
    return out, at


def program(nc, A, out):
    with ExitStack() as ctx:
        def sb(name, shape, dt=F32):
            return ctx.enter_context(nc.sbuf_tensor(name, shape, dt))

        def sem(name):
            return ctx.enter_context(nc.semaphore(name))

        col_at, ncol = offsets(COLS)
        const_at, nconst = offsets(CONSTS)
        row_at, nrow = offsets(ROWS)

        x = sb("x", [P, T, D])
        x0 = sb("x0", [P, T, D])
        hn = sb("hn", [P, T, D])
        hT = sb("hT", [P, K2, N])
        cols = sb("cols", [P, ncol])
        consts = sb("consts", [P, nconst])
        rows = sb("rows", [1, nrow])
        b2_l0 = sb("b2_l0", [E + 1, D])
        b2_l2 = sb("b2_l2", [E, D])
        b2_l3 = sb("b2_l3", [E + 1, D])
        routers = sb("routers", [P, 4, K2, E])
        ones = sb("ones", [P, P])
        ln_st = sb("ln_st", [P, KT, 6])
        ln_mv = sb("ln_mv", [P, KT, 2])
        ln_ve = sb("ln_ve", [P, KT])
        ln_sd = sb("ln_sd", [P, KT])
        ln_rs = sb("ln_rs", [P, KT])
        w1 = [sb(f"w1_{i}", [P, K2, 1024]) for i in range(2)]
        w2 = [sb(f"w2_{i}", [P, 8, D]) for i in range(2)]
        wp = [sb(f"wp_{i}", [P, 4, K2, D]) for i in range(2)]
        SCRATCH = 30700
        scratch_at = nc.sbuf_base
        scratch = sb("scratch", [P, SCRATCH])
        ROUNDED_AT = 3368
        rounded = nc.alloc_sbuf_tensor_at("rounded", [P, SCRATCH - ROUNDED_AT], F32R,
                                          offset=scratch_at + 4 * ROUNDED_AT)
        ps = ctx.enter_context(nc.psum_tensor("ps", [P, 8, CHUNK], F32))

        def col(name, i=0, w=1):
            a = col_at[name][0]
            return cols[:, a + i:a + i + w]

        def dcol(name, i):
            return cols[:, ds(i + col_at[name][0], 1)]

        def const(name, rows_=P):
            a, w = const_at[name]
            return consts[0:rows_, a:a + w]

        def row(name, i=0, w=None):
            a, full = row_at[name]
            return rows[0:1, a + i:a + i + (w or full)]

        def carve(*shapes, start=0, memory=scratch, ends=None):
            at, views = start, []
            for shape in shapes:
                n = int(np.prod(shape))
                v = memory[:, at:at + n]
                if len(shape) == 2:
                    v = v.rearrange("p (a b) -> p a b", a=shape[0])
                if len(shape) == 3:
                    v = v.rearrange("p (a b c) -> p a b c", a=shape[0], b=shape[1])
                views.append(v)
                at += n
            assert at <= SCRATCH - (ROUNDED_AT if memory is rounded else 0), at
            if ends is not None:
                ends.append(at)
            return views

        THREE = (("hi", "hi"), ("hi", "lo"), ("lo", "hi"))

        ident = const("ident")
        one_row = ones[0:1, :]

        def bank(i, w=CHUNK, p=P):
            return ps[0:p, i, 0:w]

        stage_done = sem("stage_done")
        inputs_loaded = sem("inputs_loaded")
        stored = sem("stored")
        ones_ready = sem("ones_ready")
        ln_var, ln_std, ln_norm, ln_turned = (sem(n) for n in ("ln_var", "ln_std", "ln_norm", "ln_turned"))
        wp_loaded = [sem("wp_loaded0"), sem("wp_loaded1")]
        ffn_w = [sem("ffn_w0"), sem("ffn_w1")]
        hid_psum, silu_ready, hid_ready = sem("hid_psum"), sem("silu_ready"), sem("hid_ready")
        y_psum, y_used = sem("y_psum"), sem("y_used")
        x0_loaded = sem("x_weights_loaded")
        ctx_loaded = sem("ctx_loaded")
        latent_keys_loaded = sem("latent_keys_loaded")
        kvraw_loaded = sem("kvraw_loaded")
        lw_loaded = sem("layer_weights_loaded")

        def ln_dve(dve, s, n, src, dst):
            dve.wait_ge(stage_done, s)
            for t in range(T):
                dve.bn_stats(ln_st[:, t, :], src[:, t, :])
            dve.drain()
            for t in range(T):
                dve.bn_aggr(ln_mv[:, t, :], ln_st[:, t, :])
            dve.drain()
            dve.tensor_scalar(ln_ve[:, 0:T], ln_mv[:, 0:T, 1], EPS, None, ALU.add).then_inc(ln_var, 1)
            dve.wait_ge(ln_std, n + 1)
            dve.reciprocal(ln_rs[:, 0:T], ln_sd[:, 0:T])
            dve.drain()
            for t in range(T):
                ins = dve.tensor_scalar(dst[:, t, :], src[:, t, :], ln_mv[:, t, 0:1], ln_rs[:, t:t + 1],
                                        ALU.subtract, ALU.mult)
            ins.then_inc(ln_norm, 1)

        def ln_act(act, s, n, scale=None, bias=None):
            act.wait_ge(stage_done, s)
            act.wait_ge(ln_var, n + 1)
            act.activation(ln_sd[:, 0:T], ln_ve[:, 0:T], ACT.Sqrt).then_inc(ln_std, 1)
            act.wait_ge(ln_turned, n + 1)
            for k in range(K2):
                if scale is None:
                    ins = act.activation(hT[:, k, :], bank(k), ACT.Copy)
                else:
                    ins = act.activation(hT[:, k, :], bank(k), ACT.Identity, bias=bias(k), scale=scale(k))
            act.drain().then_inc(stage_done, 1)

        def ln_pe(pe, s, n, src):
            pe.wait_ge(stage_done, s)
            pe.wait_ge(ln_norm, n + 1)
            for k in range(K2):
                for t in range(T):
                    ins = pe.transpose(ps[:, k, t * P:(t + 1) * P], src[:, t, k * P:(k + 1) * P], ident)
            ins.then_inc(ln_turned, 1)

        def own(v):
            return v.bitcast(F32)


        def ffn_load(sp, par, first, second, third):
            for dst, src in (first, second, third):
                sp.dma_start(dst, src).then_inc(ffn_w[par], 16)

        def ffn_pe(pe, loads, c, h0, hidden, b2row):
            nh = 8
            pe.wait_ge(ffn_w[0], 48 * loads)
            for j in range(nh):
                if j >= 4:
                    pe.wait_ge(hid_ready, h0 + j - 3)
                for k in range(K2):
                    ins = pe.matmul(bank(j % 4), w1[0][:, k, j * P:(j + 1) * P], hT[:, k, :], start=(k == 0),
                                    stop=(k == K2 - 1))
                ins.then_inc(hid_psum, 1)
            for m in range(nh):
                pe.wait_ge(hid_ready, h0 + m + 1)
                for t in range(T):
                    if m == 0:
                        pe.matmul(bank(4 + t, D), one_row, b2row, start=True, stop=False)
                    ins = pe.matmul(bank(4 + t, D), hidden[:, m, t * P:(t + 1) * P], w2[0][:, m, :], start=False,
                                    stop=(m == nh - 1))
                    if m == nh - 1:
                        ins.then_inc(y_psum, 1)

        def ffn_act(act, h0, func, bias, hidden):
            for j in range(8):
                act.wait_ge(hid_psum, h0 + j + 1)
                act.activation(hidden[:, j, :], bank(j % 4), func, bias=bias(j)).then_inc(hid_ready, 1)

        def ffn_dve(dve, c, acc):
            for t in range(T):
                dve.wait_ge(y_psum, 4 * c + t + 1)
                dve.tensor_tensor(acc[:, t, :], bank(4 + t, D), acc[:, t, :], ALU.add).then_inc(y_used, 1)
            dve.drain()

        MSEM = [sem("moe_" + n) for n in ("logits_psum", "shifted", "exp", "cw_ready", "cwT_psum", "cwT_ready",
                                          "base_psum", "w1_split", "w2_split")]

        class Moe:

            def __init__(self, name, experts, nh, func, glu, router, rbias, rule, b1, b2, m0, c0, h0, g0, loads0):
                self.m0 = m0
                self.name, self.experts, self.nh, self.func, self.glu = name, experts, nh, func, glu
                self.router, self.rbias, self.rule, self.b1, self.b2 = router, rbias, rule, b1, b2
                self.c0, self.h0, self.g0, self.loads0 = c0, h0, g0, loads0
                (self.logits_ready, self.shifted, self.expd, self.cw_ready, self.cwT_psum, self.cwT_ready,
                 self.base_psum, self.w1_split, self.w2_split) = MSEM
                o = int(name[3])
                self.o, self.exps, self.tables, self.turns = o, (0, 1, 3, 4)[o], (0, 1, 1, 2)[o], (0, 1, 1, 2)[o]
                if rule == "capacity":
                    self.choice_psum, self.kept, self.kept_sum, self.assigned, self.plan, self.plan_ready = (
                        sem(name + n) for n in ("_choice_psum", "_kept", "_kept_sum", "_assigned", "_plan",
                                                "_plan_ready"))
                ends = []
                (self.lg, self.pr, self.eq, self.oh1, self.oh2, self.mx, self.m2,
                 self.sm, self.cw, self.cwT, self.t1, self.t2, self.t3, self.t4, self.t5) = carve(
                    (T, E), (T, E), (T, E), (T, E), (T, E), (T,), (T,), (T,),
                    (E + 1, T), (N,), (N,), (N,), (N,), (N,), (N,), ends=ends)
                assert ends[0] <= ROUNDED_AT, ends
                W1, W2 = (K2, 1024), (8, D)
                (hT_hi, hT_lo, a_hi, a_lo, b_hi, b_lo, w2_hi, w2_lo, hid_hi, hid_lo) = carve(
                    (K2, N), (K2, N), W1, W1, W1, W1, W2, W2, (8, N), (8, N), memory=rounded)
                self.hT = {"hi": hT_hi, "lo": hT_lo}
                self.w1 = ({"hi": a_hi, "lo": a_lo}, {"hi": b_hi, "lo": b_lo})
                self.w2 = {"hi": w2_hi, "lo": w2_lo}
                self.hid = {"hi": hid_hi, "lo": hid_lo}
                self.gated = hn[:, :, :].rearrange("p t d -> p (t d)").rearrange("p (a n) -> p a n", a=2)
                self.product = x0[:, :, :].rearrange("p t d -> p (t d)").rearrange("p (a n) -> p a n", a=2)
                self.off = experts - E if rule != "capacity" else 0
                self.bodies = [(e, e % 2) for e in range(experts)]

            def counts(self, i, par):
                e = 2 * i + par
                return e, e + self.c0, self.nh * e + self.h0, self.nh * e + self.g0, i + (self.loads0[par] + 1)

            def each(self, eng, body):
                with eng.Fori(0, self.experts // 2) as i:
                    body(*self.counts(i, 0), 0)
                    body(*self.counts(i, 1), 1)
                if self.experts % 2:
                    body(*self.counts(self.experts // 2, 0), 0)

            def b1_col(self, e, j):
                width = self.nh * (2 if self.glu else 1)
                return dcol(self.b1, e * width + j) if not isinstance(e, int) else col(self.b1, e * width + j)

            def sp(self, sp, sources):
                sp.wait_ge(y_psum, 4 * self.c0)

                def body(e, c, h, g, loads, par):
                    sp.wait_ge(y_psum, 4 * c - 4)
                    ffn_load(sp, par, *sources(e, par))
                self.each(sp, body)

            def pe(self, pe, s):
                pe.wait_ge(stage_done, s)
                for t in range(T):
                    o = ps[:, 0, t * E:(t + 1) * E]
                    if self.rbias:
                        pe.matmul(o, one_row, row(self.rbias), start=True, stop=False)
                    for k in range(K2):
                        ins = pe.matmul(o, hT[:, k, t * P:(t + 1) * P], routers[:, self.router, k, :],
                                        start=(k == 0 and not self.rbias), stop=(k == K2 - 1))
                ins.then_inc(self.logits_ready, 1)
                nE = self.experts
                if self.rule == "capacity":
                    pe.wait_ge(self.cw_ready, self.o + 1)
                    for i, oh in enumerate((self.oh1, self.oh2)):
                        for t in range(T):
                            ins = pe.transpose(ps[0:E, 1 + i, t * P:(t + 1) * P], oh[:, t, :], ident)
                    ins.then_inc(self.choice_psum, 1)
                    pe.wait_ge(self.kept, 1)
                    pe.matmul(bank(3, N, E), ones[0:E, 0:E], self.t2[0:E, :], start=True, stop=True)\
                        .then_inc(self.kept_sum, 1)
                    pe.wait_ge(self.assigned, 1)
                    pe.matmul(bank(4, N, E + 1), const("split9", E), self.t2[0:E, :], start=True, stop=True)\
                        .then_inc(self.plan, 1)
                    pe.wait_ge(self.cwT_ready, self.tables + 1)
                    for t in range(T):
                        ins = pe.transpose(ps[:, 5, t * 16:t * 16 + E + 1], self.cwT[0:E + 1, t * P:(t + 1) * P],
                                           ident[0:E + 1, 0:E + 1])
                    ins.then_inc(self.plan_ready, 1)
                elif self.b2 is not None:
                    pe.wait_ge(self.cw_ready, self.o + 1)
                    for t in range(T):
                        ins = pe.transpose(ps[0:nE, 1, t * P:(t + 1) * P], self.cw[:, 0:nE, t], ident)
                    ins.then_inc(self.cwT_psum, 1)
                    pe.wait_ge(self.cwT_ready, self.tables + 1)
                if self.b2 is not None:
                    for t in range(T):
                        ins = pe.matmul(ps[:, 6 + t // 2, (t % 2) * D:(t % 2 + 1) * D],
                                        self.cwT[0:nE, t * P:(t + 1) * P], self.b2[:, :], start=True, stop=True)
                    ins.then_inc(self.base_psum, 1)
                    pe.wait_ge(self.shifted, 2 * self.o + 2)
                else:
                    pe.wait_ge(self.cw_ready, self.o + 1)

                def body(e, c, h, g, loads, par):
                    nh, w = self.nh, self.w1[par]
                    depth = 2 if self.glu else 4
                    pe.wait_ge(self.w1_split, e + (self.m0 + 1))
                    for j in range(nh):
                        pe.wait_ge(hid_ready, h + (j - depth + 1))
                        for bk, m in ((2 * (j % 2), j), (2 * (j % 2) + 1, nh + j)) if self.glu else ((j % 4, j),):
                            for n, (ii, jj) in enumerate(THREE):
                                for k in range(K2):
                                    ins = pe.matmul(bank(bk), w[ii][:, k, m * P:(m + 1) * P], self.hT[jj][:, k, :],
                                                    start=(n == 0 and k == 0), stop=(n == 2 and k == K2 - 1))
                        ins.then_inc(hid_psum, 1)
                    pe.wait_ge(self.w2_split, e + (self.m0 + 1))
                    for m in range(nh):
                        pe.wait_ge(hid_ready, h + (m + 1))
                        for t in range(T):
                            if m == 0:
                                pe.wait_ge(y_used, 4 * c - 4 + t + 1)
                            for n, (ii, jj) in enumerate(THREE):
                                ins = pe.matmul(bank(4 + t, D), self.hid[ii][:, m, t * P:(t + 1) * P],
                                                self.w2[jj][:, m, :], start=(m == 0 and n == 0),
                                                stop=(m == nh - 1 and n == 2))
                            if m == nh - 1:
                                ins.then_inc(y_psum, 1)
                self.each(pe, body)

            def act(self, act, s):
                act.wait_ge(stage_done, s)
                act.wait_ge(self.shifted, 2 * self.o + 1)
                act.activation(self.pr, self.lg, ACT.Exp).then_inc(self.expd, 1)
                if self.rule == "renormalised":
                    act.wait_ge(self.shifted, 2 * self.o + 2)
                    act.activation(self.sm, self.m2, ACT.Exp).then_inc(self.expd, 1)

                def body(e, c, h, g, loads, par):
                    for j in range(self.nh):
                        bias = lambda: dict(bias=self.b1_col(e, j)) if self.b1 else {}
                        if not self.glu:
                            act.wait_ge(hid_ready, h + (j - 1))
                        act.wait_ge(hid_psum, h + (j + 1))
                        if self.glu:
                            act.activation(self.gated[:, j % 2, :], bank(2 * (j % 2)), self.func, **bias())\
                                .then_inc(silu_ready, 1)
                        else:
                            act.activation(self.hid["hi"][:, j, :], bank(j % 4), self.func, **bias())
                            act.activation(self.gated[:, j % 2, :], bank(j % 4), self.func, **bias())\
                                .then_inc(silu_ready, 1)
                self.each(act, body)

            def one_hot(self, dve, pr, mx, oh):
                dve.tensor_reduce(mx, pr, AX.X, ALU.max)
                dve.drain()
                dve.tensor_tensor(self.eq, pr, mx.unsqueeze(2).to_broadcast([P, T, E]), ALU.is_equal)
                dve.drain()
                dve.tensor_tensor(self.eq, self.eq, const("first_of").unsqueeze(1).to_broadcast([P, T, E]), ALU.mult)
                dve.drain()
                dve.tensor_reduce(self.t1[:, 0:T], self.eq, AX.X, ALU.max)
                dve.drain()
                dve.tensor_tensor(oh, self.eq, self.t1[:, 0:T].unsqueeze(2).to_broadcast([P, T, E]), ALU.is_equal)
                dve.drain()

            def dve(self, dve, s):
                bc = lambda v: v.unsqueeze(2).to_broadcast([P, T, E])
                dve.wait_ge(stage_done, s)
                dve.wait_ge(self.logits_ready, self.o + 1)
                logits = ps[:, 0, 0:T * E].rearrange("p (t e) -> p t e", t=T)
                dve.tensor_reduce(self.mx, logits, AX.X, ALU.max)
                dve.drain()
                dve.tensor_tensor(self.lg, logits, bc(self.mx), ALU.subtract).then_inc(self.shifted, 1)
                dve.wait_ge(self.expd, self.exps + 1)
                dve.tensor_reduce(self.mx, self.pr, AX.X, ALU.add)
                dve.drain()
                dve.reciprocal(self.sm, self.mx)
                dve.drain()
                dve.tensor_tensor(self.pr, self.pr, bc(self.sm), ALU.mult)
                dve.drain()
                self.one_hot(dve, self.pr, self.mx, self.oh1)
                cw = self.cw.rearrange("p e t -> p t e")
                routed = cw[:, :, self.off:self.off + E]
                if self.rule == "top1":
                    dve.tensor_tensor(routed, self.oh1, bc(self.mx), ALU.mult)
                else:
                    dve.scalar_tensor_tensor(out=self.lg, in0=self.oh1, scalar=-4.0, in1=self.pr,
                                             op0=ALU.mult, op1=ALU.add)
                    dve.drain()
                    self.one_hot(dve, self.lg, self.m2, self.oh2)
                if self.rule == "top2":
                    dve.tensor_tensor(self.eq, self.oh1, self.oh2, ALU.add)
                    dve.drain()
                    dve.tensor_tensor(routed, self.eq, self.pr, ALU.mult)
                    dve.memset(self.cw[:, 0, :], 1.0)
                if self.rule == "renormalised":
                    dve.tensor_tensor(self.m2, self.m2, self.mx, ALU.subtract)
                    dve.drain().then_inc(self.shifted, 1)
                    dve.wait_ge(self.expd, self.exps + 2)
                    dve.tensor_scalar(self.mx, self.sm, 1.0, None, ALU.add)
                    dve.drain()
                    dve.reciprocal(self.m2, self.mx)
                    dve.drain()
                    dve.tensor_tensor(self.sm, self.sm, self.m2, ALU.mult)
                    dve.tensor_tensor(self.oh1, self.oh1, bc(self.m2), ALU.mult)
                    dve.drain()
                    dve.tensor_tensor(self.oh2, self.oh2, bc(self.sm), ALU.mult)
                    dve.drain()
                    dve.tensor_tensor(routed, self.oh1, self.oh2, ALU.add)
                dve.drain().then_inc(self.cw_ready, 1)
                nE = self.experts
                if self.rule == "capacity":
                    o1, o2, t2, t3, t4, t5 = (v[0:E, :] for v in (self.t1, self.cwT, self.t2, self.t3, self.t4, self.t5))
                    unit = ones[0:E, 0:1].to_broadcast([E, N])
                    dve.wait_ge(self.choice_psum, 1)
                    dve.tensor_copy(o1, bank(1, N, E))
                    dve.tensor_copy(o2, bank(2, N, E))
                    dve.drain()
                    dve.tensor_tensor_scan(t3, unit, o1, 0.0, ALU.mult, ALU.add)
                    dve.drain()
                    dve.scalar_tensor_tensor(out=t2, in0=t3, scalar=float(CAP), in1=o1, op0=ALU.is_le, op1=ALU.mult)\
                        .then_inc(self.kept, 1)
                    dve.tensor_scalar(self.mx[0:E, 0:1], t3[:, N - 1:N], float(CAP), None, ALU.min)
                    dve.wait_ge(self.kept_sum, 1)
                    dve.tensor_scalar(t4, bank(3, N, E), -1.0, 1.0, ALU.mult, ALU.add)
                    dve.drain()
                    dve.tensor_tensor(t4, t4, o2, ALU.mult)
                    dve.drain()
                    dve.tensor_tensor_scan(t5, unit, t4, 0.0, ALU.mult, ALU.add)
                    dve.drain()
                    dve.tensor_scalar(t5, t5, self.mx[0:E, 0:1], float(CAP), ALU.add, ALU.is_le)
                    dve.drain()
                    dve.tensor_tensor(t4, t4, t5, ALU.mult)
                    dve.drain()
                    dve.tensor_tensor(t2, t2, t4, ALU.add)
                    dve.drain().then_inc(self.assigned, 1)
                    dve.wait_ge(self.plan, 1)
                    dve.tensor_scalar(self.cwT[0:E + 1, :], bank(4, N, E + 1), const("rest9", E + 1), None, ALU.add)\
                        .then_inc(self.cwT_ready, 1)
                    dve.wait_ge(self.plan_ready, 1)
                    dve.tensor_copy(cw, ps[:, 5, 0:16 * T].rearrange("p (t e) -> p t e", t=T)[:, :, 0:E + 1])
                    dve.drain()
                elif self.b2 is not None:
                    dve.wait_ge(self.cwT_psum, self.turns + 1)
                    dve.tensor_copy(self.cwT[0:nE, :], bank(1, N, nE)).then_inc(self.cwT_ready, 1)
                if self.b2 is not None:
                    dve.wait_ge(self.base_psum, self.tables + 1)
                    dve.tensor_tensor(x[:, :, :].rearrange("p t d -> p (t d)"),
                                      ps[:, 6:8, :].rearrange("p a b -> p (a b)"),
                                      x[:, :, :].rearrange("p t d -> p (t d)"), ALU.add)
                    dve.drain().then_inc(self.shifted, 1)
                flat = self.cw.rearrange("p e t -> p (e t)")

                def body(e, c, h, g, loads, par):
                    weight = lambda t: (flat[:, ds(e * T + t, 1)] if not isinstance(e, int)
                                        else flat[:, e * T + t:e * T + t + 1])
                    for j in range(self.nh):
                        high, low = self.hid["hi"][:, j, :], self.hid["lo"][:, j, :]
                        full = self.gated[:, j % 2, :]
                        dve.wait_ge(silu_ready, g + (j + 1))
                        if self.glu:
                            up = bank(2 * (j % 2) + 1)
                            if self.b1:
                                dve.scalar_tensor_tensor(out=self.product[:, j % 2, :], in0=up,
                                                         scalar=self.b1_col(e, self.nh + j), in1=full, op0=ALU.add,
                                                         op1=ALU.mult)
                            else:
                                dve.tensor_tensor(self.product[:, j % 2, :], up, full, ALU.mult)
                            full = self.product[:, j % 2, :]
                            dve.drain()
                            dve.tensor_copy(high, full)
                            dve.drain()
                        dve.tensor_tensor(low, full, own(high), ALU.subtract).then_inc(hid_ready, 1)
                    for t in range(T):
                        dve.wait_ge(y_psum, 4 * c + t + 1)
                        dve.scalar_tensor_tensor(out=x[:, t, :], in0=bank(4 + t, D), scalar=weight(t), in1=x[:, t, :],
                                                 op0=ALU.mult, op1=ALU.add).then_inc(y_used, 1)
                    dve.drain()
                self.each(dve, body)
                dve.drain().then_inc(stage_done, 1)

            def pool(self, pool, s):
                def split(src, parts):
                    one = ones[:, 0:1].unsqueeze(2).to_broadcast([P, src.shape[1], src.shape[2]])
                    pool.tensor_tensor(parts[0], src, one, ALU.mult)
                    pool.drain()
                    pool.tensor_tensor(parts[1], src, own(parts[0]), ALU.subtract)

                pool.wait_ge(stage_done, s)
                split(hT[:, :, :], (self.hT["hi"], self.hT["lo"]))
                width = self.nh * P * (2 if self.glu else 1)

                def body(e, c, h, g, loads, par):
                    w = self.w1[par]
                    pool.wait_ge(ffn_w[par], 48 * loads)
                    split(w1[par][:, :, 0:width], (w["hi"][:, :, 0:width], w["lo"][:, :, 0:width]))
                    pool.drain().then_inc(self.w1_split, 1)
                    pool.wait_ge(y_psum, 4 * c)
                    split(w2[par][:, 0:self.nh, :], (self.w2["hi"][:, 0:self.nh, :], self.w2["lo"][:, 0:self.nh, :]))
                    pool.drain().then_inc(self.w2_split, 1)
                self.each(pool, body)

        LSEM = {n: sem("local_" + n) for n in (
            "kv_rows_copied", "qk_psum", "q_ready", "k_ready", "v_psum", "v_ready", "scores_psum", "shifted", "exp",
            "p_ready", "pT_psum", "pT_ready", "o_psum", "o_ready", "oT_psum", "oT_ready", "y_psum", "y_added",
            "prepared")}

        class Local:

            def __init__(self, order, slot, loads, scale, mask, kvsrc, extra_mask=False, grouped=False, bo=None):
                self.t0 = T * order
                self.slot, self.loads, self.scale, self.mask, self.bo = slot, loads, scale, mask, bo
                self.extra_mask, self.grouped = extra_mask, grouped
                (self.copied, self.qk_psum, self.q_ready, self.k_ready, self.v_psum, self.v_ready, self.s_psum,
                 self.shifted, self.expd, self.pT_psum, self.pT_ready, self.o_psum, self.o_ready,
                 self.oT_psum, self.oT_ready, self.y_ps, self.added, self.prepared) = (
                    LSEM[n] for n in
                    ("kv_rows_copied", "qk_psum", "q_ready", "k_ready", "v_psum", "v_ready", "scores_psum",
                     "shifted", "exp", "pT_psum", "pT_ready", "o_psum", "o_ready", "oT_psum", "oT_ready",
                     "y_psum", "y_added", "prepared"))
                (self.src64, self.kvt, self.q, self.k, self.v, self.sm, self.pT, self.o, self.oT, self.mx, self.rs,
                 self.keysT, self.maskt, self.keyrow, self.raw, self.keyraw, self.kraw) = carve(
                    (K2, N), (K2, P), (K2, P), (K2, HG, P), (D,), (H, P), (H, P), (D,), (K2, P), (H,), (H,),
                    (T, D), (T, P), (N,), (K2, P), (N,), (K2, P))
                self.kvsrc = self.src64 if kvsrc is None else kvsrc

            def group(self, t, g):
                return 2 * t + (2 * self.t0 + g + 1)

            def pe(self, pe, s):
                W = wp[self.slot]
                pe.wait_ge(stage_done, s)
                pe.wait_ge(wp_loaded[self.slot], 64 * self.loads)
                if self.extra_mask:
                    pe.wait_ge(latent_keys_loaded, 32)
                    for k in range(K2):
                        for t in range(T):
                            pe.transpose(ps[:, k, t * P:(t + 1) * P], self.keysT[:, t, k * P:(k + 1) * P], ident)
                    pe.wait_ge(self.prepared, 1)
                    pe.matmul(bank(2), one_row, self.keyrow[0:1, :], start=True, stop=True).then_inc(self.qk_psum, 1)
                    pe.wait_ge(self.prepared, 3)
                if self.grouped:
                    pe.wait_ge(self.prepared, 4)
                with pe.Fori(0, T) as t:
                    pe.wait_ge(self.added, t + (self.t0 + 1))
                    for m in range(K2):
                        for k in range(K2):
                            pe.matmul(ps[:, 7, m * P:(m + 1) * P], W[:, 0, k, m * P:(m + 1) * P],
                                      hT[:, k, ds(t * P, P)], start=(k == 0), stop=(k == K2 - 1))
                    pe.wait_ge(self.copied, t + (self.t0 + 1))
                    for m in range(K2):
                        for k in range(K2):
                            ins = pe.matmul(ps[:, 0, D + m * P:D + (m + 1) * P], W[:, 1, k, m * P:(m + 1) * P],
                                            self.kvt[:, k, :], start=(k == 0), stop=(k == K2 - 1))
                    ins.then_inc(self.qk_psum, 1)
                    for k in range(K2):
                        ins = pe.matmul(bank(1, D), self.kvt[:, k, :], W[:, 2, k, :], start=(k == 0), stop=(k == K2 - 1))
                    ins.then_inc(self.v_psum, 1)
                    pe.wait_ge(self.q_ready, t + (self.t0 + 1))
                    for g in range(K2):
                        pe.wait_ge(self.k_ready, self.group(t, g))
                        for half in range(2):
                            ins = pe.matmul(bank(2 + 2 * g + half), self.q[:, g, :],
                                            self.k[:, g, 4 * half:4 * half + 4, :], start=True, stop=True)
                        ins.then_inc(self.s_psum, 1)
                    for g in range(K2):
                        pe.wait_ge(self.expd, self.group(t, g))
                        for h in range(g * HG, (g + 1) * HG):
                            ins = pe.transpose(ps[:, 2 + h // 4, (h % 4) * P:(h % 4 + 1) * P], self.sm[:, h, :], ident)
                        ins.then_inc(self.pT_psum, 1)
                    pe.wait_ge(self.v_ready, t + (self.t0 + 1))
                    for g in range(K2):
                        pe.wait_ge(self.pT_ready, self.group(t, g))
                        for h in range(g * HG, (g + 1) * HG):
                            ins = pe.matmul(ps[:, 6, h * HD:(h + 1) * HD], self.pT[:, h, :],
                                            self.v[:, h * HD:(h + 1) * HD], start=True, stop=True)
                    ins.then_inc(self.o_psum, 1)
                    pe.wait_ge(self.o_ready, t + (self.t0 + 1))
                    for k in range(K2):
                        ins = pe.transpose(ps[:, 7, k * P:(k + 1) * P], self.o[:, k * P:(k + 1) * P], ident)
                    ins.then_inc(self.oT_psum, 1)
                    pe.wait_ge(self.oT_ready, t + (self.t0 + 1))
                    if self.bo:
                        pe.matmul(bank(1, D), one_row, row(self.bo), start=True, stop=False)
                    for k in range(K2):
                        ins = pe.matmul(bank(1, D), self.oT[:, k, :], W[:, 3, k, :], start=(k == 0 and not self.bo),
                                        stop=(k == K2 - 1))
                    ins.then_inc(self.y_ps, 1)

            def act(self, act, s):
                act.wait_ge(stage_done, s)
                if self.extra_mask:
                    act.wait_ge(self.prepared, 3)
                with act.Fori(0, T) as t:
                    act.activation(self.kvt, self.kvsrc[:, :, ds(t * P, P)], ACT.Copy).then_inc(self.copied, 1)
                    act.wait_ge(self.qk_psum, t + (self.t0 + 2))
                    act.activation(self.q, ps[:, 7, 0:D].rearrange("p (m n) -> p m n", m=K2), ACT.Copy,
                                   scale=self.scale).then_inc(self.q_ready, 1)
                    act.wait_ge(self.v_psum, t + (self.t0 + 1))
                    act.activation(self.v, bank(1, D), ACT.Copy).then_inc(self.v_ready, 1)
                    for g in range(K2):
                        sm = self.sm[:, g * HG:(g + 1) * HG, :]
                        act.wait_ge(self.shifted, self.group(t, g))
                        act.activation(sm, sm, ACT.Exp).then_inc(self.expd, 1)
                    for g in range(K2):
                        act.wait_ge(self.pT_psum, self.group(t, g))
                        act.activation(self.pT[:, g * HG:(g + 1) * HG, :].rearrange("p h n -> p (h n)"),
                                       ps[:, 2 + 2 * g:4 + 2 * g, :].rearrange("p a b -> p (a b)"), ACT.Copy)\
                            .then_inc(self.pT_ready, 1)
                    act.wait_ge(self.oT_psum, t + (self.t0 + 1))
                    act.activation(self.oT, ps[:, 7, 0:D].rearrange("p (m n) -> p m n", m=K2), ACT.Copy)\
                        .then_inc(self.oT_ready, 1)

            def dve(self, dve, s):
                dve.wait_ge(stage_done, s)
                if self.extra_mask:
                    dve.wait_ge(latent_keys_loaded, 32)
                    dve.tensor_copy(self.keyrow[0:1, :], self.keyraw[0:1, :].bitcast(I32))
                    dve.drain()
                    dve.tensor_scalar(self.keyrow[0:1, :], self.keyrow[0:1, :], 0.0, BLOCKED, ALU.is_equal, ALU.mult)\
                        .then_inc(self.prepared, 1)
                    dve.wait_ge(self.qk_psum, 1)
                    dve.tensor_copy(self.src64, ps[:, 0:2, :]).then_inc(self.prepared, 1)
                    dve.tensor_tensor(self.maskt, ps[:, 2, :].rearrange("p (t n) -> p t n", t=T),
                                      const(self.mask).unsqueeze(1).to_broadcast([P, T, P]), ALU.add)\
                        .then_inc(self.prepared, 1)
                if self.grouped:
                    dve.wait_ge(kvraw_loaded, 32)
                    dve.wait_ge(wp_loaded[self.slot], 64 * self.loads)
                    for i, raw in enumerate((self.raw, self.kraw)):
                        for k in range(K2):
                            g = raw[:, k, 0:64].rearrange("p (g d) -> p g d", g=4).unsqueeze(2).to_broadcast([P, 4, 4, HD])
                            o = wp[self.slot][:, 1 + i, k, :].rearrange("p (g r d) -> p g r d", g=4, r=4)
                            dve.tensor_copy(o, g)
                    dve.drain().then_inc(self.prepared, 1)
                dve.drain()
                with dve.Fori(0, T) as t:
                    dve.wait_ge(self.qk_psum, t + (self.t0 + 2))
                    for g in range(K2):
                        dve.tensor_tensor(self.k[:, g, :, :],
                                          ps[:, 0, D + g * P:D + (g + 1) * P].unsqueeze(1).to_broadcast([P, HG, P]),
                                          const("head_of").unsqueeze(2).to_broadcast([P, HG, P]), ALU.mult)\
                            .then_inc(self.k_ready, 1)
                    m = (self.maskt[:, ds(t, 1), :] if self.extra_mask else const(self.mask).unsqueeze(1))
                    for g in range(K2):
                        hs = slice(g * HG, (g + 1) * HG)
                        dve.wait_ge(self.s_psum, self.group(t, g))
                        scores = ps[:, 2 + 2 * g:4 + 2 * g, :].rearrange("p a (c n) -> p (a c) n", n=P)
                        dve.tensor_tensor(self.sm[:, hs, :], scores, m.to_broadcast([P, HG, P]), ALU.add)
                        dve.drain()
                        dve.tensor_reduce(self.mx[:, hs], self.sm[:, hs, :], AX.X, ALU.max)
                        dve.drain()
                        dve.tensor_tensor(self.sm[:, hs, :], self.sm[:, hs, :],
                                          self.mx[:, hs].unsqueeze(2).to_broadcast([P, HG, P]), ALU.subtract)\
                            .then_inc(self.shifted, 1)
                    for g in range(K2):
                        hs = slice(g * HG, (g + 1) * HG)
                        dve.wait_ge(self.expd, self.group(t, g))
                        dve.tensor_reduce(self.rs[:, hs], self.sm[:, hs, :], AX.X, ALU.add)
                    dve.drain()
                    dve.reciprocal(self.mx, self.rs)
                    dve.drain()
                    dve.wait_ge(self.o_psum, t + (self.t0 + 1))
                    dve.tensor_tensor(self.o.rearrange("p (h d) -> p h d", h=H),
                                      bank(6, D).rearrange("p (h d) -> p h d", h=H),
                                      self.mx.unsqueeze(2).to_broadcast([P, H, HD]), ALU.mult).then_inc(self.o_ready, 1)
                    dve.wait_ge(self.y_ps, t + (self.t0 + 1))
                    xt = x[:, ds(t, 1), :]
                    dve.tensor_tensor(xt, bank(1, D).unsqueeze(1), xt, ALU.add).then_inc(self.added, 1)
                dve.drain().then_inc(stage_done, 1)

        chunks = [(c * CHUNK, min(CHUNK, KEYS - c * CHUNK)) for c in range(4)]

        FSEM, CSEM = {}, {}

        def cross_sem(n):
            if n not in CSEM:
                CSEM[n] = sem("cross_" + n)
            return CSEM[n]

        class Flash:

            def __init__(self, name, nj, tiles):
                if name not in FSEM:
                    FSEM[name] = [sem(f"{name}_{n}") for n in ("scores_psum", "max_ready", "exp_done", "pT_psum",
                                                               "pT_by_act", "pT_by_dve", "o_psum", "o_taken",
                                                               "batch_done")]
                self.nj, self.tiles = nj, tiles
                self.keys = sum(tiles)
                self.chunks = [(c * CHUNK, min(CHUNK, self.keys - c * CHUNK)) for c in range(4)]
                self.turns = [range(c, min(c + 4, len(tiles))) for c in range(0, len(tiles), 4)]
                (self.s_psum, self.max_ready, self.exp_done, self.pT_psum, self.pT_act, self.pT_dve, self.o_psum,
                 self.o_taken, self.batch_done) = FSEM[name]

            def start(self, kt):
                return kt * P if kt < KT else KEYS

            def pe_turn(self, pe, J, p):
                for c, tiles in enumerate(self.turns):
                    if c != 3:
                        pe.wait_ge(self.exp_done, 3 * J + c + 4)
                    if c >= 2:
                        pe.wait_ge((self.pT_act, self.pT_dve)[c % 2], 2 * J + 1)
                    for i, kt in enumerate(tiles):
                        n = self.tiles[kt]
                        ins = pe.transpose(ps[0:n, 4 + c % 2, i * P:(i + 1) * P],
                                           p[:, self.start(kt):self.start(kt) + n], ident)
                    ins.then_inc(self.pT_psum, 1)

            def copy_turned(self, eng, copy, J, c, pT, done):
                tiles = self.turns[c]
                eng.wait_ge(self.pT_psum, 4 * J + c + 1)
                full = [kt for kt in tiles if self.tiles[kt] == P]
                if full:
                    ins = copy(pT[:, full[0]:full[-1] + 1, :],
                               ps[:, 4 + c % 2, 0:len(full) * P].rearrange("p (a b) -> p a b", b=P))
                for kt in tiles:
                    if self.tiles[kt] != P:
                        n, i = self.tiles[kt], kt - tiles[0]
                        ins = copy(pT[0:n, kt, :], ps[0:n, 4 + c % 2, i * P:(i + 1) * P])
                ins.then_inc(done, 1)

            def act_turn(self, act, J, pT):
                for c in (0, 2):
                    self.copy_turned(act, lambda o, i: act.activation(o, i, ACT.Copy), J, c, pT, self.pT_act)

            def dve_turn(self, dve, J, pT):
                for c in (1, 3):
                    self.copy_turned(dve, dve.tensor_copy, J, c, pT, self.pT_dve)

            def pe_wait_turned(self, pe, J, c):
                pe.wait_ge((self.pT_act, self.pT_dve)[c % 2], 2 * J + c // 2 + 1)

            def act_exp(self, act, J, p, negmax, den):
                act.wait_ge(self.max_ready, J + 1)
                flat = ps[:, 0:4, :].rearrange("p a b -> p (a b)")
                for g, (a, z) in enumerate(((0, CHUNK), (CHUNK, 2 * CHUNK), (2 * CHUNK, self.keys))):
                    act.activation(p[:, a:z], flat[:, a:z], ACT.Exp, bias=negmax, accum_out=den[:, g:g + 1])\
                        .then_inc(self.exp_done, 1)

            def dve_max(self, dve, J, part, negmax, which=range(4)):
                for c in which:
                    dve.wait_ge(self.s_psum, 4 * J + c + 1)
                    dve.tensor_reduce(part[:, c:c + 1], bank(c, self.chunks[c][1]), AX.X, ALU.max)
                if 3 in which:
                    dve.drain()
                    dve.tensor_reduce(negmax, part, AX.X, ALU.max, negate=True).then_inc(self.max_ready, 1)

            def dve_sums(self, dve, J, den, total, rden):
                dve.wait_ge(self.o_psum, J + 1)
                dve.tensor_reduce(total, den, AX.X, ALU.add)
                dve.drain()
                dve.reciprocal(rden, total)
                dve.drain()

        class Cross(Flash):
            WIDE = KEYS + 1

            def __init__(self, order, slot, loads, ctx_before, biased):
                super().__init__("cross", H // 2, [P] * FULL + [TAIL])
                self.b0, self.order = B * order, order
                self.slot, self.loads, self.ctx_before, self.biased = slot, loads, ctx_before, biased
                (self.w_ready, self.q_psum, self.q_ready, self.qbd_ready, self.turned, self.x_hi, self.x_lo,
                 self.k_psum, self.k_hi, self.k_lo, self.v_psum, self.v_hi, self.v_lo, self.pv_psum, self.pv_copied,
                 self.o_rows, self.oT_psum, self.oT_final, self.y_ps) = (
                    cross_sem(n) for n in ("weights_split", "q_psum", "q_split", "q_blocks", "ctx_turned", "ctxT_high",
                                           "ctxT_low", "k_psum", "k_high", "k_low", "v_psum", "v_high", "v_low",
                                           "pv_psum", "pv_copied", "o_rows", "oT_psum", "oT_final", "y_psum"))
                ends = []
                W = self.WIDE
                self.ctx, self.st = carve((KT, D), (40,), ends=ends)
                self.oT = hn[:, :, :].rearrange("p t d -> p (t d)").rearrange("p (k n) -> p k n", k=K2)
                self.o = x0[:, 0, 0:self.nj * 2 * HD].rearrange("p (j d) -> p j d", j=self.nj)
                assert ends[0] == ROUNDED_AT, ends
                names = ("x_low", "x_high", "k_high", "k_low", "qb_high", "qb_low", "q_high", "q_low", "w_high",
                         "w_low", "values", "pT_low")
                shapes = ((K2, W), (K2, W), (K2, W), (K2, W), (K2, HG * S), (K2, HG * S), (K2, N), (K2, N),
                          (2 * K2, D), (2 * K2, D), (KT * self.nj, 4 * HD), (KT, P))
                r = dict(zip(names, carve(*shapes, memory=rounded)))
                self.xT = {"hi": r["x_high"], "lo": r["x_low"]}
                self.kT = {"hi": r["k_high"], "lo": r["k_low"]}
                self.qbd = {"hi": r["qb_high"], "lo": r["qb_low"]}
                self.q = {"hi": r["q_high"], "lo": r["q_low"]}
                self.w = {"hi": r["w_high"], "lo": r["w_low"]}
                self.p = carve((KEYS,), (KEYS,), start=ROUNDED_AT)
                pT_high, = carve((KT, P), start=2 * KEYS, memory=rounded)
                self.pT = {"hi": pT_high, "lo": r["pT_low"]}
                self.v = r["values"].rearrange("p (t j) c -> p t j c", t=KT)
                self.v_part = {"hi": self.v[:, :, :, 0:2 * HD], "lo": self.v[:, :, :, 2 * HD:4 * HD]}
                self.sums = x0[0:4 * HD, 1, 0:2 * P].rearrange("p (q r) -> p q r", q=2)
                self.pT_hi, self.pT_lo = self.pT_act, self.pT_dve

            def sp(self, sp, s, ctx_rows):
                sp.wait_ge(stage_done, s)
                with sp.Fori(0, B) as b:
                    n = b + self.b0
                    sp.wait_ge(self.turned, 8 * n + 8)
                    sp.dma_start(self.ctx[:, 0:FULL, :],
                                 ctx_rows[b, 0:FULL * P, :].rearrange("(t p) d -> p t d", p=P)).then_inc(ctx_loaded, 16)
                    sp.dma_start(self.ctx[0:TAIL, FULL, :], ctx_rows[b, FULL * P:KEYS, :]).then_inc(ctx_loaded, 16)

            def pool(self, pool, s):
                pool.wait_ge(stage_done, s)
                pool.wait_ge(wp_loaded[self.slot], 64 * self.loads)
                kv = wp[self.slot][:, 1:3, :, :].rearrange("p a k n -> p (a k) n")
                pool.tensor_copy(self.w["hi"], kv)
                pool.drain()
                pool.tensor_tensor(self.w["lo"], kv, own(self.w["hi"]), ALU.subtract)
                pool.drain().then_inc(self.w_ready, 1)
                pool.wait_ge(self.q_ready, self.order + 1)
                with pool.Fori(0, B) as b:
                    u = b + self.b0
                    pool.wait_ge(self.batch_done, u + 1)
                    for part in ("hi", "lo"):
                        for g in range(K2):
                            pool.tensor_tensor(self.qbd[part][:, g, :].rearrange("p (h q) -> p h q", h=HG),
                                               own(self.q[part])[:, g, ds(b * S, S)].unsqueeze(1)
                                               .to_broadcast([P, HG, S]),
                                               const("head_of").unsqueeze(2).to_broadcast([P, HG, S]), ALU.mult)
                        pool.memset(own(self.xT[part])[:, :, KEYS:self.WIDE], 0.0)
                    pool.drain().then_inc(self.qbd_ready, 1)

            PROLOGUE = (("x", 0), ("x", 1), ("k", 0), ("x", 2), ("k", 1), ("x", 3), ("k", 2), ("k", 3))

            def width(self, c, kind):
                a, w = self.chunks[c]
                return a, (w + 1 if kind == "k" and c == 3 else w)

            def pe_rows(self, pe, J, q):
                pe.wait_ge(self.pv_copied, J + 1)
                pe.matmul(ps[:, 6 + q, P:P + 2 * HD], self.sums[:, q, :], const("stack", 4 * HD), start=True, stop=True)\
                    .then_inc(self.o_psum, 1)

            def pe_scores(self, pe, J, j, half):
                g, jj = j // 4, j % 4
                for c in (2 * half, 2 * half + 1):
                    a, w = self.width(c, "k")
                    if c < 3:
                        pe.wait_ge(self.exp_done, 3 * J + c + 1)
                    for n, (ii, kk) in enumerate(THREE):
                        ins = pe.matmul(bank(c, w), self.qbd[ii][:, g, 2 * jj * S:(2 * jj + 2) * S],
                                        self.kT[kk][:, g, a:a + w], start=(n == 0), stop=(n == 2))
                    ins.then_inc(self.s_psum, 1)

            def pe_turn(self, pe, J, p, half):
                for c in (2 * half, 2 * half + 1):
                    if c != 3:
                        pe.wait_ge(self.exp_done, 3 * J + c + 4)
                    if c >= 2:
                        pe.wait_ge(self.pT_lo, 4 * J + c - 1)
                    for i, kt in enumerate(self.turns[c]):
                        n = self.tiles[kt]
                        ins = pe.transpose(ps[0:n, 4 + c % 2, i * P:(i + 1) * P],
                                           p[:, self.start(kt):self.start(kt) + n], ident)
                    ins.then_inc(self.pT_psum, 1)

            def turned_views(self, c, part):
                tiles, n = self.turns[c], self.tiles[self.turns[c][0]]
                return (ps[0:n, 4 + c % 2, 0:len(tiles) * P].rearrange("p (a b) -> p a b", b=P),
                        self.pT[part][0:n, tiles[0]:tiles[-1] + 1, :])

            def value_views(self, i, part):
                if 2 * i + 1 < KT:
                    return (bank(i).rearrange("p (t j c) -> p t j c", t=2, j=self.nj),
                            self.v_part[part][:, 2 * i:2 * i + 2, :, :])
                return (bank(i, D, TAIL).rearrange("p (j c) -> p j c", j=self.nj), self.v_part[part][0:TAIL, 2 * i, :, :])

            def act_turn(self, act, J):
                for c in range(4):
                    act.wait_ge(self.pT_psum, 4 * J + c + 1)
                    turned, high = self.turned_views(c, "hi")
                    act.activation(high, turned, ACT.Copy).then_inc(self.pT_hi, 1)

            def dve_rows(self, dve, J, j):
                q = j % 2
                dve.wait_ge(self.o_psum, J + 1)
                dve.scalar_tensor_tensor(out=self.o[:, j, :], in0=ps[:, 6 + q, P:P + 2 * HD],
                                         scalar=self.st[:, 20 + q:21 + q], in1=const("own_half"), op0=ALU.mult,
                                         op1=ALU.mult).then_inc(self.o_taken, 1)

            def dve_turn(self, dve, J, half):
                for c in (2 * half, 2 * half + 1):
                    dve.wait_ge(self.pT_hi, 4 * J + c + 1)
                    turned, high = self.turned_views(c, "hi")
                    dve.tensor_tensor(self.turned_views(c, "lo")[1], turned, own(high), ALU.subtract)\
                        .then_inc(self.pT_lo, 1)

            def pe(self, pe, s):
                W = wp[self.slot]
                pe.wait_ge(stage_done, s)
                pe.wait_ge(wp_loaded[self.slot], 64 * self.loads)
                for m in range(K2):
                    for k in range(K2):
                        ins = pe.matmul(bank(m), W[:, 0, k, m * P:(m + 1) * P], hT[:, k, :], start=(k == 0),
                                        stop=(k == K2 - 1))
                ins.then_inc(self.q_psum, 1)
                pe.wait_ge(self.q_ready, self.order + 1)
                pe.wait_ge(self.w_ready, self.order + 1)
                with pe.Fori(0, B) as b:
                    u = b + self.b0
                    pe.wait_ge(self.batch_done, u + 1)
                    pe.wait_ge(ctx_loaded, 32 * b + (32 * self.ctx_before + 32))
                    for kind, c in self.PROLOGUE:
                        a, w = self.width(c, kind)
                        if kind == "x":
                            for f in range(K2):
                                if c >= 2:
                                    pe.wait_ge(self.x_lo, 8 * u + 2 * (c - 2) + f + 1)
                                for i, kt in enumerate(self.turns[c]):
                                    n = self.tiles[kt]
                                    ins = pe.transpose(ps[:, 2 * (c % 2) + f, i * P:i * P + n],
                                                       self.ctx[0:n, kt, f * P:(f + 1) * P], ident[0:n, 0:n])
                                ins.then_inc(self.turned, 1)
                        else:
                            pe.wait_ge(self.x_lo, 8 * u + 2 * c + 2)
                            if c == 3:
                                pe.wait_ge(self.qbd_ready, u + 1)
                            for m in range(K2):
                                if c >= 2:
                                    pe.wait_ge(self.k_lo, 8 * u + 2 * (c - 2) + m + 1)
                                for n, (i, j) in enumerate(THREE):
                                    for k in range(K2):
                                        ins = pe.matmul(bank(4 + 2 * (c % 2) + m, w),
                                                        self.w[i][:, k, m * P:(m + 1) * P],
                                                        self.xT[j][:, k, a:a + w],
                                                        start=(n == 0 and k == 0), stop=(n == 2 and k == K2 - 1))
                                ins.then_inc(self.k_psum, 1)
                    for i in range((KT + 1) // 2):
                        if i >= 4:
                            pe.wait_ge(self.k_lo, 8 * u + i + 1)
                        for kt in range(2 * i, min(2 * i + 2, KT)):
                            n = self.tiles[kt]
                            for q, (ii, jj) in enumerate(THREE):
                                for k in range(K2):
                                    ins = pe.matmul(ps[0:n, i, (kt % 2) * D:(kt % 2 + 1) * D],
                                                    self.xT[ii][:, k, kt * P:kt * P + n], self.w[jj][:, K2 + k, :],
                                                    start=(q == 0 and k == 0), stop=(q == 2 and k == K2 - 1))
                        ins.then_inc(self.v_psum, 1)
                    pe.wait_ge(self.k_lo, 8 * u + 8)
                    pe.wait_ge(self.v_lo, 7 * u + 7)
                    for j in range(self.nj + 1):
                        for half in (0, 1):
                            if j < self.nj:
                                self.pe_scores(pe, self.nj * u + j, j, half)
                            if j:
                                self.pe_turn(pe, self.nj * u + (j - 1), self.p[(j - 1) % 2], half)
                            if half == 0 and j >= 2:
                                self.pe_rows(pe, self.nj * u + (j - 2), j % 2)
                        if j:
                            J = self.nj * u + (j - 1)
                            pe.wait_ge(self.o_taken, J + 1)
                            o = 6 + (j - 1) % 2
                            for c, tiles in enumerate(self.turns):
                                pe.wait_ge(self.pT_lo, 4 * J + c + 1)
                                for kt in tiles:
                                    n = self.tiles[kt]
                                    for part in ("hi", "lo"):
                                        ins = pe.matmul(ps[0:4 * HD, o, 0:P], self.v[0:n, kt, j - 1, :],
                                                        self.pT[part][0:n, kt, :],
                                                        start=(kt == 0 and part == "hi"),
                                                        stop=(kt == KT - 1 and part == "lo"))
                            ins.then_inc(self.pv_psum, 1)
                    self.pe_rows(pe, self.nj * u + (self.nj - 1), (self.nj - 1) % 2)
                    pe.wait_ge(self.o_rows, u + 1)
                    for g in range(K2):
                        ins = pe.matmul(ps[:, 6, g * S:(g + 1) * S],
                                        self.o[:, 4 * g:4 * g + 4, :].rearrange("p a b -> p (a b)"), const("fold"),
                                        start=True, stop=True)
                    ins.then_inc(self.oT_psum, 1)
                pe.wait_ge(self.oT_final, self.order + 1)
                for t in range(T):
                    if self.biased:
                        pe.matmul(bank(t, D), one_row, row("bo3"), start=True, stop=False)
                    for k in range(K2):
                        ins = pe.matmul(bank(t, D), self.oT[:, k, t * P:(t + 1) * P], W[:, 3, k, :],
                                        start=(k == 0 and not self.biased), stop=(k == K2 - 1))
                    ins.then_inc(self.y_ps, 1)

            def act(self, act, s):
                act.wait_ge(stage_done, s)
                with act.Fori(0, B) as b:
                    u = b + self.b0
                    for kind, c in self.PROLOGUE:
                        a, w = self.width(c, kind)
                        for f in range(K2):
                            if kind == "x":
                                act.wait_ge(self.turned, 8 * u + 8 + 2 * c + f + 1)
                                act.activation(self.xT["hi"][:, f, a:a + w], bank(2 * (c % 2) + f, w), ACT.Copy)\
                                    .then_inc(self.x_hi, 1)
                            else:
                                act.wait_ge(self.k_psum, 8 * u + 2 * c + f + 1)
                                o, i = self.kT["hi"][:, f, a:a + w], bank(4 + 2 * (c % 2) + f, w)
                                if self.biased:
                                    ins = act.activation(o, i, ACT.Identity, bias=col("bk3", f))
                                else:
                                    ins = act.activation(o, i, ACT.Copy)
                                ins.then_inc(self.k_hi, 1)
                    for i in range((KT + 1) // 2):
                        act.wait_ge(self.v_psum, 7 * u + i + 1)
                        values, high = self.value_views(i, "hi")
                        act.activation(high, values, ACT.Copy).then_inc(self.v_hi, 1)
                    for j in range(self.nj + 1):
                        if j:
                            self.act_turn(act, self.nj * u + (j - 1))
                        if j < self.nj:
                            q = j % 2
                            self.act_exp(act, self.nj * u + j, self.p[q], self.st[:, q:q + 1],
                                         self.st[:, 4 + 3 * q:7 + 3 * q])
                        if j:
                            q = (j - 1) % 2
                            act.wait_ge(self.pv_psum, self.nj * u + j)
                            act.activation(self.sums[:, q, :], ps[0:4 * HD, 6 + q, 0:P], ACT.Copy)\
                                .then_inc(self.pv_copied, 1)

            def dve(self, dve, s):
                dve.wait_ge(stage_done, s)
                dve.wait_ge(self.q_psum, self.order + 1)
                for m in range(K2):
                    qf = self.oT[:, m, :]
                    if self.biased:
                        dve.tensor_scalar(qf, bank(m), col("bq3", m), HD ** -0.5, ALU.add, ALU.mult)
                    else:
                        dve.tensor_scalar(qf, bank(m), HD ** -0.5, None, ALU.mult)
                    dve.drain()
                    dve.tensor_copy(self.q["hi"][:, m, :], qf)
                    dve.drain()
                    dve.tensor_tensor(self.q["lo"][:, m, :], qf, own(self.q["hi"])[:, m, :], ALU.subtract)
                dve.drain().then_inc(self.q_ready, 1)
                with dve.Fori(0, B) as b:
                    u = b + self.b0
                    for kind, c in self.PROLOGUE:
                        a, w = self.width(c, kind)
                        for f in range(K2):
                            if kind == "x":
                                dve.wait_ge(self.x_hi, 8 * u + 2 * c + f + 1)
                                dve.tensor_tensor(self.xT["lo"][:, f, a:a + w], bank(2 * (c % 2) + f, w),
                                                  own(self.xT["hi"])[:, f, a:a + w], ALU.subtract).then_inc(self.x_lo, 1)
                            else:
                                dve.wait_ge(self.k_hi, 8 * u + 2 * c + f + 1)
                                o, i = self.kT["lo"][:, f, a:a + w], bank(4 + 2 * (c % 2) + f, w)
                                hi = own(self.kT["hi"])[:, f, a:a + w]
                                if self.biased:
                                    ins = dve.scalar_tensor_tensor(out=o, in0=i, scalar=col("bk3", f), in1=hi,
                                                                   op0=ALU.add, op1=ALU.subtract)
                                else:
                                    ins = dve.tensor_tensor(o, i, hi, ALU.subtract)
                                ins.then_inc(self.k_lo, 1)
                    for i in range((KT + 1) // 2):
                        dve.wait_ge(self.v_hi, 7 * u + i + 1)
                        values, high = self.value_views(i, "hi")
                        dve.tensor_tensor(self.value_views(i, "lo")[1], values, own(high), ALU.subtract)\
                            .then_inc(self.v_lo, 1)
                    for j in range(self.nj + 1):
                        q = j % 2
                        for half in (0, 1):
                            if j < self.nj:
                                self.dve_max(dve, self.nj * u + j, self.st[:, 12 + 4 * q:16 + 4 * q],
                                             self.st[:, q:q + 1], (2 * half, 2 * half + 1))
                            if j:
                                self.dve_turn(dve, self.nj * u + (j - 1), half)
                        if j:
                            q = (j - 1) % 2
                            dve.tensor_reduce(self.st[:, 2:3], self.st[:, 4 + 3 * q:7 + 3 * q], AX.X, ALU.add)
                            dve.drain()
                            dve.reciprocal(self.st[:, 20 + q:21 + q], self.st[:, 2:3])
                        if j >= 2:
                            self.dve_rows(dve, self.nj * u + (j - 2), j - 2)
                    dve.drain()
                    self.dve_rows(dve, self.nj * u + (self.nj - 1), self.nj - 1)
                    dve.drain().then_inc(self.o_rows, 1)
                    dve.wait_ge(self.oT_psum, u + 1)
                    dve.tensor_copy(self.oT[:, :, ds(b * S, S)], ps[:, 6, 0:K2 * S].rearrange("p (g q) -> p g q", g=K2))
                    dve.drain().then_inc(self.batch_done, 1)
                if self.biased:
                    for k in range(K2):
                        dve.tensor_scalar(self.oT[:, k, :], self.oT[:, k, :], col("bv3", k), None, ALU.add)
                dve.drain().then_inc(self.oT_final, 1)
                for t in range(T):
                    dve.wait_ge(self.y_ps, 4 * self.order + t + 1)
                    dve.tensor_tensor(x[:, t, :], bank(t, D), x[:, t, :], ALU.add)
                dve.drain().then_inc(stage_done, 1)

        class First(Flash):

            def __init__(self):
                super().__init__("x0", H0 // 2, [P] * FULL + [TAIL, S])
                name = "x0"
                (self.q_psum, self.q_ready, self.qp_psum, self.qp_ready, self.var, self.std, self.norm, self.turned,
                 self.xT_act, self.xT_dve, self.lat_psum, self.lat_ready, self.kv_ready, self.oh_psum, self.oh_ready,
                 self.y_ps, self.bcast, self.o_rows, self.u_psum, self.qp_copied) = (
                    sem(f"{name}_{n}") for n in ("q_psum", "q_ready", "qk_psum", "qk_ready", "var", "std", "norm",
                                                 "ctx_turned", "xT_by_act", "xT_by_dve", "latents_psum",
                                                 "latents_ready", "kv_ready", "heads_psum", "heads_ready", "y_psum",
                                                 "affine_loaded",
                                                 "o_rows", "u_psum", "qk_copied"))
                (self.ctx, self.kv, self.xT, self.p0, self.p1, self.pT, self.oT, self.qp, self.gb, self.st,
                 self.qp_all) = carve((KT, D), (KT + 1, D), (K2, KEYS + S), (KEYS + S,), (KEYS + S,), (KT + 1, P),
                                      (H0, N), (K2, H0 * S), (2, D), (32,), (K2 * H0, N))
                self.qp_all = self.qp_all.rearrange("p (k h) n -> p k h n", k=K2)
                self.qT = self.oT
                self.u_all = self.qp_all
                self.o = hn[:, :, :]
                self.p = (self.p0, self.p1)
                self.wq = w1[0]
                self.wv = w1[1]
                self.wkT = w2[0]
                self.wo = w2[1]

            def sp(self, sp, ctx_rows):
                sp.dma_start(self.wq[:, :, :], A["Wq0"].rearrange("(k p) n -> p k n", p=P)).then_inc(x0_loaded, 16)
                sp.dma_start(self.wkT[:, :, :], A["Wk0T"].rearrange("(h p) n -> p h n", p=P)).then_inc(x0_loaded, 16)
                sp.dma_start(self.gb[:, 0, :], A["g_media_row"].to_broadcast([P, D])).then_inc(self.bcast, 16)
                sp.dma_start(self.gb[:, 1, :], A["b_media_row"].to_broadcast([P, D])).then_inc(self.bcast, 16)
                with sp.Fori(0, B) as b:
                    sp.wait_ge(self.kv_ready, b + 1)
                    sp.dma_start(self.ctx[:, 0:FULL, :],
                                 ctx_rows[b, 0:FULL * P, :].rearrange("(t p) d -> p t d", p=P)).then_inc(ctx_loaded, 16)
                    sp.dma_start(self.ctx[0:TAIL, FULL, :], ctx_rows[b, FULL * P:KEYS, :]).then_inc(ctx_loaded, 16)
                sp.dma_start(self.wv[:, :, :], A["Wv0"].rearrange("(k p) n -> p k n", p=P)).then_inc(x0_loaded, 16)
                sp.dma_start(self.wo[:, :, :], A["Wo0"].rearrange("(h p) n -> p h n", p=P)).then_inc(x0_loaded, 16)

            def pool(self, pool):
                pool.wait_ge(self.bcast, 32)
                with pool.Fori(0, B) as b:
                    pool.wait_ge(self.batch_done, b + 1)
                    pool.wait_ge(self.norm, b + 1)
                    for n, lo, hi in ((P, 0, FULL), (TAIL, FULL, KT)):
                        bc = lambda i: self.gb[0:n, i, :].unsqueeze(1).to_broadcast([n, hi - lo, D])
                        pool.tensor_tensor(self.kv[0:n, lo:hi, :], self.ctx[0:n, lo:hi, :], bc(0), ALU.mult)
                        pool.drain()
                        if n == TAIL:
                            pool.wait_ge(self.turned, 8 * b + 16)
                        pool.tensor_tensor(self.kv[0:n, lo:hi, :], self.kv[0:n, lo:hi, :], bc(1), ALU.add)
                    pool.drain().then_inc(self.kv_ready, 1)

            def pe(self, pe, s):
                pe.wait_ge(stage_done, s)
                pe.wait_ge(x0_loaded, 32)
                for h in range(H0):
                    for k in range(K2):
                        ins = pe.matmul(bank(h), self.wq[:, k, h * P:(h + 1) * P], hT[:, k, :], start=(k == 0),
                                        stop=(k == K2 - 1))
                ins.then_inc(self.q_psum, 1)
                pe.wait_ge(self.q_ready, 1)
                for f in range(K2):
                    for h in range(H0):
                        if f:
                            pe.wait_ge(self.qp_copied, h + 1)
                        pe.matmul(bank(h), self.wkT[:, h, f * P:(f + 1) * P], self.qT[:, h, :], start=True, stop=True)\
                            .then_inc(self.qp_psum, 1)
                pe.wait_ge(self.qp_copied, K2 * H0)
                with pe.Fori(0, B) as b:
                    pe.wait_ge(self.batch_done, b + 1)
                    pe.wait_ge(self.norm, b + 1)
                    for f in range(K2):
                        for c in range(4):
                            for i, kt in enumerate(self.turns[c][0:4 if c < 3 else 1]):
                                n = self.tiles[kt]
                                ins = pe.transpose(ps[:, 4 * f + c, i * P:i * P + n],
                                                   self.ctx[0:n, kt, f * P:(f + 1) * P], ident[0:n, 0:n])
                            ins.then_inc(self.turned, 1)
                    pe.wait_ge(self.xT_dve, 5 * b + 5)
                    pe.wait_ge(self.xT_act, 4 * b + 4)
                    for f in range(K2):
                        ins = pe.matmul(ps[0:S, 7, f * P:(f + 1) * P], self.xT[:, f, KEYS:KEYS + S], ident,
                                        start=True, stop=True)
                    ins.then_inc(self.lat_psum, 1)
                    pe.wait_ge(self.lat_ready, b + 1)
                    pe.wait_ge(self.qp_ready, b + 1)
                    for j in range(self.nj + 1):
                        if j < self.nj:
                            J = self.nj * b + j
                            for c, (a, w) in enumerate(self.chunks):
                                if c < 3:
                                    pe.wait_ge(self.exp_done, 3 * J + c + 1)
                                for k in range(K2):
                                    ins = pe.matmul(bank(c, w), self.qp[:, k, 2 * j * S:(2 * j + 2) * S],
                                                    self.xT[:, k, a:a + w], start=(k == 0), stop=(k == K2 - 1))
                                ins.then_inc(self.s_psum, 1)
                        if j:
                            J = self.nj * b + (j - 1)
                            self.pe_turn(pe, J, self.p[(j - 1) % 2])
                            if j == 1:
                                pe.wait_ge(self.kv_ready, b + 2)
                            pe.wait_ge(self.o_taken, J + 1)
                            for c, tiles in enumerate(self.turns):
                                self.pe_wait_turned(pe, J, c)
                                for kt in tiles:
                                    n = self.tiles[kt]
                                    ins = pe.matmul(bank(6 + (j - 1) % 2, D), self.pT[0:n, kt, :], self.kv[0:n, kt, :],
                                                    start=(kt == 0), stop=(kt == KT))
                            ins.then_inc(self.o_psum, 1)
                    pe.wait_ge(self.o_rows, b + 1)
                    for f in range(K2):
                        for j in range(self.nj):
                            ins = pe.transpose(ps[:, 4 + f, j * P:(j + 1) * P], self.o[:, j, f * P:(f + 1) * P], ident)
                    ins.then_inc(self.u_psum, 1)
                pe.wait_ge(self.batch_done, B + 1)
                pe.wait_ge(x0_loaded, 64)
                for h in range(H0):
                    for k in range(K2):
                        ins = pe.matmul(bank(h), self.wv[:, k, h * P:(h + 1) * P], self.u_all[:, k, h, :],
                                        start=(k == 0), stop=(k == K2 - 1))
                    ins.then_inc(self.oh_psum, 1)
                pe.wait_ge(self.oh_ready, 1)
                for t in range(T):
                    pe.matmul(bank(t, D), one_row, row("bo0"), start=True, stop=False)
                    for h in range(H0):
                        ins = pe.matmul(bank(t, D), self.oT[:, h, t * P:(t + 1) * P], self.wo[:, h, :], start=False,
                                        stop=(h == H0 - 1))
                    ins.then_inc(self.y_ps, 1)

            def act(self, act, s):
                act.wait_ge(stage_done, s)
                self.act_std(act, 0)
                for i in range(K2 * H0):
                    act.wait_ge(self.qp_psum, i + 1)
                    act.activation(self.qp_all[:, i // H0, i % H0, :], bank(i % H0), ACT.Copy).then_inc(self.qp_copied, 1)
                act.drain()
                with act.Fori(0, B - 1) as b:
                    self.act_batch(act, b, True)
                self.act_batch(act, B - 1, False)

            def act_std(self, act, b):
                act.wait_ge(self.var, b + 1)
                act.activation(ln_sd[:, :], ln_ve[:, :], ACT.Sqrt).then_inc(self.std, 1)

            def act_batch(self, act, b, more):
                act.activation(self.qp.rearrange("p k (h q) -> p k h q", h=H0), self.qp_all[:, :, :, ds(b * S, S)],
                               ACT.Copy).then_inc(self.qp_ready, 1)
                for c, (a, w) in enumerate(chunks):
                    act.wait_ge(self.turned, 8 * b + 8 + c + 1)
                    act.activation(self.xT[:, 0, a:a + w], bank(c, w), ACT.Identity, bias=col("b_media", 0),
                                   scale=col("g_media", 0)).then_inc(self.xT_act, 1)
                for j in range(self.nj + 1):
                    if j:
                        self.act_turn(act, self.nj * b + (j - 1), self.pT)
                    if j < self.nj:
                        q = j % 2
                        self.act_exp(act, self.nj * b + j, self.p[q], self.st[:, q:q + 1],
                                     self.st[:, 4 + 3 * q:7 + 3 * q])
                    if j == 2 and more:
                        self.act_std(act, b + 1)

            def dve(self, dve, s):
                dve.wait_ge(stage_done, s)
                self.dve_stats(dve, 0)
                dve.wait_ge(self.q_psum, 1)
                for h in range(H0):
                    dve.tensor_scalar(self.qT[:, h, :], bank(h), col("bq0", h), DH0 ** -0.5, ALU.add, ALU.mult)
                dve.drain().then_inc(self.q_ready, 1)
                self.dve_norm(dve, 0)
                with dve.Fori(0, B - 1) as b:
                    self.dve_batch(dve, b, True)
                self.dve_batch(dve, B - 1, False)
                for h in range(H0):
                    dve.wait_ge(self.oh_psum, h + 1)
                    dve.tensor_scalar(self.oT[:, h, :], bank(h), col("bv0", h), None, ALU.add)
                dve.drain().then_inc(self.oh_ready, 1)
                for t in range(T):
                    dve.wait_ge(self.y_ps, t + 1)
                    dve.tensor_tensor(x[:, t, :], bank(t, D), x[:, t, :], ALU.add)
                dve.drain().then_inc(stage_done, 1)

            def dve_stats(self, dve, b):
                dve.wait_ge(ctx_loaded, 32 * b + 32)
                for kt in range(KT):
                    n = self.tiles[kt]
                    dve.bn_stats(ln_st[0:n, kt, :], self.ctx[0:n, kt, :])
                dve.drain()
                for kt in range(KT):
                    n = self.tiles[kt]
                    dve.bn_aggr(ln_mv[0:n, kt, :], ln_st[0:n, kt, :])
                dve.drain()
                dve.tensor_scalar(ln_ve[:, :], ln_mv[:, :, 1], EPS, None, ALU.add).then_inc(self.var, 1)

            def dve_norm(self, dve, b):
                dve.wait_ge(self.std, b + 1)
                dve.reciprocal(ln_rs[:, :], ln_sd[:, :])
                dve.drain()
                for kt in range(KT):
                    n = self.tiles[kt]
                    dve.tensor_scalar(self.ctx[0:n, kt, :], self.ctx[0:n, kt, :], ln_mv[0:n, kt, 0:1],
                                      ln_rs[0:n, kt:kt + 1], ALU.subtract, ALU.mult)
                dve.drain().then_inc(self.norm, 1)

            def dve_batch(self, dve, b, more):
                dve.wait_ge(self.turned, 8 * b + 8 + 1)
                dve.tensor_copy(self.xT[:, :, KEYS:KEYS + S], hT[:, :, ds(b * S, S)]).then_inc(self.xT_dve, 1)
                for c, (a, w) in enumerate(chunks):
                    dve.wait_ge(self.turned, 8 * b + 8 + 4 + c + 1)
                    dve.tensor_scalar(self.xT[:, 1, a:a + w], bank(4 + c, w), col("g_media", 1), col("b_media", 1),
                                      ALU.mult, ALU.add).then_inc(self.xT_dve, 1)
                dve.wait_ge(self.lat_psum, b + 1)
                dve.tensor_copy(self.kv[0:S, KT, :], bank(7, D, S)).then_inc(self.lat_ready, 1)
                for j in range(self.nj + 1):
                    if j < self.nj:
                        q = j % 2
                        self.dve_max(dve, self.nj * b + j, self.st[:, 12 + 4 * q:16 + 4 * q], self.st[:, q:q + 1])
                    if j:
                        J, q = self.nj * b + (j - 1), (j - 1) % 2
                        self.dve_turn(dve, J, self.pT)
                        if j == 2 and more:
                            self.dve_stats(dve, b + 1)
                        if j == 3 and more:
                            self.dve_norm(dve, b + 1)
                        self.dve_sums(dve, J, self.st[:, 4 + 3 * q:7 + 3 * q], self.st[:, 2:3], self.st[:, 3:4])
                        dve.tensor_scalar(self.o[:, j - 1, :], bank(6 + q, D), self.st[:, 3:4], None, ALU.mult)\
                            .then_inc(self.o_taken, 1)
                dve.drain().then_inc(self.o_rows, 1)
                dve.wait_ge(self.u_psum, b + 1)
                dve.tensor_copy(self.u_all[:, :, :, ds(b * S, S)],
                                ps[:, 4:6, :].rearrange("p k (h q) -> p k h q", h=H0))
                dve.drain().then_inc(self.batch_done, 1)

        class Quat:

            def __init__(self):
                (self.pw_psum, self.pw_ready, self.qkv_psum, self.qkv_ready, self.diff_psum, self.diff_ready,
                 self.rolled, self.reduced, self.cos_ready, self.p3_ready, self.c_ready, self.cT_psum, self.cT_ready,
                 self.z_psum, self.z_ready, self.y_ps) = (
                    sem(f"quat_{n}") for n in ("pw_psum", "pw_ready", "qkv_psum", "qkv_ready", "diff_psum",
                                               "diff_ready", "rolled", "reduced", "cos_ready", "p3_ready",
                                               "c_ready", "cT_psum", "cT_ready", "z_psum", "z_ready", "y_psum"))
                TD = T * D
                (self.aw, self.pw, self.ab, self.pw2, self.q, self.k, self.v, self.red, self.pr, self.tmp,
                 self.ptmp, self.half2) = carve((K2, 3 * D), (K2, D), (3 * D,), (K2, D), (4, TD), (4, TD), (4, TD),
                                                (3, TD), (4, TD), (TD,), (TD,), (TD,))
                self.parts = (self.q, self.k, self.v)
                self.q_at = 2 * K2 * D + K2 * 3 * D + 3 * D
                self.cT = self.q[:, 0, :].rearrange("p (k n) -> p k n", k=K2)
                self.zT = self.q[:, 1, :].rearrange("p (k n) -> p k n", k=K2)
                self.hidden = scratch[:, 3072:3072 + 8 * N].rearrange("p (a b) -> p a b", a=8)

            def sp(self, sp, s0):
                sp.wait_ge(stage_done, s0)
                with sp.Fori(0, LAYERS) as l:
                    sp.wait_ge(stage_done, 4 * l + (s0 - 2))
                    sp.dma_start(self.aw, A["attn_w"][l, :, :].rearrange("(k p) n -> p k n", p=P)).then_inc(lw_loaded, 16)
                    sp.dma_start(self.pw, A["aproj_w"][l, :, :].rearrange("(k p) n -> p k n", p=P)).then_inc(lw_loaded, 16)
                    sp.dma_start(self.ab, A["attn_b"][ds(l, 1), :].to_broadcast([P, 3 * D])).then_inc(lw_loaded, 16)
                    sp.wait_ge(y_psum, 4 * l + 4)
                    fc = A["fc_w"][l, :, :].rearrange("(k p) n -> p k n", p=P)
                    ffn_load(sp, 0, (w1[0][:, 0, :], fc[:, 0, :]), (w1[0][:, 1, :], fc[:, 1, :]),
                             (w2[0][:, :, :], A["mproj_w"][l, :, :].rearrange("(k p) n -> p k n", p=P)))

            def pe(self, pe, s, l):
                pe.wait_ge(stage_done, s)
                pe.wait_ge(lw_loaded, 48 * l + 48)
                basis = const("basis").rearrange("p (k n) -> p k n", k=K2)
                for m in range(K2):
                    for k in range(K2):
                        ins = pe.matmul(ps[:, 6, m * D:(m + 1) * D], basis[:, k, m * P:(m + 1) * P], self.pw[:, k, :],
                                        start=(k == 0), stop=(k == K2 - 1))
                ins.then_inc(self.pw_psum, 1)
                for t in range(T):
                    b0 = 2 * (t % 2)
                    if t >= 2:
                        pe.wait_ge(self.qkv_ready, 4 * l + t - 1)
                    for bk, a, w in ((b0, 0, CHUNK), (b0 + 1, CHUNK, 3 * D - CHUNK)):
                        for k in range(K2):
                            ins = pe.matmul(bank(bk, w), hT[:, k, t * P:(t + 1) * P], self.aw[:, k, a:a + w],
                                            start=(k == 0), stop=(k == K2 - 1))
                    ins.then_inc(self.qkv_psum, 1)
                pe.wait_ge(self.qkv_ready, 4 * l + 4)
                for i, part in enumerate(self.parts):
                    for t in range(T):
                        at = i * T + t
                        ins = pe.matmul(ps[:, at // 2, (at % 2) * D:(at % 2 + 1) * D], const("diff"),
                                        part[:, 0, t * D:(t + 1) * D], start=True, stop=True)
                    ins.then_inc(self.diff_psum, 1)
                pe.wait_ge(self.c_ready, l + 1)
                for k in range(K2):
                    for t in range(T):
                        ins = pe.transpose(ps[:, k, t * P:(t + 1) * P], self.pr[:, 0, t * D + k * P:t * D + (k + 1) * P],
                                           ident)
                ins.then_inc(self.cT_psum, 1)
                pe.wait_ge(self.cT_ready, l + 1)
                for m in range(K2):
                    for k in range(K2):
                        ins = pe.matmul(bank(2 + m), basis[:, k, m * P:(m + 1) * P], self.cT[:, k, :], start=(k == 0),
                                        stop=(k == K2 - 1))
                ins.then_inc(self.z_psum, 1)
                pe.wait_ge(self.z_ready, l + 1)
                pe.wait_ge(self.pw_ready, l + 1)
                pbias = rows[0:1, ds(l * D + row_at["aproj_b"][0], D)]
                for t in range(T):
                    pe.matmul(bank(4 + t, D), one_row, pbias, start=True, stop=False)
                    for k in range(K2):
                        ins = pe.matmul(bank(4 + t, D), self.zT[:, k, t * P:(t + 1) * P], self.pw2[:, k, :],
                                        start=False, stop=(k == K2 - 1))
                    ins.then_inc(self.y_ps, 1)

            def act(self, act, s, l):
                act.wait_ge(stage_done, s)
                act.wait_ge(self.pw_psum, l + 1)
                act.activation(self.pw2.rearrange("p k n -> p (k n)"), bank(6), ACT.Copy).then_inc(self.pw_ready, 1)
                act.wait_ge(self.qkv_ready, 4 * l + 4)
                for part in self.parts:
                    dst = part[:, 2, :].rearrange("p (t d) -> p t d", t=T)
                    src = part[:, 0, :].rearrange("p (t d) -> p t d", t=T)
                    act.activation(dst[:, :, HD:D], src[:, :, 0:D - HD], ACT.Copy)
                    act.activation(dst[:, :, 0:HD], src[:, :, D - HD:D], ACT.Copy)
                act.drain().then_inc(self.rolled, 1)
                for i, part in enumerate(self.parts):
                    act.wait_ge(self.diff_psum, 3 * l + i + 1)
                    act.activation(part[:, 1, :], ps[:, 2 * i:2 * i + 2, :].rearrange("p a b -> p (a b)"), ACT.Copy)\
                        .then_inc(self.diff_ready, 1)
                act.wait_ge(self.reduced, l + 1)
                act.activation(self.red, self.red, ACT.Abs)
                act.drain()
                for i, part in enumerate(self.parts):
                    act.activation(part[:, 3, :], self.red[:, i, :], ACT.Sin, bias=half_pi[:, :], scale=-1.0)\
                        .then_inc(self.cos_ready, 1)
                act.wait_ge(self.cT_psum, l + 1)
                act.activation(self.cT, ps[:, 0:2, :], ACT.Copy).then_inc(self.cT_ready, 1)

            def pool(self, pool, l):
                pool.wait_ge(self.rolled, l + 1)
                pool.wait_ge(self.diff_ready, 3 * l + 2)
                self.combine(pool, self.pr[:, 3, :], self.TERMS[3][0:2], self.ptmp)
                pool.wait_ge(self.cos_ready, 3 * l + 2)
                self.combine(pool, self.pr[:, 3, :], self.TERMS[3][2:], self.ptmp, more=True)
                pool.wait_ge(self.cos_ready, 3 * l + 3)
                pool.tensor_tensor(self.pr[:, 3, :], self.pr[:, 3, :], self.v[:, 3, :], ALU.mult)
                pool.drain()
                self.combine(pool, self.half2, self.TERMS[2][2:], self.ptmp)
                pool.drain().then_inc(self.p3_ready, 1)

            TERMS = {0: ((0, 0, 1), (1, 1, -1), (2, 2, -1), (3, 3, -1)),
                     1: ((0, 1, 1), (1, 0, 1), (2, 3, 1), (3, 2, -1)),
                     2: ((0, 2, 1), (1, 3, -1), (2, 0, 1), (3, 1, 1)),
                     3: ((1, 2, 1), (2, 1, -1), (0, 3, 1), (3, 0, 1))}

            def combine(self, eng, total, terms, tmp, more=False):
                for n, (i, j, sign) in enumerate(terms):
                    eng.tensor_tensor(tmp if n or more else total, self.q[:, i, :], self.k[:, j, :], ALU.mult)
                    eng.drain()
                    if n or more:
                        eng.tensor_tensor(total, total, tmp, ALU.add if sign > 0 else ALU.subtract)
                        eng.drain()

            def dve(self, dve, s, l):
                dve.wait_ge(stage_done, s)
                dve.wait_ge(lw_loaded, 48 * l + 48)
                qkv = scratch[:, self.q_at:self.q_at + 12 * T * D].rearrange("p (c j n) -> p c j n", c=3, j=4)
                bias = self.ab.rearrange("p (h c d) -> p c h d", c=3, d=HD)
                for t in range(T):
                    b0 = 2 * (t % 2)
                    dve.wait_ge(self.qkv_psum, 4 * l + t + 1)
                    src = ps[:, b0:b0 + 2, :].rearrange("p a b -> p (a b)")[:, 0:3 * D]\
                        .rearrange("p (h c d) -> p c h d", c=3, d=HD)
                    for c in range(3):
                        ins = dve.tensor_tensor(qkv[:, c, 0, t * D:(t + 1) * D].rearrange("p (h d) -> p h d", h=H),
                                                src[:, c, :, :], bias[:, c, :, :], ALU.add)
                    ins.then_inc(self.qkv_ready, 1)
                dve.drain()
                vals = qkv[:, :, 0, :]
                dve.tensor_scalar(self.red, vals, 1.0 / TWO_PI, ROUND, ALU.mult, ALU.add)
                dve.drain()
                dve.tensor_scalar(self.red, self.red, ROUND, -TWO_PI, ALU.subtract, ALU.mult)
                dve.drain()
                dve.tensor_tensor(self.red, self.red, vals, ALU.add).then_inc(self.reduced, 1)
                dve.wait_ge(self.diff_ready, 3 * l + 3)
                dve.wait_ge(self.rolled, l + 1)
                self.combine(dve, self.pr[:, 0, :], self.TERMS[0][0:3], self.tmp)
                self.combine(dve, self.pr[:, 1, :], self.TERMS[1][0:2], self.tmp)
                dve.wait_ge(self.cos_ready, 3 * l + 2)
                self.combine(dve, self.pr[:, 0, :], self.TERMS[0][3:], self.tmp, more=True)
                self.combine(dve, self.pr[:, 1, :], self.TERMS[1][2:], self.tmp, more=True)
                self.combine(dve, self.pr[:, 2, :], self.TERMS[2][0:2], self.tmp)
                c0 = self.pr[:, 0, :]
                dve.tensor_tensor(c0, c0, self.v[:, 0, :], ALU.mult)
                for c in (1, 2):
                    if c == 2:
                        dve.wait_ge(self.p3_ready, l + 1)
                        dve.tensor_tensor(self.pr[:, 2, :], self.pr[:, 2, :], self.half2, ALU.add)
                    dve.drain()
                    dve.tensor_tensor(self.tmp, self.pr[:, c, :], self.v[:, c, :], ALU.mult)
                    dve.drain()
                    dve.tensor_tensor(c0, c0, self.tmp, ALU.subtract)
                dve.drain()
                dve.tensor_tensor(c0, c0, self.pr[:, 3, :], ALU.subtract)
                dve.drain().then_inc(self.c_ready, 1)
                dve.wait_ge(self.z_psum, l + 1)
                spectrum = const("spectrum").rearrange("p (k s) -> p k s", k=K2)
                for m in range(K2):
                    dve.tensor_tensor(self.zT[:, m, :].rearrange("p (b s) -> p b s", b=B),
                                      ps[:, 2 + m, :].rearrange("p (b s) -> p b s", b=B),
                                      spectrum[:, m, :].unsqueeze(1).to_broadcast([P, B, S]), ALU.mult)
                dve.drain().then_inc(self.z_ready, 1)
                for t in range(T):
                    dve.wait_ge(self.y_ps, 4 * l + t + 1)
                    dve.tensor_tensor(x0[:, t, :], bank(4 + t, D), x0[:, t, :], ALU.add)
                dve.drain().then_inc(stage_done, 1)

        half_pi = sb("half_pi", [P, 1])

        class Scan:
            NS = 64

            def __init__(self):
                (self.loaded, self.z_psum, self.l_ready, self.d_ready, self.decay_ready, self.hs_ready, self.y_ps,
                 self.hid_next, self.out_psum, self.asp) = (
                    sem(f"scan_{n}") for n in ("loaded", "z_psum", "log_ready", "delta_ready", "decay_ready",
                                               "states_ready", "y_psum", "hidden_ready", "out_psum", "a_log_ready"))
                (self.win, self.wout, self.small, self.z, self.az, self.delta, self.decay, self.drive, self.hs,
                 self.cs, self.hid, self.sa) = carve((4 * K2, self.NS), (4, D), (6,), (N,), (N,), (N,), (N,), (N,),
                                                     (N,), (K2, B), (K2, N), (8,))

            def sp(self, sp, s):
                sp.wait_ge(stage_done, s)
                for l in range(2):
                    for i, name in enumerate(("Wd", "Wi")):
                        a = (2 * l + i) * K2
                        sp.dma_start(self.win[:, a:a + K2, :], A[name][l, :, :].rearrange("(k p) n -> p k n", p=P))\
                            .then_inc(self.loaded, 16)
                    for i, name in enumerate(("Wos", "Wss")):
                        sp.dma_start(self.wout[0:self.NS, 2 * l + i, :], A[name][l, :, :]).then_inc(self.loaded, 16)
                sp.dma_start(self.small[0:self.NS, :], A["scan_small"]).then_inc(self.loaded, 16)

            def pe(self, pe, s):
                ns = self.NS
                pe.wait_ge(stage_done, s)
                pe.wait_ge(self.loaded, 16 * 9)
                for l in range(2):
                    src = hT if l == 0 else self.hid
                    if l:
                        pe.wait_ge(self.hid_next, 1)
                    for i in range(2):
                        for k in range(K2):
                            ins = pe.matmul(bank(i, N, ns), self.win[:, (2 * l + i) * K2 + k, :], src[:, k, :],
                                            start=(k == 0), stop=(k == K2 - 1))
                    ins.then_inc(self.z_psum, 1)
                    pe.wait_ge(self.hs_ready, l + 1)
                    last = self.hs[0:ns, :].rearrange("p (b s) -> p b s", b=B)[:, :, S - 1]
                    for m in range(K2):
                        pe.matmul(bank(2 + m), self.wout[0:ns, 2 * l, m * P:(m + 1) * P], self.hs[0:ns, :],
                                  start=True, stop=True)
                        ins = pe.matmul(bank(4 + m, B), self.wout[0:ns, 2 * l + 1, m * P:(m + 1) * P], last,
                                        start=True, stop=True)
                    ins.then_inc(self.y_ps, 1)
                pe.wait_ge(self.hid_next, 2)
                for t in range(T):
                    for k in range(K2):
                        ins = pe.transpose(ps[:, t // 2, (t % 2) * D + k * P:(t % 2) * D + (k + 1) * P],
                                           self.hid[:, k, t * P:(t + 1) * P], ident)
                ins.then_inc(self.out_psum, 1)

            def act(self, act, s):
                ns = self.NS
                act.wait_ge(stage_done, s)
                act.wait_ge(self.loaded, 16 * 9)
                al = self.small[0:ns, 4:6]
                ab, ex, lg = (self.sa[0:ns, i:i + 2] for i in (0, 2, 4))
                act.activation(ab, al, ACT.Abs)
                act.drain()
                act.activation(ex, ab, ACT.Exp, scale=-1.0)
                act.drain()
                act.activation(lg, ex, ACT.Ln, bias=ones[0:ns, 0:1]).then_inc(self.asp, 1)
                for l in range(2):
                    act.wait_ge(self.z_psum, l + 1)
                    act.activation(self.z[0:ns, :], bank(0, N, ns), ACT.Identity, bias=self.small[0:ns, l:l + 1])
                    act.drain()
                    act.activation(self.az[0:ns, :], self.z[0:ns, :], ACT.Abs)
                    act.drain()
                    act.activation(self.az[0:ns, :], self.az[0:ns, :], ACT.Exp, scale=-1.0)
                    act.drain()
                    act.activation(self.az[0:ns, :], self.az[0:ns, :], ACT.Ln, bias=ones[0:ns, 0:1])\
                        .then_inc(self.l_ready, 1)
                    act.wait_ge(self.d_ready, l + 1)
                    act.activation(self.decay[0:ns, :], self.delta[0:ns, :], ACT.Exp, scale=self.sa[0:ns, 6 + l:7 + l])\
                        .then_inc(self.decay_ready, 1)

            def dve(self, dve, s):
                ns = self.NS
                dve.wait_ge(stage_done, s)
                dve.wait_ge(self.asp, 1)
                sp_a = self.sa[0:ns, 6:8]
                dve.scalar_tensor_tensor(out=sp_a, in0=self.small[0:ns, 4:6], scalar=0.0, in1=self.sa[0:ns, 4:6],
                                         op0=ALU.max, op1=ALU.add)
                dve.drain()
                dve.tensor_scalar(sp_a, sp_a, -1.0, None, ALU.mult)
                for l in range(2):
                    dve.drain()
                    dve.wait_ge(self.l_ready, l + 1)
                    dve.scalar_tensor_tensor(out=self.delta[0:ns, :], in0=self.z[0:ns, :], scalar=0.0,
                                             in1=self.az[0:ns, :], op0=ALU.max, op1=ALU.add)
                    dve.drain().then_inc(self.d_ready, 1)
                    dve.scalar_tensor_tensor(out=self.drive[0:ns, :], in0=bank(1, N, ns),
                                             scalar=self.small[0:ns, 2 + l:3 + l], in1=self.delta[0:ns, :],
                                             op0=ALU.add, op1=ALU.mult)
                    dve.wait_ge(self.decay_ready, l + 1)
                    dve.memset(self.decay[0:ns, :].rearrange("p (b s) -> p b s", b=B)[:, :, 0], 0.0)
                    dve.drain()
                    dve.tensor_tensor_scan(self.hs[0:ns, :], self.decay[0:ns, :], self.drive[0:ns, :], 0.0,
                                           ALU.mult, ALU.add).then_inc(self.hs_ready, 1)
                    dve.wait_ge(self.y_ps, l + 1)
                    for m in range(K2):
                        dve.tensor_scalar(self.cs[:, m, :], bank(4 + m, B), col("bs_scan", 2 * l + m),
                                          col("bo_scan", 2 * l + m), ALU.add, ALU.add)
                    dve.drain()
                    for m in range(K2):
                        dve.tensor_tensor(self.hid[:, m, :].rearrange("p (b s) -> p b s", b=B),
                                          ps[:, 2 + m, :].rearrange("p (b s) -> p b s", b=B),
                                          self.cs[:, m, :].unsqueeze(2).to_broadcast([P, B, S]), ALU.add)
                    dve.drain().then_inc(self.hid_next, 1)
                dve.wait_ge(self.out_psum, 1)
                dve.tensor_tensor(x[:, :, :].rearrange("p t d -> p (t d)"), ps[:, 0:2, :].rearrange("p a b -> p (a b)"),
                                  x[:, :, :].rearrange("p t d -> p (t d)"), ALU.add)
                dve.drain().then_inc(stage_done, 1)

        first = First()
        quat = Quat()
        moe0 = Moe("moe0", 9, 2, ACT.Silu, True, 0, "gate_b", "top2", "sw_b1", b2_l0, 0, 5, 32, 0, (4, 0))
        moe1 = Moe("moe1", 8, 4, ACT.Silu, True, 1, None, "renormalised", None, None, 9, 14, 50, 18, (9, 4))
        moe2 = Moe("moe2", 8, 8, ACT.Gelu_apprx_tanh, False, 2, "switch_b", "top1", "l2_b1", b2_l2, 17, 22, 82, 50,
                   (13, 8))
        moe3 = Moe("moe3", 9, 8, ACT.Gelu, False, 3, "router_b", "capacity", "l3_b1", b2_l3, 25, 30, 146, 114, (17, 12))
        cross1 = Local(0, 0, 1, HD ** -0.5, "causal", None, extra_mask=True)
        self1 = Local(1, 1, 1, HD ** -0.5, "same_batch", hT, grouped=True)
        cross2 = Cross(0, 0, 2, B, False)
        self2 = Local(2, 1, 2, D ** -0.5, "same_batch", hT, bo="bff2")
        cross3 = Cross(1, 0, 3, 2 * B, True)
        scan = Scan()

        (LN_A, LN_B, FIRST, LN_C, QUAT) = range(5)
        QUAT_END = QUAT + 4 * LAYERS
        (LN_D, MOE0, LN_E, CROSS1, LN_F, SELF1, LN_G, MOE1, LN_H, CROSS2, LN_I, SELF2, LN_J, MOE2, LN_K, CROSS3,
         LN_L, SCAN, LN_M, MOE3, END) = range(QUAT_END + 1, QUAT_END + 22)
        NL = 3 + 2 * LAYERS

        later_stages = ((LN_D, MOE0, moe0), (LN_E, CROSS1, cross1), (LN_F, SELF1, self1), (LN_G, MOE1, moe1),
                        (LN_H, CROSS2, cross2), (LN_I, SELF2, self2), (LN_J, MOE2, moe2), (LN_K, CROSS3, cross3),
                        (LN_L, SCAN, scan), (LN_M, MOE3, moe3))
        block = ctx.enter_context(nc.Block())

        @block.sync
        def _(sp):
            sp.dma_start(x[:, :, :], A["x"].rearrange("(t p) d -> p t d", p=P)).then_inc(inputs_loaded, 16)
            sp.dma_start(cols[:, :], A["cols"]).then_inc(inputs_loaded, 16)
            sp.dma_start(consts[:, :], A["consts"]).then_inc(inputs_loaded, 16)
            sp.dma_start(rows[:, :], A["rows"]).then_inc(inputs_loaded, 16)
            sp.dma_start(b2_l0[:, :], A["b2_l0"]).then_inc(inputs_loaded, 16)
            sp.dma_start(b2_l2[:, :], A["b2_l2"]).then_inc(inputs_loaded, 16)
            sp.dma_start(b2_l3[:, :], A["b2_l3"]).then_inc(inputs_loaded, 16)
            sp.dma_start(routers[:, :, :, :], A["routers"].rearrange("r (k p) e -> p r k e", p=P))\
                .then_inc(inputs_loaded, 16)

            def attention_weights(slot, names):
                for i, name in enumerate(names):
                    dst = wp[slot][:, i, :, :]
                    sp.dma_start(dst, A[name].rearrange("(k p) n -> p k n", p=P)).then_inc(wp_loaded[slot], 16)

            first.sp(sp, A["ctx"])
            attention_weights(0, ("Wq1", "Wk1", "Wv1", "Wo1"))
            attention_weights(1, ("Wqa", "Wqa", "Wqa", "Woa"))
            quat.sp(sp, QUAT)

            def shared_then_routed(e, par):
                w = A["w1_l0"][e, :, :].rearrange("(k p) n -> p k n", p=P)
                return ((w1[par][:, 0, 0:512], w[:, 0, :]), (w1[par][:, 1, 0:512], w[:, 1, :]),
                        (w2[par][:, 0:2, :], A["w2_l0"][e, :, :].rearrange("(k p) n -> p k n", p=P)))

            def gate_up_down(e, par):
                return ((w1[par][:, :, 0:512], A["gate_l1"][e, :, :].rearrange("(k p) n -> p k n", p=P)),
                        (w1[par][:, :, 512:1024], A["up_l1"][e, :, :].rearrange("(k p) n -> p k n", p=P)),
                        (w2[par][:, 0:4, :], A["down_l1"][e, :, :].rearrange("(k p) n -> p k n", p=P)))

            def wide(a, b):
                def sources(e, par):
                    w = A[a][e, :, :].rearrange("(k p) n -> p k n", p=P)
                    return ((w1[par][:, 0, :], w[:, 0, :]), (w1[par][:, 1, :], w[:, 1, :]),
                            (w2[par][:, :, :], A[b][e, :, :].rearrange("(k p) n -> p k n", p=P)))
                return sources

            moe0.sp(sp, shared_then_routed)
            sp.wait_ge(stage_done, CROSS1)
            sp.dma_start(cross1.keysT, A["ctx64"].rearrange("(t p) d -> p t d", p=P)).then_inc(latent_keys_loaded, 16)
            sp.dma_start(cross1.keyraw[0:1, :].bitcast(I32), A["mask64"]).then_inc(latent_keys_loaded, 16)
            sp.wait_ge(stage_done, SELF1)
            sp.dma_start(self1.raw[:, :, 0:64], A["Wka"].rearrange("(k p) n -> p k n", p=P)).then_inc(kvraw_loaded, 16)
            sp.dma_start(self1.kraw[:, :, 0:64], A["Wva"].rearrange("(k p) n -> p k n", p=P)).then_inc(kvraw_loaded, 16)
            attention_weights(0, ("Wq2", "Wq2", "Wq2", "Wo2"))
            sp.wait_ge(stage_done, LN_G)
            attention_weights(1, ("Wqb", "Wkb", "Wvb", "Wff"))
            moe1.sp(sp, gate_up_down)
            cross2.sp(sp, CROSS2, A["ctx"])
            moe2.sp(sp, wide("w1_l2", "w2_l2"))
            attention_weights(0, ("Wq3", "Wk3", "Wv3", "Wo3"))
            cross3.sp(sp, CROSS3, A["ctx"])
            scan.sp(sp, SCAN)
            moe3.sp(sp, wide("w1_l3", "w2_l3"))
            sp.wait_ge(stage_done, END)
            sp.dma_start(out.rearrange("(t p) d -> p t d", p=P), x[:, :, :]).then_inc(stored, 16)
            sp.wait_ge(stored, 16)

        @block.gpsimd
        def _(pool):
            pool.drain().then_inc(first.kv_ready, 1)
            pool.memset(ones[:, :], 1.0)
            pool.memset(half_pi[:, :], float(np.pi / 2))
            pool.memset(ln_mv[:, :, :], 0.0)
            pool.drain().then_inc(ones_ready, 1)
            first.pool(pool)
            with pool.Fori(0, LAYERS) as l:
                quat.pool(pool, l)
            moe0.pool(pool, MOE0)
            moe1.pool(pool, MOE1)
            cross2.pool(pool, CROSS2)
            moe2.pool(pool, MOE2)
            cross3.pool(pool, CROSS3)
            moe3.pool(pool, MOE3)

        @block.tensor
        def _(pe):
            pe.drain().then_inc(first.turned, 8)
            pe.drain().then_inc(cross2.turned, 8)
            pe.drain().then_inc(y_psum, 4)
            pe.wait_ge(inputs_loaded, 128)
            pe.wait_ge(ones_ready, 1)
            ln = lambda s, n: ln_pe(pe, s, n, hn)
            ln(LN_A, 0)
            ln(LN_B, 1)
            first.pe(pe, FIRST)
            ln(LN_C, 2)
            with pe.Fori(0, LAYERS) as l:
                ln(4 * l + QUAT, 2 * l + 3)
                quat.pe(pe, 4 * l + (QUAT + 1), l)
                ln(4 * l + (QUAT + 2), 2 * l + 4)
                pe.wait_ge(stage_done, 4 * l + (QUAT + 3))
                ffn_pe(pe, l + 1, l + 1, 8 * l, quat.hidden,
                       rows[0:1, ds(l * D + row_at["mproj_b"][0], D)])
            for i, (norm_at, stage_at, stage) in enumerate(later_stages):
                ln(norm_at, NL + i)
                stage.pe(pe, stage_at)

        @block.scalar
        def _(act):
            act.drain().then_inc(first.exp_done, 3)
            act.drain().then_inc(cross2.exp_done, 3)
            act.wait_ge(inputs_loaded, 128)
            act.wait_ge(ones_ready, 1)
            ln_act(act, LN_A, 0)
            ln_act(act, LN_B, 1, lambda k: col("g_lat", k), lambda k: col("b_lat", k))
            first.act(act, FIRST)
            ln_act(act, LN_C, 2)
            with act.Fori(0, LAYERS) as l:
                ln_act(act, 4 * l + QUAT, 2 * l + 3, lambda k: dcol("ln1_w", l * 2 + k),
                       lambda k: dcol("ln1_b", l * 2 + k))
                quat.act(act, 4 * l + (QUAT + 1), l)
                ln_act(act, 4 * l + (QUAT + 2), 2 * l + 4, lambda k: dcol("ln2_w", l * 2 + k),
                       lambda k: dcol("ln2_b", l * 2 + k))
                act.wait_ge(stage_done, 4 * l + (QUAT + 3))
                ffn_act(act, 8 * l, ACT.Gelu, lambda j: dcol("fc_b", l * 8 + j), quat.hidden)
            for i, (norm_at, stage_at, stage) in enumerate(later_stages):
                ln_act(act, norm_at, NL + i)
                stage.act(act, stage_at)

        @block.vector
        def _(dve):
            for primed in (first.batch_done, cross2.batch_done, cross1.added):
                dve.drain().then_inc(primed, 1)
            for primed in (first.o_taken, cross2.o_taken):
                dve.drain().then_inc(primed, 2)
            dve.drain().then_inc(y_used, 4)
            dve.wait_ge(inputs_loaded, 128)
            dve.wait_ge(ones_ready, 1)
            ln_dve(dve, LN_A, 0, x, hn)
            ln_dve(dve, LN_B, 1, hn, hn)
            first.dve(dve, FIRST)
            ln_dve(dve, LN_C, 2, x, hn)
            dve.wait_ge(stage_done, QUAT)
            dve.tensor_copy(x0[:, :, :], hn[:, :, :])
            dve.drain()
            with dve.Fori(0, LAYERS) as l:
                ln_dve(dve, 4 * l + QUAT, 2 * l + 3, x0, hn)
                quat.dve(dve, 4 * l + (QUAT + 1), l)
                ln_dve(dve, 4 * l + (QUAT + 2), 2 * l + 4, x0, hn)
                dve.wait_ge(stage_done, 4 * l + (QUAT + 3))
                ffn_dve(dve, l + 1, x0)
                dve.drain().then_inc(stage_done, 1)
            dve.tensor_tensor(x[:, :, :], x[:, :, :], x0[:, :, :], ALU.add)
            dve.drain().then_inc(stage_done, 1)
            for i, (norm_at, stage_at, stage) in enumerate(later_stages):
                ln_dve(dve, norm_at, NL + i, x, hn)
                stage.dve(dve, stage_at)


def shape_constants():
    p = np.arange(P)
    same = (p[:, None] // S) == (p[None, :] // S)
    c = {"ident": np.eye(P), "same_batch": np.where(same, 0.0, BLOCKED),
         "causal": np.where(same & (p[None, :] <= p[:, None]), 0.0, BLOCKED)}
    diff = np.eye(P) - np.eye(P, k=1)
    diff[:, p % S == 0] = 0.0
    c["diff"] = diff
    c["head_of"] = (p[:, None] // HD == np.arange(HG)[None, :])
    c["first_of"] = np.tile(np.arange(E, 0, -1), (P, 1))
    k = np.arange(D)
    angle = 2 * np.pi * (np.outer(k // HD, k // HD) / H + np.outer(k % HD, k % HD) / HD)
    c["basis"] = ((np.cos(angle) + np.sin(angle)) / np.sqrt(H * HD)).reshape(K2, P, D).transpose(1, 0, 2).reshape(P, -1)
    ks, kh, kd = np.fft.fftfreq(S), np.fft.fftfreq(H), np.fft.fftfreq(HD)
    km = np.sqrt(ks[None, :] ** 2 + kh[k // HD][:, None] ** 2 + kd[k % HD][:, None] ** 2 + 1e-10)
    lam, t = np.arange(S) / S, np.arange(S) * 0.1
    gain = 1.0 + 0.1 * np.sin(t + lam) * np.cos(t - 2.0 * lam + 0.5 * lam ** 2)
    c["spectrum"] = (np.cos(np.arctan(np.log(km + 1e-10))) * gain).reshape(K2, P, S).transpose(1, 0, 2).reshape(P, -1)
    split = np.zeros((P, E + 1))
    split[:E, :E] = np.eye(E)
    split[:E, E] = -1.0
    c["split9"] = split
    c["own_half"] = (p[:, None] // S == np.arange(2 * HD)[None, :] // HD)
    c["stack"] = (p[:, None] % (2 * HD) == np.arange(2 * HD)[None, :]) & (p[:, None] < 4 * HD)
    c["fold"] = (p[:, None] % S == np.arange(S)[None, :])
    c["rest9"] = (p == E).astype(float)[:, None]
    return np.ascontiguousarray(np.concatenate([c[n].astype(np.float32).reshape(P, w) for n, w in CONSTS.items()], 1))


def kernel(**inputs):
    import concourse.bacc as bacc
    from concourse.bass_utils import run_bass_kernel_spmd as run

    I = {k: np.asarray(v) for k, v in inputs.items()}

    def down(v):
        return v.reshape(-1, P).T

    c = {"g_media": I["L0_xattn_gamma_media"], "b_media": I["L0_xattn_beta_media"], "g_lat": I["L0_xattn_gamma_lat"],
         "b_lat": I["L0_xattn_beta_lat"], "bq0": I["L0_xattn_bq"], "bv0": I["L0_xattn_bkv"][H0 * DH0:],
         "ln1_w": I["L0_attn_ln1_w"], "ln1_b": I["L0_attn_ln1_b"], "ln2_w": I["L0_attn_ln2_w"],
         "ln2_b": I["L0_attn_ln2_b"], "fc_b": I["L0_attn_fc_b"],
         "sw_b1": np.concatenate([I["L0_ffn_sb1"], I["L0_ffn_rb1"]], 0), "l2_b1": I["L2_ffn_b1"],
         "l3_b1": np.concatenate([I["L3_ffn_b1"], I["L3_ffn_sb1"][None]], 0),
         "bq3": I["L3_xattn_bq"], "bk3": I["L3_xattn_bk"], "bv3": I["L3_xattn_bv"],
         "bo_scan": I["L3_attn_bo"], "bs_scan": I["L3_attn_bs"]}
    r = {"bo0": I["L0_xattn_bo"], "aproj_b": I["L0_attn_aproj_b"], "mproj_b": I["L0_attn_mproj_b"],
         "gate_b": I["L0_ffn_gate_b"], "switch_b": I["L2_ffn_switch_b"], "router_b": I["L3_ffn_rb"],
         "bff2": I["L2_attn_bff"], "bo3": I["L3_xattn_bo"]}
    inner = H0 * DH0
    arrays = {
        "x": I["x"].reshape(N, D), "ctx": I["ctx_1024"], "ctx64": I["ctx_1024"][:, :S].reshape(N, D),
        "mask64": I["mask_BxS2_if1"][:, :S].reshape(1, N),
        "cols": np.concatenate([down(c[n]) for n in COLS], 1), "consts": shape_constants(),
        "rows": np.concatenate([r[n].reshape(1, -1) for n in ROWS], 1),
        "b2_l0": np.concatenate([I["L0_ffn_sb2"], I["L0_ffn_rb2"]], 0), "b2_l2": I["L2_ffn_b2"],
        "b2_l3": np.concatenate([I["L3_ffn_b2"], I["L3_ffn_sb2"][None]], 0),
        "routers": np.stack([I["L0_ffn_gate_w"], I["L1_ffn_router_kernel_DE"], I["L2_ffn_switch_w"],
                             I["L3_ffn_rw"].T], 0),
        "Wq0": I["L0_xattn_Wq"], "Wk0T": I["L0_xattn_Wkv"][:, :inner].T, "Wv0": I["L0_xattn_Wkv"][:, inner:],
        "Wo0": I["L0_xattn_Wo"], "g_media_row": I["L0_xattn_gamma_media"][None],
        "b_media_row": I["L0_xattn_beta_media"][None],
        "attn_w": I["L0_attn_attn_w"], "attn_b": I["L0_attn_attn_b"], "aproj_w": I["L0_attn_aproj_w"],
        "fc_w": I["L0_attn_fc_w"], "mproj_w": I["L0_attn_mproj_w"],
        "w1_l0": np.concatenate([I["L0_ffn_sw1"], I["L0_ffn_rw1"]], 0),
        "w2_l0": np.concatenate([I["L0_ffn_sw2"], I["L0_ffn_rw2"]], 0),
        "Wq1": I["L1_xattn_Wq"], "Wk1": I["L1_xattn_Wk"], "Wv1": I["L1_xattn_Wv"], "Wo1": I["L1_xattn_Wo"],
        "Wqa": I["L1_attn_Wq"], "Wka": I["L1_attn_Wk"], "Wva": I["L1_attn_Wv"], "Woa": I["L1_attn_Wo"],
        "gate_l1": I["L1_ffn_kernel_gating_EDF"], "up_l1": I["L1_ffn_kernel_up_EDF"],
        "down_l1": I["L1_ffn_kernel_down_EFD"],
        "Wq2": I["L2_xattn_Wq"].T, "Wo2": I["L2_xattn_Wo"].T,
        "Wqb": I["L2_attn_Wq"].T, "Wkb": I["L2_attn_Wk"].T, "Wvb": I["L2_attn_Wv"].T, "Wff": I["L2_attn_Wff"].T,
        "w1_l2": I["L2_ffn_w1"], "w2_l2": I["L2_ffn_w2"],
        "Wq3": I["L3_xattn_Wq"].T, "Wk3": I["L3_xattn_Wk"].T, "Wv3": I["L3_xattn_Wv"].T, "Wo3": I["L3_xattn_Wo"].T,
        "Wd": I["L3_attn_Wd"], "Wi": I["L3_attn_Wi"], "Wos": I["L3_attn_Wo"], "Wss": I["L3_attn_Ws"],
        "scan_small": np.concatenate([I["L3_attn_bd"].T, I["L3_attn_bi"].T, I["L3_attn_A_log"].T], 1),
        "w1_l3": np.concatenate([I["L3_ffn_w1"], I["L3_ffn_sw1"][None]], 0),
        "w2_l3": np.concatenate([I["L3_ffn_w2"], I["L3_ffn_sw2"][None]], 0),
    }
    nc = bacc.Bacc("TRN2", target_bir_lowering=False, num_devices=1)
    feed, A = {}, {}
    for name, a in arrays.items():
        a = np.ascontiguousarray(a)
        feed["in_" + name] = a
        A[name] = nc.dram_tensor("in_" + name, a.shape, mybir.dt.from_np(a.dtype), kind="ExternalInput").ap()
    out = nc.dram_tensor("out", (N, D), F32, kind="ExternalOutput").ap()
    program(nc, A, out)
    got = run(nc, [feed], core_ids=[0])
    return got.results[0]["out"].reshape(B, S, D)
```
